# Optimizing a Trainium2 kernel written in Bass

```python
import numpy as np
import jax
import jax.numpy as jnp

def _softmax(x, axis=-1):
    return jax.nn.softmax(x, axis=axis)

def _gelu(x):
    return jax.nn.gelu(x, approximate=True)

def _silu(x):
    return jax.nn.silu(x)

def _sigmoid(x):
    return jax.nn.sigmoid(x)

def _layernorm(x, axis=-1, eps=1e-05):
    m = jnp.mean(x, axis=axis, keepdims=True)
    v = jnp.var(x, axis=axis, keepdims=True)
    return (x - m) / jnp.sqrt(v + eps)

def _scatter_add(tgt, idx, src, axis=0):
    return tgt.at[idx].add(src)

def _segment_sum(src, seg, n):
    return jax.ops.segment_sum(src, seg, n)
kernel_name = 'mk_lm_tower_d2_tok_ids768_r4_a683bb'

def setup_inputs(seed: int=0):
    np.random.seed(seed)
    _w = jnp.asarray

    def _rec_inputs():
        import jax
        import jax.numpy as jnp
        _rk = jax.random.key(seed)
        x = jax.random.randint(jax.random.fold_in(_rk, 1), (16, 512), 0, 31993, jnp.int32)
        return x
    x = _rec_inputs()

    def _L0_tok_setup():
        import jax, jax.numpy as jnp
        import numpy as np
        EPS = 1e-05

        def pos_encoding(max_steps, d):
            p, i = np.meshgrid(np.arange(max_steps), np.arange(d // 2))
            pe = np.zeros((max_steps, d), dtype=np.float32)
            pe[:, ::2] = np.sin(p / 2500 ** (2 * i / d)).T
            pe[:, 1::2] = np.cos(p / 2500 ** (2 * i / d)).T
            return jnp.asarray(pe)

        def batchnorm(x, gamma, beta):
            mean = jnp.mean(x, axis=(0, 1))
            var = jnp.var(x, axis=(0, 1))
            return (x - mean) * jax.lax.rsqrt(var + EPS) * gamma + beta
        key = jax.random.key(seed)
        ks = jax.random.split(key, 12)
        B, S, D, V = (8, 256, 192, 8000)
        Dc = D // 3
        s = 0.02
        return {'x': jax.random.randint(ks[0], (B, S), 0, V, dtype=jnp.int32), 'emb': jax.random.normal(ks[1], (V, D), dtype=jnp.float32) * s, 'Wq': jax.random.normal(ks[2], (Dc, D), dtype=jnp.float32) * s, 'bq': jnp.zeros((D,), jnp.float32), 'Wk': jax.random.normal(ks[3], (Dc, D), dtype=jnp.float32) * s, 'bk': jnp.zeros((D,), jnp.float32), 'Wv': jax.random.normal(ks[4], (Dc, D), dtype=jnp.float32) * s, 'bv': jnp.zeros((D,), jnp.float32), 'Wf': jax.random.normal(ks[5], (D, D), dtype=jnp.float32) * s, 'bf': jnp.zeros((D,), jnp.float32), 'g1': jnp.ones((D,), jnp.float32), 'b1': jnp.zeros((D,), jnp.float32), 'g2': jnp.ones((D,), jnp.float32), 'b2': jnp.zeros((D,), jnp.float32)}
    _L0_tok_all = _L0_tok_setup()
    _L0_tok_in = {k: v for k, v in _L0_tok_all.items() if k in ('emb', 'Wq', 'bq', 'Wk', 'bk', 'Wv', 'bv', 'Wf', 'bf', 'g1', 'b1', 'g2', 'b2')}
    del _L0_tok_all

    def _L0_attn_setup():
        import jax, jax.numpy as jnp
        import numpy as np
        KERNEL = 5
        NUM_HEADS = 4

        def _window_starts(L, k):
            pad = k // 2
            return jnp.clip(jnp.arange(L) - pad, 0, L - k)

        def _neighborhood_attention_2d(xs, qkv_w, qkv_b, rpb, proj_w, proj_b):
            H, W, D = xs.shape
            nh, k = (NUM_HEADS, KERNEL)
            dh = D // nh
            qkv = xs @ qkv_w.T + qkv_b
            qkv = qkv.reshape(H, W, 3, nh, dh).transpose(2, 3, 0, 1, 4)
            q, kmat, vmat = (qkv[0], qkv[1], qkv[2])
            q = q * dh ** (-0.5)
            sh = _window_starts(H, k)
            sw = _window_starts(W, k)
            off = jnp.arange(k)
            idx_h = sh[:, None] + off[None, :]
            idx_w = sw[:, None] + off[None, :]
            kk = kmat[:, idx_h][:, :, :, idx_w]
            vv = vmat[:, idx_h][:, :, :, idx_w]
            logits = jnp.einsum('nhwd,nhawbd->nhwab', q, kk)
            bh = idx_h - jnp.arange(H)[:, None] + (k - 1)
            bw = idx_w - jnp.arange(W)[:, None] + (k - 1)
            bias = rpb[:, bh[:, None, :, None], bw[None, :, None, :]]
            logits = logits + bias
            attn = jax.nn.softmax(logits.reshape(nh, H, W, k * k), axis=-1).reshape(nh, H, W, k, k)
            out = jnp.einsum('nhwab,nhawbd->nhwd', attn, vv)
            out = out.transpose(1, 2, 0, 3).reshape(H, W, D)
            return out @ proj_w.T + proj_b
        H, W = (96, 96)
        IN_D, HID, OUT_D = (192, 96, 192)
        key = jax.random.key(seed)
        ks = jax.random.split(key, 16)
        s = 0.02
        return {'x': jax.random.normal(ks[0], (H, W, IN_D), dtype=jnp.float32), 'fc1_w': jax.random.normal(ks[1], (HID, IN_D), dtype=jnp.float32) * s, 'fc1_b': jnp.zeros((HID,), dtype=jnp.float32), 'convA_w': jax.random.normal(ks[2], (64, HID), dtype=jnp.float32) * s, 'convA_b': jnp.zeros((64,), dtype=jnp.float32), 'convB_w': jax.random.normal(ks[3], (HID, 64), dtype=jnp.float32) * s, 'convB_b': jnp.zeros((HID,), dtype=jnp.float32), 'qkv_w': jax.random.normal(ks[4], (3 * HID, HID), dtype=jnp.float32) * s, 'qkv_b': jnp.zeros((3 * HID,), dtype=jnp.float32), 'rpb': jax.random.normal(ks[5], (NUM_HEADS, 2 * KERNEL - 1, 2 * KERNEL - 1), dtype=jnp.float32) * s, 'proj_w': jax.random.normal(ks[6], (HID, HID), dtype=jnp.float32) * s, 'proj_b': jnp.zeros((HID,), dtype=jnp.float32), 'fc2_w': jax.random.normal(ks[7], (OUT_D, HID), dtype=jnp.float32) * s, 'fc2_b': jnp.zeros((OUT_D,), dtype=jnp.float32)}
    _L0_attn_all = _L0_attn_setup()
    _L0_attn_in = {k: v for k, v in _L0_attn_all.items() if k in ('fc1_w', 'fc1_b', 'convA_w', 'convA_b', 'convB_w', 'convB_b', 'qkv_w', 'qkv_b', 'rpb', 'proj_w', 'proj_b', 'fc2_w', 'fc2_b')}
    del _L0_attn_all

    def _L0_ffn_setup():
        import jax, jax.numpy as jnp
        import numpy as np
        B, S, D_IN, D_HID, D_OUT = (32, 128, 192, 768, 192)
        key = jax.random.key(seed)
        k1, k2, k3, k4 = jax.random.split(key, 4)
        init_k = float(np.sqrt(1.0 / D_IN))
        init_k2 = float(np.sqrt(1.0 / D_HID))
        x = jax.random.normal(k1, (B, S, D_IN), dtype=jnp.float32)
        in_weight = jax.random.uniform(k2, (D_HID, D_IN), dtype=jnp.float32, minval=-init_k, maxval=init_k)
        in_bias = jax.random.uniform(k3, (D_HID,), dtype=jnp.float32, minval=-init_k, maxval=init_k)
        out_weight = jax.random.uniform(k4, (D_HID, D_OUT), dtype=jnp.float32, minval=-init_k2, maxval=init_k2)
        return {'x': x, 'in_weight': in_weight, 'in_bias': in_bias, 'out_weight': out_weight}
    _L0_ffn_all = _L0_ffn_setup()
    _L0_ffn_in = {k: v for k, v in _L0_ffn_all.items() if k in ('in_weight', 'in_bias', 'out_weight')}
    del _L0_ffn_all

    def _L1_attn_setup():
        import jax, jax.numpy as jnp
        import numpy as np
        NH = 12
        LEVEL = 4

        def _build_sets(T, Lmin):
            l_list, r_list = ([], [])
            L = Lmin
            while L <= T:
                for i in range(T // L):
                    l_list.append(i * L)
                    r_list.append((i + 1) * L - 1)
                L *= 2
            return (np.asarray(l_list, np.int32), np.asarray(r_list, np.int32))

        def _get_slice(x_cum, l_idx, r_idx):
            r = x_cum[:, :, r_idx, :]
            l = x_cum[:, :, np.maximum(np.asarray(l_idx) - 1, 0), :]
            mask = (np.asarray(l_idx) >= 1).astype(x_cum.dtype)[None, None, :, None]
            return r - l * mask

        def _get_slice_dyn(x_cum, l_idx, r_idx):
            r = x_cum[:, :, r_idx, :]
            l = x_cum[:, :, jnp.maximum(l_idx - 1, 0), :]
            mask = (l_idx >= 1).astype(x_cum.dtype)[None, None, :, None]
            return r - l * mask
        key = jax.random.key(seed)
        k0, k1, k2, k3 = jax.random.split(key, 4)
        B, T, C = (8, 512, 192)
        hs = C // NH
        s = 0.02
        return {'x': jax.random.normal(k0, (B, T, C), jnp.float32), 'Wqkv': jax.random.normal(k1, (3 * C, C), jnp.float32) * s, 'Wproj': jax.random.normal(k2, (C, C), jnp.float32) * s, 'Wv': jax.random.normal(k3, (hs, hs * hs), jnp.float32) * s, 'bv': jnp.zeros((hs,), jnp.float32)}
    _L1_attn_all = _L1_attn_setup()
    _L1_attn_in = {k: v for k, v in _L1_attn_all.items() if k in ('Wqkv', 'Wproj', 'Wv', 'bv')}
    del _L1_attn_all

    def _L1_ffn_setup():
        import jax, jax.numpy as jnp
        import numpy as np
        D_MODEL, D_FF, N_EXPERTS, TOP_K = (192, 768, 8, 2)
        B, S = (2, 256)
        LN_EPS = 1e-05

        def _layernorm(x, gamma, beta):
            mu = jnp.mean(x, axis=-1, keepdims=True)
            var = jnp.mean(jnp.square(x - mu), axis=-1, keepdims=True)
            return (x - mu) * jax.lax.rsqrt(var + LN_EPS) * gamma + beta
        key = jax.random.key(seed)
        k1, k2, k3, k4 = jax.random.split(key, 4)
        return {'hidden_states': jax.random.normal(k1, (B, S, D_MODEL), dtype=jnp.float32), 'ln_gamma': jnp.ones((D_MODEL,), dtype=jnp.float32), 'ln_beta': jnp.zeros((D_MODEL,), dtype=jnp.float32), 'router_w': jax.random.normal(k2, (D_MODEL, N_EXPERTS), dtype=jnp.float32) * 0.02, 'w1': jax.random.normal(k3, (N_EXPERTS, D_MODEL, D_FF), dtype=jnp.float32) * 0.02, 'w2': jax.random.normal(k4, (N_EXPERTS, D_FF, D_MODEL), dtype=jnp.float32) * 0.02}
    _L1_ffn_all = _L1_ffn_setup()
    _L1_ffn_in = {k: v for k, v in _L1_ffn_all.items() if k in ('ln_gamma', 'ln_beta', 'router_w', 'w1', 'w2')}
    del _L1_ffn_all
    return {'x': x, 'L0_tok_emb': _L0_tok_in['emb'], 'L0_tok_Wq': _L0_tok_in['Wq'], 'L0_tok_bq': _L0_tok_in['bq'], 'L0_tok_Wk': _L0_tok_in['Wk'], 'L0_tok_bk': _L0_tok_in['bk'], 'L0_tok_Wv': _L0_tok_in['Wv'], 'L0_tok_bv': _L0_tok_in['bv'], 'L0_tok_Wf': _L0_tok_in['Wf'], 'L0_tok_bf': _L0_tok_in['bf'], 'L0_tok_g1': _L0_tok_in['g1'], 'L0_tok_b1': _L0_tok_in['b1'], 'L0_tok_g2': _L0_tok_in['g2'], 'L0_tok_b2': _L0_tok_in['b2'], 'L0_attn_fc1_w': _L0_attn_in['fc1_w'], 'L0_attn_fc1_b': _L0_attn_in['fc1_b'], 'L0_attn_convA_w': _L0_attn_in['convA_w'], 'L0_attn_convA_b': _L0_attn_in['convA_b'], 'L0_attn_convB_w': _L0_attn_in['convB_w'], 'L0_attn_convB_b': _L0_attn_in['convB_b'], 'L0_attn_qkv_w': _L0_attn_in['qkv_w'], 'L0_attn_qkv_b': _L0_attn_in['qkv_b'], 'L0_attn_rpb': _L0_attn_in['rpb'], 'L0_attn_proj_w': _L0_attn_in['proj_w'], 'L0_attn_proj_b': _L0_attn_in['proj_b'], 'L0_attn_fc2_w': _L0_attn_in['fc2_w'], 'L0_attn_fc2_b': _L0_attn_in['fc2_b'], 'L0_ffn_in_weight': _L0_ffn_in['in_weight'], 'L0_ffn_in_bias': _L0_ffn_in['in_bias'], 'L0_ffn_out_weight': _L0_ffn_in['out_weight'], 'L1_attn_Wqkv': _L1_attn_in['Wqkv'], 'L1_attn_Wproj': _L1_attn_in['Wproj'], 'L1_attn_Wv': _L1_attn_in['Wv'], 'L1_attn_bv': _L1_attn_in['bv'], 'L1_ffn_ln_gamma': _L1_ffn_in['ln_gamma'], 'L1_ffn_ln_beta': _L1_ffn_in['ln_beta'], 'L1_ffn_router_w': _L1_ffn_in['router_w'], 'L1_ffn_w1': _L1_ffn_in['w1'], 'L1_ffn_w2': _L1_ffn_in['w2']}

def reference(x, L0_tok_emb, L0_tok_Wq, L0_tok_bq, L0_tok_Wk, L0_tok_bk, L0_tok_Wv, L0_tok_bv, L0_tok_Wf, L0_tok_bf, L0_tok_g1, L0_tok_b1, L0_tok_g2, L0_tok_b2, L0_attn_fc1_w, L0_attn_fc1_b, L0_attn_convA_w, L0_attn_convA_b, L0_attn_convB_w, L0_attn_convB_b, L0_attn_qkv_w, L0_attn_qkv_b, L0_attn_rpb, L0_attn_proj_w, L0_attn_proj_b, L0_attn_fc2_w, L0_attn_fc2_b, L0_ffn_in_weight, L0_ffn_in_bias, L0_ffn_out_weight, L1_attn_Wqkv, L1_attn_Wproj, L1_attn_Wv, L1_attn_bv, L1_ffn_ln_gamma, L1_ffn_ln_beta, L1_ffn_router_w, L1_ffn_w1, L1_ffn_w2):
    import jax
    import jax.numpy as jnp

    def _L0_tok_ref(x, emb, Wq, bq, Wk, bk, Wv, bv, Wf, bf, g1, b1, g2, b2):
        import jax, jax.numpy as jnp
        import numpy as np
        EPS = 1e-05

        def pos_encoding(max_steps, d):
            p, i = np.meshgrid(np.arange(max_steps), np.arange(d // 2))
            pe = np.zeros((max_steps, d), dtype=np.float32)
            pe[:, ::2] = np.sin(p / 2500 ** (2 * i / d)).T
            pe[:, 1::2] = np.cos(p / 2500 ** (2 * i / d)).T
            return jnp.asarray(pe)

        def batchnorm(x, gamma, beta):
            mean = jnp.mean(x, axis=(0, 1))
            var = jnp.var(x, axis=(0, 1))
            return (x - mean) * jax.lax.rsqrt(var + EPS) * gamma + beta
        B, S = x.shape
        D = emb.shape[1]
        H = 12
        hd = D // H
        N = 2
        scale = 1.0 / jnp.sqrt(jnp.asarray(D, jnp.float32))
        e = emb[x]
        P = pos_encoding(S, D)
        h = e + (e + P)

        def split_heads(t):
            return t.reshape(B, S, H, hd)
        for _ in range(N):
            q, k, v = jnp.split(h, 3, axis=-1)
            Q = split_heads(jax.nn.relu(q @ Wq + bq))
            K = split_heads(jax.nn.relu(k @ Wk + bk))
            V = split_heads(jax.nn.relu(v @ Wv + bv))
            scores = jnp.einsum('bqhd,bkhd->bhqk', Q, K) * scale
            attn = jax.nn.softmax(scores, axis=-1)
            o = jnp.einsum('bhqk,bkhd->bqhd', attn, V).reshape(B, S, D)
            t = batchnorm(h + o, g1, b1)
            h = batchnorm(t + (t @ Wf + bf), g2, b2)
        return h

    def _L0_attn_ref(x, fc1_w, fc1_b, convA_w, convA_b, convB_w, convB_b, qkv_w, qkv_b, rpb, proj_w, proj_b, fc2_w, fc2_b):
        import jax, jax.numpy as jnp
        import numpy as np
        KERNEL = 5
        NUM_HEADS = 4

        def _window_starts(L, k):
            pad = k // 2
            return jnp.clip(jnp.arange(L) - pad, 0, L - k)

        def _neighborhood_attention_2d(xs, qkv_w, qkv_b, rpb, proj_w, proj_b):
            H, W, D = xs.shape
            nh, k = (NUM_HEADS, KERNEL)
            dh = D // nh
            qkv = xs @ qkv_w.T + qkv_b
            qkv = qkv.reshape(H, W, 3, nh, dh).transpose(2, 3, 0, 1, 4)
            q, kmat, vmat = (qkv[0], qkv[1], qkv[2])
            q = q * dh ** (-0.5)
            sh = _window_starts(H, k)
            sw = _window_starts(W, k)
            off = jnp.arange(k)
            idx_h = sh[:, None] + off[None, :]
            idx_w = sw[:, None] + off[None, :]
            kk = kmat[:, idx_h][:, :, :, idx_w]
            vv = vmat[:, idx_h][:, :, :, idx_w]
            logits = jnp.einsum('nhwd,nhawbd->nhwab', q, kk)
            bh = idx_h - jnp.arange(H)[:, None] + (k - 1)
            bw = idx_w - jnp.arange(W)[:, None] + (k - 1)
            bias = rpb[:, bh[:, None, :, None], bw[None, :, None, :]]
            logits = logits + bias
            attn = jax.nn.softmax(logits.reshape(nh, H, W, k * k), axis=-1).reshape(nh, H, W, k, k)
            out = jnp.einsum('nhwab,nhawbd->nhwd', attn, vv)
            out = out.transpose(1, 2, 0, 3).reshape(H, W, D)
            return out @ proj_w.T + proj_b
        xs = x @ fc1_w.T + fc1_b
        a = xs @ convA_w.T + convA_b
        b = a @ convB_w.T + convB_b
        xs = b * 1.0 + xs
        xs = jax.nn.gelu(xs, approximate=False)
        xs = _neighborhood_attention_2d(xs, qkv_w, qkv_b, rpb, proj_w, proj_b)
        xs = xs @ fc2_w.T + fc2_b
        return x + xs

    def _L0_ffn_ref(x, in_weight, in_bias, out_weight):
        import jax, jax.numpy as jnp
        import numpy as np
        B, S, D_IN, D_HID, D_OUT = (32, 128, 192, 768, 192)
        lead = x.shape[:-1]
        xt = x.reshape(-1, in_weight.shape[1])
        h = jax.nn.gelu(jnp.einsum('td,hd->th', xt, in_weight) + in_bias, approximate=False)
        out = jnp.einsum('th,ho->to', h, out_weight)
        return out.reshape(*lead, out_weight.shape[1])

    def _L1_attn_ref(x, Wqkv, Wproj, Wv, bv):
        import jax, jax.numpy as jnp
        import numpy as np
        NH = 12
        LEVEL = 4

        def _build_sets(T, Lmin):
            l_list, r_list = ([], [])
            L = Lmin
            while L <= T:
                for i in range(T // L):
                    l_list.append(i * L)
                    r_list.append((i + 1) * L - 1)
                L *= 2
            return (np.asarray(l_list, np.int32), np.asarray(r_list, np.int32))

        def _get_slice(x_cum, l_idx, r_idx):
            r = x_cum[:, :, r_idx, :]
            l = x_cum[:, :, np.maximum(np.asarray(l_idx) - 1, 0), :]
            mask = (np.asarray(l_idx) >= 1).astype(x_cum.dtype)[None, None, :, None]
            return r - l * mask

        def _get_slice_dyn(x_cum, l_idx, r_idx):
            r = x_cum[:, :, r_idx, :]
            l = x_cum[:, :, jnp.maximum(l_idx - 1, 0), :]
            mask = (l_idx >= 1).astype(x_cum.dtype)[None, None, :, None]
            return r - l * mask
        B, T, C = x.shape
        nh = NH
        hs = C // nh
        Lmin = 2 ** LEVEL
        scale = 1.0 / jnp.sqrt(jnp.asarray(hs, x.dtype))
        qkv = x @ Wqkv.T
        q, k, v0 = jnp.split(qkv, 3, axis=-1)
        q = q.reshape(B, T, nh, hs).transpose(0, 2, 1, 3)
        k = k.reshape(B, T, nh, hs).transpose(0, 2, 1, 3)
        v0 = v0.reshape(B, T, nh, hs).transpose(0, 2, 1, 3)
        Wv3 = Wv.reshape(hs, hs, hs)
        v = jnp.einsum('bhti,bhtj,eij->bhte', k, v0, Wv3) + bv
        k_cum = jnp.cumsum(k, axis=2)
        v_cum = jnp.cumsum(v, axis=2)
        l_idx, r_idx = _build_sets(T, Lmin)
        K = _get_slice(k_cum, l_idx, r_idx)
        V = _get_slice(v_cum, l_idx, r_idx)
        t_idx = jnp.arange(T)
        mask = t_idx[:, None] >= jnp.asarray(r_idx)[None, :]
        logits = jnp.einsum('bhtd,bhsd->bhts', q, K) * scale
        logits = jnp.where(mask[None, None], logits, -jnp.inf)
        l_tail = t_idx // Lmin * Lmin
        K_tail = _get_slice_dyn(k_cum, l_tail, t_idx)
        V_tail = _get_slice_dyn(v_cum, l_tail, t_idx)
        tail_logits = jnp.sum(q * K_tail, axis=-1) * scale
        att = jax.nn.softmax(jnp.concatenate([logits, tail_logits[..., None]], axis=-1), axis=-1)
        out = jnp.einsum('bhts,bhsd->bhtd', att[..., :-1], V) + att[..., -1:] * V_tail
        out = out.transpose(0, 2, 1, 3).reshape(B, T, C)
        return out @ Wproj.T

    def _L1_ffn_ref(hidden_states, ln_gamma, ln_beta, router_w, w1, w2):
        import jax, jax.numpy as jnp
        import numpy as np
        D_MODEL, D_FF, N_EXPERTS, TOP_K = (192, 768, 8, 2)
        B, S = (2, 256)
        LN_EPS = 1e-05

        def _layernorm(x, gamma, beta):
            mu = jnp.mean(x, axis=-1, keepdims=True)
            var = jnp.mean(jnp.square(x - mu), axis=-1, keepdims=True)
            return (x - mu) * jax.lax.rsqrt(var + LN_EPS) * gamma + beta
        Bz, Sz, D = hidden_states.shape
        residual = hidden_states
        x = _layernorm(hidden_states, ln_gamma, ln_beta)
        tokens = x.reshape(-1, D)
        T = tokens.shape[0]
        logits = tokens @ router_w
        probs = jax.nn.softmax(logits, axis=-1)
        topw, topi = jax.lax.top_k(probs, TOP_K)
        topw = topw / jnp.sum(topw, axis=-1, keepdims=True)
        gates = jnp.zeros((T, N_EXPERTS), dtype=tokens.dtype)
        gates = gates.at[jnp.arange(T)[:, None], topi].set(topw)
        h = jnp.einsum('td,edf->etf', tokens, w1)
        h = jax.nn.silu(h)
        y = jnp.einsum('etf,efd->etd', h, w2)
        out = jnp.einsum('te,etd->td', gates, y)
        return residual + out.reshape(Bz, Sz, D)
    h = _L0_tok_ref(x, L0_tok_emb, L0_tok_Wq, L0_tok_bq, L0_tok_Wk, L0_tok_bk, L0_tok_Wv, L0_tok_bv, L0_tok_Wf, L0_tok_bf, L0_tok_g1, L0_tok_b1, L0_tok_g2, L0_tok_b2)
    h = h + _L0_attn_ref(_layernorm(h, axis=-1), L0_attn_fc1_w, L0_attn_fc1_b, L0_attn_convA_w, L0_attn_convA_b, L0_attn_convB_w, L0_attn_convB_b, L0_attn_qkv_w, L0_attn_qkv_b, L0_attn_rpb, L0_attn_proj_w, L0_attn_proj_b, L0_attn_fc2_w, L0_attn_fc2_b)
    h = h + _L0_ffn_ref(_layernorm(h, axis=-1), L0_ffn_in_weight, L0_ffn_in_bias, L0_ffn_out_weight)
    h = h + _L1_attn_ref(_layernorm(h, axis=-1), L1_attn_Wqkv, L1_attn_Wproj, L1_attn_Wv, L1_attn_bv)
    h = h + _L1_ffn_ref(_layernorm(h, axis=-1), L1_ffn_ln_gamma, L1_ffn_ln_beta, L1_ffn_router_w, L1_ffn_w1, L1_ffn_w2)
    return h

_drawn_inputs = setup_inputs


def setup_inputs(seed=0):
    import zlib

    import numpy as np

    out = dict(_drawn_inputs(seed))
    spreads = {'L0_tok_bq': (0.0, 0.8),
     'L0_tok_bk': (0.0, 0.8),
     'L0_tok_bv': (0.0, 0.8),
     'L0_tok_bf': (0.0, 2.0),
     'L0_tok_g1': (1.0, 0.2),
     'L0_tok_b1': (0.0, 2.0),
     'L0_tok_g2': (1.0, 0.2),
     'L0_tok_b2': (0.0, 0.1),
     'L0_attn_fc1_b': (0.0, 0.8),
     'L0_attn_convA_b': (0.0, 0.8),
     'L0_attn_convB_b': (0.0, 0.8),
     'L0_attn_qkv_b': (0.0, 0.8),
     'L0_attn_proj_b': (0.0, 0.472),
     'L0_attn_fc2_b': (0.0, 0.339),
     'L1_attn_bv': (0.0, 0.1),
     'L1_ffn_ln_gamma': (1.0, 0.6),
     'L1_ffn_ln_beta': (0.0, 0.8)}
    factors = {'L0_tok_Wq': 8.0,
     'L0_tok_Wk': 8.0,
     'L0_tok_Wv': 8.0,
     'L0_attn_fc1_w': 8.0,
     'L0_attn_convA_w': 8.0,
     'L0_attn_convB_w': 8.0,
     'L0_attn_qkv_w': 8.0,
     'L0_attn_rpb': 30.676,
     'L0_attn_proj_w': 8.0,
     'L0_attn_fc2_w': 3.655,
     'L0_ffn_in_bias': 14.91,
     'L1_ffn_router_w': 5.366,
     'L1_ffn_w1': 4.527,
     'L1_ffn_w2': 4.552}
    for name, (base, spread) in spreads.items():
        noise = np.random.default_rng([zlib.crc32(name.encode()), seed]).standard_normal(out[name].shape)
        drawn = base * np.exp(spread * noise) if base else spread * noise
        out[name] = jnp.asarray(drawn.astype(out[name].dtype))
    for name, factor in factors.items():
        out[name] = (out[name] * factor).astype(out[name].dtype)
    return out
```

```python
from contextlib import ExitStack

import concourse.bass as bass
import numpy as np
from concourse import mybir

F32 = mybir.dt.float32
BF16 = mybir.dt.bfloat16
I32 = mybir.dt.int32
U32 = mybir.dt.uint32
ALU = mybir.AluOpType
ACT = mybir.ActivationFunctionType
AX = mybir.AxisListType

P = 128
NB, SEQ, D = 16, 512, 192
TOKENS = NB * SEQ
VOCAB = 8000
NH, HD = 12, 16
PAD = 32
NG, GH = 3, 4
TT = SEQ // P
TILES = TOKENS // P
EPS = 1e-5
LAYERS = 2
NEG = -1.0e30


class Chain:

    def __init__(self, eng, sem, per=0, turn=0):
        self.eng, self.sem, self.base, self.per, self.n = eng, sem, turn * per, per, 0

    def __call__(self, ins):
        ins.then_inc(self.sem, 1)
        self.n += 1

    def wait(self):
        self.eng.wait_ge(self.sem, self.base + self.n)

    def end(self):
        assert self.n == self.per, (self.n, self.per)


class Store:

    def __init__(self, nc, ctx, stage):
        self.nc, self.ctx, self.stage = nc, ctx, stage

    def sb(self, name, shape, dt=F32):
        return self.ctx.enter_context(self.nc.sbuf_tensor(f"{self.stage}_{name}", shape, dt))

    def ps(self, name, shape, dt=F32):
        return self.ctx.enter_context(self.nc.psum_tensor(f"{self.stage}_{name}", shape, dt))

    def sem(self, name):
        return self.nc.alloc_semaphore(name=f"{self.stage}_{name}")




def token_stage(nc, x, emb, weights, pos, pad_rows, ident, h1, scratch):
    Wq, bq, Wk, bk, Wv, bv, Wf, bf, g1, b1, g2, b2 = weights
    q_parts, k_parts, v_rows = scratch
    SCALE = float(np.float32(1.0) / np.sqrt(np.float32(D)))
    UNITS = NB * NG
    SLOTS = 4

    with ExitStack() as stage:
        st = Store(nc, stage, "tok")
        hT = st.sb("hT", [P, NB, NG, SEQ])
        hT_u = hT[:, :, :, :].rearrange("p b g t -> p (b g) t")
        wq = st.sb("wq", [P, D])
        wk = st.sb("wk", [P, D])
        wv = st.sb("wv", [P, NH * PAD])
        wf = st.sb("wf", [P, NG, NH * PAD])
        affine = st.sb("affine", [P, NG, 4])
        norm = st.sb("norm", [P, 2, 2, NG])
        mean_var = st.sb("mean_var", [P, NG, 2])
        power = st.sb("power", [P, 2, NG])
        stats = st.sb("stats", [P, NG, NB, 6])
        idn = st.sb("idn", [P, P])
        idn_b = st.sb("idn_b", [P, P], BF16)

        with ExitStack() as part:
            pt = Store(nc, part, "emb")
            ids = pt.sb("ids", [P, TILES], I32)
            wrap = pt.sb("wrap", [P, TILES], I32)
            wrapped = pt.sb("wrapped", [P, TILES], I32)
            rows = pt.sb("rows", [P, TILES, D])
            posn = pt.sb("posn", [P, TT, D])
            tmp = pt.sb("tmp", [P, TT, D])
            padded = pt.sb("padded", [P, 2, TT, NH, PAD])
            turned = pt.ps("turned", [P, 2, 4, SEQ])
            ids_in, pos_in, idn_in = pt.sem("ids_in"), pt.sem("pos_in"), pt.sem("idn_in")
            zeroed, weights_in = pt.sem("zeroed"), pt.sem("weights_in")
            rows_in = [pt.sem("rows_in_even"), pt.sem("rows_in_odd")]
            own, idn_copied = pt.sem("own"), pt.sem("idn_copied")
            ready, padded_done, turned_done, copied = (
                pt.sem("ready"), pt.sem("padded_done"), pt.sem("turned_done"), pt.sem("copied"))
            with nc.Block() as block:

                @block.sync
                def _(sp):
                    with nc.allow_non_contiguous_dma(reason="one token number per partition"):
                        sp.dma_start(ids[:, :], x.rearrange("b (q p) -> p (b q)", p=P)).then_inc(ids_in, 16)
                    sp.dma_start(posn[:, :, :], pos.rearrange("(q p) d -> p q d", p=P)).then_inc(pos_in, 16)
                    sp.dma_start(idn[:, :], ident).then_inc(idn_in, 16)
                    sp.wait_ge(zeroed, 4)
                    sp.dma_start(wv[:, :], pad_rows[:, 0:NH * PAD]).then_inc(weights_in, 16)
                    sp.dma_start(affine[:, :, :], pad_rows[:, NH * PAD:].rearrange("p (g k) -> p g k", g=NG)).then_inc(weights_in, 16)
                    sp.wait_ge(weights_in, 32)
                    for j in range(GH):
                        rows_j = slice(PAD * j, PAD * j + HD)
                        in_j = slice(HD * j, HD * j + HD)
                        sp.dma_start(wq[rows_j, :], Wq[in_j, :]).then_inc(weights_in, 16)
                        sp.dma_start(wk[rows_j, :], Wk[in_j, :]).then_inc(weights_in, 16)
                        sp.dma_start(wv[rows_j, :].rearrange("p (h c) -> p h c", h=NH)[:, :, 0:HD],
                                     Wv[in_j, :].rearrange("p (h c) -> p h c", h=NH)).then_inc(weights_in, 16)
                        for g in range(NG):
                            c0 = HD * (GH * g + j)
                            sp.dma_start(wf[rows_j, g, :].rearrange("p (h c) -> p h c", h=NH)[:, :, 0:HD],
                                         Wf[c0:c0 + HD, :].rearrange("p (h c) -> p h c", h=NH)).then_inc(weights_in, 16)
                            for n, vec in enumerate((g1, b1, g2, b2)):
                                sp.dma_start(affine[rows_j, g, n:n + 1],
                                             vec[c0:c0 + HD].rearrange("(p a) -> p a", a=1)).then_inc(weights_in, 16)
                    one = slice(HD, HD + 1)
                    sp.dma_start(wq[one, :], bq.rearrange("(a n) -> a n", a=1)).then_inc(weights_in, 16)
                    sp.dma_start(wk[one, :], bk.rearrange("(a n) -> a n", a=1)).then_inc(weights_in, 16)
                    sp.dma_start(wv[one, :].rearrange("p (h c) -> p h c", h=NH)[:, :, 0:HD],
                                 bv.rearrange("(a h c) -> a h c", a=1, h=NH)).then_inc(weights_in, 16)
                    sp.dma_start(wf[one, 0, :].rearrange("p (h c) -> p h c", h=NH)[:, :, 0:HD],
                                 bf.rearrange("(a h c) -> a h c", a=1, h=NH)).then_inc(weights_in, 16)
                    sp.wait_ge(weights_in, 16 * (2 + GH * (3 + NG * 5) + 4))

                @block.gpsimd
                def _(pool):
                    pool.memset(wq[:, :], 0.0).then_inc(zeroed, 1)
                    pool.memset(wk[:, :], 0.0).then_inc(zeroed, 1)
                    pool.memset(wv[:, :], 0.0).then_inc(zeroed, 1)
                    pool.memset(wf[:, :, :], 0.0).then_inc(zeroed, 1)
                    pool.wait_ge(ready, 1)
                    for t in range(TILES):
                        b = t // TT
                        if t % TT == 0 and b >= 2:
                            pool.wait_ge(rows_in[b % 2], 16 * TT * (b // 2))
                        pool.indirect_dma_start(rows[:, t, :], None, emb[:, :],
                                                bass.IndirectOffsetOnAxis(ap=wrapped[:, t:t + 1].bitcast(U32), axis=0)
                                                ).then_inc(rows_in[b % 2], 16)

                @block.vector
                def _(dve):
                    chain = Chain(dve, own)
                    dve.wait_ge(ids_in, 16)
                    chain(dve.tensor_scalar(wrap[:, :], ids[:, :], 0.0, float(VOCAB), ALU.is_lt, ALU.mult))
                    chain.wait()
                    chain(dve.tensor_tensor(wrap[:, :], ids[:, :], wrap[:, :], ALU.add))
                    chain.wait()
                    dve.tensor_scalar(wrapped[:, :], wrap[:, :], 0.0, float(VOCAB - 1), ALU.max, ALU.min).then_inc(ready, 1)
                    chain(dve.memset(padded[:, :, :, :, :], 0.0))
                    chain.wait()
                    chain(dve.memset(padded[:, :, :, :, HD:HD + 1], 1.0))
                    chain(dve.memset(norm[:, 1, 0, :], 1.0))
                    chain(dve.memset(norm[:, 1, 1, :], 0.0))
                    chain.wait()
                    base = chain.n
                    dve.wait_ge(pos_in, 16)
                    with dve.Fori(0, NB // 2) as it:
                        for half in range(2):
                            b = it * 2 + half
                            dve.wait_ge(rows_in[half], it * (16 * TT) + 16 * TT)
                            e = rows[:, bass.ds(b * TT, TT), :]
                            dve.wait_ge(padded_done, b)
                            dve.tensor_tensor(tmp[:, :, :], e, posn[:, :, :], ALU.add).then_inc(own, 1)
                            dve.wait_ge(own, b + (base + 1))
                            dve.wait_ge(turned_done, b)
                            dve.tensor_tensor(padded[:, half, :, :, 0:HD],
                                              tmp[:, :, :].rearrange("p q (h c) -> p q h c", h=NH),
                                              e.rearrange("p q (h c) -> p q h c", h=NH), ALU.add).then_inc(padded_done, 1)

                @block.tensor
                def _(pe):
                    pe.wait_ge(idn_in, 16)
                    pe.sem_inc(turned_done, 1)
                    with pe.Fori(0, NB // 2) as it:
                        for half in range(2):
                            b = it * 2 + half
                            pe.wait_ge(padded_done, b + 1)
                            pe.wait_ge(copied, b)
                            for g in range(NG):
                                for q in range(TT):
                                    last = pe.transpose(turned[:, half, g, P * q:P * q + P],
                                                        padded[:, half, q, GH * g:GH * g + GH, :].rearrange("p h c -> p (h c)"),
                                                        idn[:, :])
                            last.then_inc(turned_done, 1)

                @block.scalar
                def _(act):
                    act.wait_ge(idn_in, 16)
                    act.activation(idn_b[:, :], idn[:, :], ACT.Copy).then_inc(idn_copied, 1)
                    act.sem_inc(copied, 1)
                    with act.Fori(0, NB // 2) as it:
                        for half in range(2):
                            b = it * 2 + half
                            act.wait_ge(turned_done, b + 2)
                            act.activation(hT[:, bass.ds(b, 1), :, :].rearrange("p b g t -> p (b g) t"),
                                           turned[:, half, 0:NG, :], ACT.Copy).then_inc(copied, 1)

        with nc.Fori(0, LAYERS) as layer:
            token_project(nc, layer, hT, wq, wk, wv, norm, q_parts, k_parts, v_rows)
            token_attention(nc, layer, hT_u, idn, idn_b, stats, q_parts, k_parts, v_rows, SCALE, UNITS, SLOTS)
            token_norm(nc, layer, 0, stats, mean_var, power, affine, norm)
            token_dense(nc, layer, hT, wf, norm, stats)
            token_norm(nc, layer, 1, stats, mean_var, power, affine, norm)

        with ExitStack() as part:
            pt = Store(nc, part, "end")
            staged = pt.sb("staged", [P, 2, NG, SEQ])
            out_rows = pt.sb("out_rows", [P, 2, TT, D])
            turned = pt.ps("turned", [P, TT, SEQ])
            staged_done, turned_done, out_done = pt.sem("staged_done"), pt.sem("turned_done"), pt.sem("out_done")
            stored = [pt.sem("stored_even"), pt.sem("stored_odd")]
            with nc.Block() as block:

                @block.scalar
                def _(act):
                    with act.Fori(0, NB // 2) as it:
                        for half in range(2):
                            b = it * 2 + half
                            act.wait_ge(turned_done, b)
                            for g in range(NG):
                                act.activation(staged[:, half, g, :], hT[:, bass.ds(b, 1), g, :].rearrange("p b t -> p (b t)"),
                                               ACT.Identity, bias=norm[:, 1, 1, g:g + 1],
                                               scale=norm[:, 1, 0, g:g + 1]).then_inc(staged_done, 1)

                @block.tensor
                def _(pe):
                    pe.sem_inc(turned_done, 1)
                    with pe.Fori(0, NB // 2) as it:
                        for half in range(2):
                            b = it * 2 + half
                            pe.wait_ge(staged_done, b * NG + NG)
                            pe.wait_ge(out_done, b * 2)
                            for q in range(TT):
                                for g in range(NG):
                                    last = pe.transpose(turned[:, q, P * g:P * g + P], staged[:, half, g, P * q:P * q + P], idn[:, :])
                            last.then_inc(turned_done, 1)

                @block.vector
                def _(dve):
                    with dve.Fori(0, NB // 2) as it:
                        for half in range(2):
                            b = it * 2 + half
                            dve.wait_ge(turned_done, b + 2)
                            dve.wait_ge(stored[half], it * 16)
                            for n in range(2):
                                dve.tensor_copy(
                                    out_rows[:, half, 2 * n:2 * n + 2, :].rearrange("p q (h c) -> p q h c", h=NH),
                                    turned[:, 2 * n:2 * n + 2, 0:NH * PAD].rearrange("p q (h c) -> p q h c", h=NH)[:, :, :, 0:HD]
                                ).then_inc(out_done, 1)

                @block.sync
                def _(sp):
                    with sp.Fori(0, NB // 2) as it:
                        for half in range(2):
                            b = it * 2 + half
                            sp.wait_ge(out_done, b * 2 + 2)
                            sp.dma_start(h1[bass.ds(b * SEQ, SEQ), :].rearrange("(q p) d -> p q d", p=P),
                                         out_rows[:, half, :, :]).then_inc(stored[half], 16)
                    for half in range(2):
                        sp.wait_ge(stored[half], 16 * NB // 2)


def token_project(nc, layer, hT, wq, wk, wv, norm, q_parts, k_parts, v_rows):
    with ExitStack() as part:
        pt = Store(nc, part, "proj")
        staged = pt.sb("staged", [P, 2, NG, SEQ])
        full = [pt.sb(f"full_{n}", [96, 2, SEQ]) for n in "qk"]
        rest = [pt.sb(f"rest_{n}", [96, 2, SEQ]) for n in "qk"]
        parts = [pt.sb(f"parts_{n}", [96, 3, 2, SEQ], BF16) for n in "qk"]
        v_sb = pt.sb("v_sb", [P, TT, NH * PAD])
        qk_ps = [pt.ps(f"{n}_ps", [96, 2, SEQ]) for n in "qk"]
        v_ps = pt.ps("v_ps", [P, TT, SEQ])
        staged_done, restored = pt.sem("staged_done"), pt.sem("restored")
        qk_done, v_done = pt.sem("qk_done"), pt.sem("v_done")
        full_done = pt.sem("full_done")
        v_copied = pt.sem("v_copied")
        split = [pt.sem(f"split_{n}") for n in "qk"]
        stored, v_stored = [pt.sem(f"stored_{n}") for n in "qk"], pt.sem("v_stored")
        all_stored = pt.sem("all_stored")
        STORES = 3
        with nc.Block() as block:

            @block.scalar
            def _(act):
                with act.Fori(0, NB // 2) as it:
                    for half in range(2):
                        n = layer * NB + it * 2 + half
                        b = it * 2 + half
                        act.wait_ge(v_done, layer * (NB + 1) + b)
                        act.wait_ge(restored, layer * (NB + 1) + b)
                        for g in range(NG):
                            act.activation(staged[:, half, g, :], hT[:, bass.ds(b, 1), g, :].rearrange("p b t -> p (b t)"),
                                           ACT.Identity, bias=norm[:, 1, 1, g:g + 1],
                                           scale=norm[:, 1, 0, g:g + 1]).then_inc(staged_done, 1)
                        act.wait_ge(qk_done, n + 1)
                        for m in range(2):
                            act.wait_ge(split[m], n * 3)
                            act.wait_ge(stored[m], n * (16 * STORES))
                            act.activation(full[m][:, :, :], qk_ps[m][:, :, :], ACT.Relu).then_inc(full_done, 1)
                            act.activation(parts[m][:, 0, :, :], qk_ps[m][:, :, :], ACT.Relu).then_inc(full_done, 1)

            @block.tensor
            def _(pe):
                pe.sem_inc(v_done, 1)
                with pe.Fori(0, NB // 2) as it:
                    for half in range(2):
                        n = layer * NB + it * 2 + half
                        pe.wait_ge(staged_done, n * NG + NG)
                        pe.wait_ge(full_done, n * 4)
                        for m, w in enumerate((wq, wk)):
                            for c in range(2):
                                last = pe.matmul(qk_ps[m][:, c, :], w[:, 96 * c:96 * c + 96], staged[:, half, m, :],
                                                 start=True, stop=True)
                        last.then_inc(qk_done, 1)
                        pe.wait_ge(v_copied, n)
                        for q in range(TT):
                            last = pe.matmul(v_ps[:, q, 0:NH * PAD], staged[:, half, 2, P * q:P * q + P], wv[:, :],
                                             start=True, stop=True)
                        last.then_inc(v_done, 1)

            def split_parts(eng, m, n):
                eng.wait_ge(full_done, n * 4 + 2 * m + 2)
                eng.tensor_tensor(rest[m][:, :, :], full[m][:, :, :], parts[m][:, 0, :, :], ALU.subtract).then_inc(split[m], 1)
                eng.tensor_tensor(parts[m][:, 1, :, :], full[m][:, :, :], parts[m][:, 0, :, :], ALU.subtract).then_inc(split[m], 1)
                eng.wait_ge(split[m], n * 3 + 2)
                eng.tensor_tensor(parts[m][:, 2, :, :], rest[m][:, :, :], parts[m][:, 1, :, :], ALU.subtract).then_inc(split[m], 1)

            @block.gpsimd
            def _(pool):
                with pool.Fori(0, NB) as b:
                    split_parts(pool, 0, layer * NB + b)

            @block.vector
            def _(dve):
                dve.sem_inc(restored, 1)
                with dve.Fori(0, NB // 2) as it:
                    for half in range(2):
                        n = layer * NB + it * 2 + half
                        b = it * 2 + half
                        dve.wait_ge(staged_done, n * NG + NG)
                        dve.tensor_copy(hT[:, bass.ds(b, 1), :, :].rearrange("p b g t -> p (b g) t"),
                                        staged[:, half, :, :]).then_inc(restored, 1)
                        dve.wait_ge(v_done, layer * (NB + 1) + b + 2)
                        dve.wait_ge(v_stored, n * (16 * NG))
                        dve.tensor_scalar(v_sb[:, :, :], v_ps[:, :, 0:NH * PAD], 0.0, None, ALU.max).then_inc(v_copied, 1)
                        split_parts(dve, 1, n)

            @block.sync
            def _(sp):
                with sp.Fori(0, NB) as b:
                    n = layer * NB + b
                    sp.wait_ge(v_copied, n + 1)
                    for g in range(NG):
                        sp.dma_start(v_rows[bass.ds(b * (NG * SEQ) + g * SEQ, SEQ), :].rearrange("(q p) c -> p q c", p=P),
                                     v_sb[:, :, P * g:P * g + P]).then_inc(v_stored, 16)
                    for m, dram in enumerate((q_parts, k_parts)):
                        sp.wait_ge(split[m], n * 3 + 3)
                        for k in range(3):
                            sp.dma_start(dram[bass.ds(b * D + k * (NB * D), D), :].rearrange("(c p) t -> p c t", c=2),
                                         parts[m][:, k, :, :]).then_inc(stored[m], 16)
                sp.wait_ge(stored[0], (layer + 1) * (16 * STORES * NB))
                sp.wait_ge(stored[1], (layer + 1) * (16 * STORES * NB))
                sp.wait_ge(v_stored, (layer + 1) * (16 * NG * NB))
                sp.sem_inc(all_stored, 1)


def token_attention(nc, layer, hT_u, idn, idn_b, stats, q_parts, k_parts, v_rows, SCALE, UNITS, SLOTS):
    ROWS = 96 + 3
    with ExitStack() as part:
        pt = Store(nc, part, "att")
        q_sb = pt.sb("q_sb", [ROWS, SLOTS, GH, SEQ], BF16)
        k_sb = pt.sb("k_sb", [ROWS, SLOTS, GH, SEQ], BF16)
        v_sb = pt.sb("v_sb", [P, SLOTS, TT, P])
        probs = pt.sb("probs", [P, 2, GH, SEQ])
        neg_max = pt.sb("neg_max", [P, 2, GH, TT])
        max_rest = pt.sb("max_rest", [P, GH, TT])
        max_parts = pt.sb("max_parts", [P, 2, 3, GH, TT], BF16)
        max_rows = pt.sb("max_rows", [3 * GH, SEQ], BF16)
        o_raw = pt.sb("o_raw", [P, SEQ])
        o_norm = pt.sb("o_norm", [P, TT, GH, PAD])
        recip = pt.sb("recip", [P, TT, GH])
        s_ps = pt.ps("s_ps", [P, 2, SEQ])
        st_ps = pt.ps("st_ps", [P, GH, SEQ])
        o_ps = pt.ps("o_ps", [P, SEQ])
        misc = pt.ps("misc", [P, SEQ])
        misc_b = misc[0:3 * GH, :].bitcast(BF16)[:, 0:SEQ]
        loaded = [pt.sem(f"loaded{s}") for s in range(SLOTS)]
        s_done, s_read = pt.sem("s_done"), pt.sem("s_read")
        st_done, exp_done, pv_done = pt.sem("st_done"), pt.sem("exp_done"), pt.sem("pv_done")
        o_copied, o_turned, o_normed, o_back, h_added = (
            pt.sem("o_copied"), pt.sem("o_turned"), pt.sem("o_normed"), pt.sem("o_back"), pt.sem("h_added"))
        max_split, rows_turned, rows_copied, rows_sent = (
            pt.sem("max_split"), pt.sem("rows_turned"), pt.sem("rows_copied"), pt.sem("rows_sent"))
        all_sent = pt.sem("all_sent")
        own, ones_set, recip_done = pt.sem("own"), pt.sem("ones_set"), pt.sem("recip_done")
        LOADS = 13
        TURNS = UNITS // SLOTS

        with nc.Block() as block:

            def load(sp, s, u):
                for dst, src, order in ((q_sb, q_parts, (0, 1, 2, 0, 1, 0)), (k_sb, k_parts, (0, 0, 0, 1, 1, 2))):
                    for at, k in enumerate(order):
                        rows = src[bass.ds(u * (GH * HD) + k * (NB * D), GH * HD), :]
                        sp.dma_start(dst[HD * at:HD * at + HD, s, :, :],
                                     rows.rearrange("(h r) t -> r h t", h=GH)).then_inc(loaded[s], 16)
                sp.dma_start(v_sb[:, s, :, :], v_rows[bass.ds(u * SEQ, SEQ), :].rearrange("(q p) c -> p q c", p=P)
                             ).then_inc(loaded[s], 16)

            @block.sync
            def _(sp):
                for s in range(SLOTS):
                    load(sp, s, s)

                def send(s, u):
                    n = layer * UNITS + u
                    sp.wait_ge(rows_copied, n + 1)
                    sp.dma_start(q_sb[96:99, s % SLOTS, :, :], max_rows[:, :]).then_inc(rows_sent, 16)

                send(0, 0)
                with sp.Fori(0, TURNS - 1) as turn:
                    for s in range(SLOTS):
                        u = turn * SLOTS + s
                        send(s + 1, u + 1)
                        sp.wait_ge(pv_done, (layer * UNITS + u) * TT + TT)
                        load(sp, s, u + SLOTS)
                for s in range(SLOTS - 1):
                    send(s + 1, (TURNS - 1) * SLOTS + s + 1)
                sp.wait_ge(rows_sent, (layer + 1) * (16 * UNITS))
                sp.sem_inc(all_sent, 1)

            def score_rows(pe, s, u, q):
                n = layer * UNITS + u
                for h in range(GH):
                    m = 4 * q + h
                    pe.wait_ge(s_read, n * 16 + max(m - 1, 0))
                    pe.matmul(s_ps[:, m % 2, :], q_sb[0:96, s, h, P * q:P * q + P], k_sb[0:96, s, h, :],
                              start=True, stop=True).then_inc(s_done, 1)

            def turn_maxima(pe, s, u):
                n = layer * UNITS + u
                pe.wait_ge(max_split, n + 1)
                for q in range(TT):
                    last = pe.transpose(misc_b[:, P * q:P * q + P],
                                        max_parts[:, s % 2, :, :, q].rearrange("p k h -> p (k h)"), idn_b[:, :])
                last.then_inc(rows_turned, 1)

            @block.tensor
            def _(pe):
                for s in range(2):
                    pe.wait_ge(loaded[s], (layer * TURNS + 1) * (16 * LOADS))
                    for q in range(TT):
                        score_rows(pe, s, s, q)
                turn_maxima(pe, 0, 0)
                pe.wait_ge(ones_set, layer * 2 + 2)

                def turn_out(n, rows):
                    pe.wait_ge(o_copied, n + 1)
                    pe.wait_ge(rows_copied, rows)
                    for q in range(TT):
                        last = pe.transpose(misc[:, P * q:P * q + P], o_raw[:, P * q:P * q + P], idn[:, :])
                    last.then_inc(o_turned, 1)

                def turn_back(n):
                    pe.wait_ge(o_normed, n + 1)
                    for q in range(TT):
                        last = pe.transpose(misc[:, P * q:P * q + P],
                                            o_norm[:, q, :, :].rearrange("p h c -> p (h c)"), idn[:, :])
                    last.then_inc(o_back, 1)

                def unit(s, u, turn, ahead, following, first):
                    n = layer * UNITS + u
                    s2, s1 = (s + 2) % SLOTS, (s + 1) % SLOTS
                    pe.wait_ge(rows_sent, n * 16 + 16)
                    if ahead:
                        pe.wait_ge(loaded[s2], (layer * TURNS + turn + (2 if s + 2 >= SLOTS else 1)) * (16 * LOADS))

                    def scores(t):
                        for half in range(2):
                            pe.wait_ge(exp_done, n * 8 + (2 * t + half - 1 if t else 0))
                            for h in (2 * half, 2 * half + 1):
                                last = pe.matmul(st_ps[:, h, :], k_sb[0:ROWS, s, h, P * t:P * t + P], q_sb[0:ROWS, s, h, :],
                                                 start=True, stop=True)
                            last.then_inc(st_done, 1)

                    def values(t):
                        pe.wait_ge(exp_done, n * 8 + 2 * t + 2)
                        if t == 0:
                            pe.wait_ge(o_copied, n)
                        for h in range(GH):
                            last = pe.matmul(o_ps[PAD * h:PAD * h + PAD, :], v_sb[:, s, t, PAD * h:PAD * h + PAD],
                                             probs[:, t % 2, h, :], start=(t == 0), stop=(t == TT - 1))
                        last.then_inc(pv_done, 1)

                    scores(0)
                    if ahead:
                        score_rows(pe, s2, u + 2, 0)
                    if not first:
                        turn_out(n - 1, n + 1)
                    scores(1)
                    values(0)
                    if ahead:
                        score_rows(pe, s2, u + 2, 1)
                    if not first:
                        turn_back(n - 1)
                    scores(2)
                    values(1)
                    if ahead:
                        score_rows(pe, s2, u + 2, 2)
                    if following:
                        if not first:
                            pe.wait_ge(h_added, n)
                        turn_maxima(pe, s1, u + 1)
                    scores(3)
                    values(2)
                    if ahead:
                        score_rows(pe, s2, u + 2, 3)
                    values(3)

                for s in range(SLOTS):
                    unit(s, s, 0, True, True, s == 0)
                with pe.Fori(1, TURNS - 1) as turn:
                    for s in range(SLOTS):
                        unit(s, turn * SLOTS + s, turn, True, True, False)
                for s in range(SLOTS):
                    unit(s, (TURNS - 1) * SLOTS + s, TURNS - 1, s < SLOTS - 2, s < SLOTS - 1, False)
                end = (layer + 1) * UNITS
                pe.wait_ge(h_added, end - 1)
                turn_out(end - 1, end)
                turn_back(end - 1)

            @block.scalar
            def _(act):
                def copy_out(n):
                    act.wait_ge(pv_done, n * TT + TT)
                    act.wait_ge(o_turned, n)
                    act.activation(o_raw[:, :], o_ps[:, :], ACT.Copy).then_inc(o_copied, 1)

                def unit(s, u, first):
                    n = layer * UNITS + u
                    for t in range(TT):
                        for half in range(2):
                            act.wait_ge(st_done, n * 8 + 2 * t + half + 1)
                            if t >= 2:
                                act.wait_ge(pv_done, n * TT + t - 1)
                            else:
                                act.wait_ge(pv_done, n * TT if t == 1 or first else n * TT - 1)
                            act.activation(probs[:, t % 2, 2 * half:2 * half + 2, :], st_ps[:, 2 * half:2 * half + 2, :],
                                           ACT.Exp, scale=SCALE).then_inc(exp_done, 1)
                        if t == 0 and not first:
                            copy_out(n - 1)

                for s in range(SLOTS):
                    unit(s, s, s == 0)
                with act.Fori(1, TURNS) as turn:
                    for s in range(SLOTS):
                        unit(s, turn * SLOTS + s, False)
                copy_out(layer * UNITS + UNITS - 1)

            @block.gpsimd
            def _(pool):
                pool.memset(k_sb[96:99, :, :, :].rearrange("p s h t -> p (s h t)"), 1.0).then_inc(ones_set, 1)

            @block.vector
            def _(dve):
                def maxima(s, u, q):
                    n = layer * UNITS + u
                    for h in range(GH):
                        m = 4 * q + h
                        dve.wait_ge(s_done, n * 16 + m + 1)
                        dve.tensor_reduce(neg_max[:, s % 2, h, q:q + 1], s_ps[:, m % 2, :], AX.X, ALU.max,
                                          negate=True).then_inc(s_read, 1)

                def split_maxima(s, u):
                    n = layer * UNITS + u
                    dve.wait_ge(s_read, n * 16 + 16)
                    if isinstance(u, int) and u < 2:
                        dve.wait_ge(rows_turned, layer * UNITS)
                    else:
                        dve.wait_ge(rows_turned, n - 1)
                    mp = max_parts[:, s % 2, :, :, :]
                    nm = neg_max[:, s % 2, :, :]
                    dve.tensor_copy(mp[:, 0, :, :], nm).then_inc(own, 1)
                    dve.wait_ge(own, n * 3 + 1)
                    dve.tensor_tensor(max_rest[:, :, :], nm, mp[:, 0, :, :], ALU.subtract).then_inc(own, 1)
                    dve.wait_ge(own, n * 3 + 2)
                    dve.tensor_copy(mp[:, 1, :, :], max_rest[:, :, :]).then_inc(own, 1)
                    dve.wait_ge(own, n * 3 + 3)
                    dve.tensor_tensor(mp[:, 2, :, :], max_rest[:, :, :], mp[:, 1, :, :], ALU.subtract).then_inc(max_split, 1)

                def copy_rows(s, u):
                    n = layer * UNITS + u
                    dve.wait_ge(rows_turned, n + 1)
                    dve.wait_ge(rows_sent, n * 16)
                    dve.tensor_copy(max_rows[:, :], misc_b).then_inc(rows_copied, 1)

                def normalise(n):
                    dve.wait_ge(o_turned, n + 1)
                    o = misc[:, :].rearrange("p (q h c) -> p q h c", q=TT, h=GH)
                    dve.reciprocal(recip[:, :, :], o[:, :, :, HD]).then_inc(recip_done, 1)
                    dve.wait_ge(recip_done, n + 1)
                    dve.wait_ge(ones_set, layer * 2 + 2)
                    dve.wait_ge(o_back, n)
                    for q in range(TT):
                        ins = dve.tensor_tensor(o_norm[:, q, :, 0:HD], o[:, q, :, 0:HD],
                                                recip[:, q, :].unsqueeze(2).to_broadcast([P, GH, HD]), ALU.mult)
                    ins.then_inc(o_normed, 1)

                def add(n, u):
                    dve.wait_ge(o_back, n + 1)
                    dst = hT_u[:, bass.ds(u, 1), :].rearrange("p u t -> p (u t)")
                    dve.tensor_tensor(dst, dst, misc[:, :], ALU.add).then_inc(h_added, 1)

                dve.memset(o_norm[:, :, :, :], 0.0).then_inc(ones_set, 1)
                for s in range(2):
                    for q in range(TT):
                        maxima(s, s, q)
                    split_maxima(s, s)
                copy_rows(0, 0)

                def unit(s, u, ahead, following, first):
                    n = layer * UNITS + u
                    if ahead:
                        maxima(s + 2, u + 2, 0)
                    if not first:
                        normalise(n - 1)
                    if ahead:
                        maxima(s + 2, u + 2, 1)
                    if not first:
                        add(n - 1, u - 1)
                    if ahead:
                        maxima(s + 2, u + 2, 2)
                    if following:
                        copy_rows(s + 1, u + 1)
                    if ahead:
                        maxima(s + 2, u + 2, 3)
                        split_maxima(s + 2, u + 2)

                for s in range(SLOTS):
                    unit(s, s, True, True, s == 0)
                with dve.Fori(1, TURNS - 1) as turn:
                    for s in range(SLOTS):
                        unit(s, turn * SLOTS + s, True, True, False)
                for s in range(SLOTS):
                    unit(s, (TURNS - 1) * SLOTS + s, s < SLOTS - 2, s < SLOTS - 1, False)
                normalise(layer * UNITS + UNITS - 1)
                add(layer * UNITS + UNITS - 1, UNITS - 1)
                with dve.Fori(0, NB) as b:
                    dve.wait_ge(h_added, (layer + 1) * UNITS)
                    for g in range(NG):
                        dve.bn_stats(stats[:, g, bass.ds(b, 1), :].rearrange("p b k -> p (b k)"),
                                     hT_u[:, bass.ds(b * NG + g, 1), :].rearrange("p u t -> p (u t)"))


def token_norm(nc, layer, which, stats, mean_var, power, affine, norm):
    with ExitStack() as part:
        pt = Store(nc, part, f"norm{which}")
        own, var_done, pow_done = pt.sem("own"), pt.sem("var_done"), pt.sem("pow_done")
        scale, shift = norm[:, which, 0, :], norm[:, which, 1, :]
        with nc.Block() as block:

            @block.vector
            def _(dve):
                for g in range(NG):
                    dve.bn_aggr(mean_var[:, g, :], stats[:, g, :, :].rearrange("p b k -> p (b k)")).then_inc(own, 1)
                dve.wait_ge(own, layer * 5 + 3)
                dve.memset(power[:, 1, :], -0.5).then_inc(var_done, 1)
                dve.tensor_scalar(power[:, 0, :], mean_var[:, :, 1], EPS, None, ALU.add).then_inc(var_done, 1)
                dve.wait_ge(pow_done, layer + 1)
                dve.tensor_tensor(scale, power[:, 0, :], affine[:, :, 2 * which], ALU.mult).then_inc(own, 1)
                dve.wait_ge(own, layer * 5 + 4)
                dve.tensor_tensor(shift, mean_var[:, :, 0], scale, ALU.mult).then_inc(own, 1)
                dve.wait_ge(own, layer * 5 + 5)
                dve.tensor_tensor(shift, affine[:, :, 2 * which + 1], shift, ALU.subtract)

            @block.gpsimd
            def _(pool):
                pool.wait_ge(var_done, layer * 2 + 2)
                pool.tensor_tensor(power[:, 0, :], power[:, 0, :], power[:, 1, :], ALU.pow).then_inc(pow_done, 1)


def token_dense(nc, layer, hT, wf, norm, stats):
    with ExitStack() as part:
        pt = Store(nc, part, "dense")
        staged = pt.sb("staged", [P, 2, NG, SEQ])
        out_ps = pt.ps("out_ps", [P, 2, 4, SEQ])
        staged_done, product_done, added, stats_done = (
            pt.sem("staged_done"), pt.sem("product_done"), pt.sem("added"), pt.sem("stats_done"))
        with nc.Block() as block:

            @block.scalar
            def _(act):
                with act.Fori(0, NB // 2) as it:
                    for half in range(2):
                        b = it * 2 + half
                        n = layer * NB + b
                        act.wait_ge(added, layer * (NB + 1) + b)
                        for g in range(NG):
                            act.activation(staged[:, half, g, :], hT[:, bass.ds(b, 1), g, :].rearrange("p b t -> p (b t)"),
                                           ACT.Identity, bias=norm[:, 0, 1, g:g + 1],
                                           scale=norm[:, 0, 0, g:g + 1]).then_inc(staged_done, 1)

            @block.tensor
            def _(pe):
                with pe.Fori(0, NB // 2) as it:
                    for half in range(2):
                        b = it * 2 + half
                        pe.wait_ge(staged_done, (layer * NB + b) * NG + NG)
                        pe.wait_ge(added, layer * (NB + 1) + b)
                        for m in range(NG):
                            for g in range(NG):
                                last = pe.matmul(out_ps[:, half, m, :], wf[:, g, P * m:P * m + P], staged[:, half, g, :],
                                                 start=(g == 0), stop=(g == NG - 1))
                        last.then_inc(product_done, 1)

            @block.vector
            def _(dve):
                dve.sem_inc(added, 1)
                with dve.Fori(0, NB // 2) as it:
                    for half in range(2):
                        b = it * 2 + half
                        n = layer * NB + b
                        dve.wait_ge(product_done, n + 1)
                        dve.tensor_tensor(hT[:, bass.ds(b, 1), :, :].rearrange("p b g t -> p (b g) t"),
                                          out_ps[:, half, 0:NG, :], staged[:, half, :, :], ALU.add).then_inc(added, 1)
                        dve.wait_ge(added, layer * (NB + 1) + b + 2)
                        for g in range(NG):
                            ins = dve.bn_stats(stats[:, g, bass.ds(b, 1), :].rearrange("p b k -> p (b k)"),
                                               hT[:, bass.ds(b, 1), g, :].rearrange("p b t -> p (b t)"))
                        ins.then_inc(stats_done, 1)


C2 = D // 2
GROUPS = TILES // TT


def row_semaphores(nc):
    rows = [nc.alloc_semaphore(name=f"row_{n}") for n in ("stats_done", "aggr_done", "var_done", "pow_done")]
    turns = [nc.alloc_semaphore(name=f"turn_{n}") for n in ("rows_done", "turned_done", "copied", "added")]
    return rows, turns


def row_statistics(nc, sems, call, H, mean, rstd):
    with ExitStack() as part:
        pt = Store(nc, part, f"row_stats{call}")
        stats = pt.sb("stats", [P, TILES, 6])
        mean_var = pt.sb("mean_var", [P, TILES, 2])
        var = pt.sb("var", [P, TILES])
        half = pt.sb("half", [P, TILES])
        stats_done, aggr_done, var_done, pow_done = sems
        before = call * TILES
        with nc.Block() as block:

            @block.vector
            def _(dve):
                with dve.Fori(0, TILES // TT) as i:
                    for k in range(TT):
                        t = bass.ds(i * TT + k, 1)
                        dve.bn_stats(stats[:, t, :].rearrange("p t k -> p (t k)"),
                                     H[:, t, :].rearrange("p t d -> p (t d)")).then_inc(stats_done, 1)
                for t in range(TILES):
                    if t % 16 == 0:
                        dve.wait_ge(stats_done, before + t + 16)
                    dve.bn_aggr(mean_var[:, t, :], stats[:, t, :]).then_inc(aggr_done, 1)
                dve.wait_ge(aggr_done, before + TILES)
                dve.memset(half[:, :], -0.5).then_inc(var_done, 1)
                dve.tensor_copy(mean[:, :], mean_var[:, :, 0])
                dve.tensor_scalar(var[:, :], mean_var[:, :, 1], EPS, None, ALU.add).then_inc(var_done, 1)

            @block.gpsimd
            def _(pool):
                pool.wait_ge(var_done, call * 2 + 2)
                pool.tensor_tensor(rstd[:, :], var[:, :], half[:, :], ALU.pow).then_inc(pow_done, 1)


def turn_rows(nc, sems, call, X, mean, rstd, idn, xT, add_to=None, gamma_beta=None):
    with ExitStack() as part:
        pt = Store(nc, part, f"turn_rows{call}")
        rows = pt.sb("rows", [P, 2, TT, D])
        turned = pt.ps("turned", [C2, 2, 2, SEQ])
        rows_done, turned_done, copied, added = sems
        turns = call * (GROUPS + 1)
        with nc.Block() as block:

            @block.vector
            def _(dve):
                with dve.Fori(0, GROUPS // 2) as it:
                    for half in range(2):
                        g = it * 2 + half
                        dve.wait_ge(turned_done, turns + g)
                        for k in range(TT):
                            t = bass.ds(g * TT + k, 1)
                            dve.tensor_scalar(rows[:, half, k, :], X[:, t, :].rearrange("p t d -> p (t d)"),
                                              mean[:, t], rstd[:, t], ALU.subtract, ALU.mult).then_inc(rows_done, 1)
                        if add_to is not None:
                            dve.wait_ge(rows_done, call * TILES + g * TT + TT)
                            dst = add_to[:, bass.ds(g * TT, TT), :]
                            dve.tensor_tensor(dst, dst, rows[:, half, :, :], ALU.add).then_inc(added, 1)

            @block.tensor
            def _(pe):
                pe.sem_inc(turned_done, 1)
                with pe.Fori(0, GROUPS // 2) as it:
                    for half in range(2):
                        g = it * 2 + half
                        pe.wait_ge(rows_done, call * TILES + g * TT + TT)
                        pe.wait_ge(copied, turns * 2 + g * 2)
                        for c in range(2):
                            for k in range(TT):
                                last = pe.transpose(turned[:, half, c, P * k:P * k + P], rows[:, half, k, C2 * c:C2 * c + C2],
                                                    idn[:, :])
                        last.then_inc(turned_done, 1)

            @block.scalar
            def _(act):
                act.sem_inc(copied, 2)
                with act.Fori(0, GROUPS // 2) as it:
                    for half in range(2):
                        g = it * 2 + half
                        act.wait_ge(turned_done, turns + g + 2)
                        for c in range(2):
                            dst = xT[:, c, bass.ds(g * SEQ, SEQ)]
                            if gamma_beta is None:
                                act.activation(dst, turned[:, half, c, :], ACT.Copy).then_inc(copied, 1)
                            else:
                                act.activation(dst, turned[:, half, c, :], ACT.Identity, bias=gamma_beta[:, c, 1:2],
                                               scale=gamma_beta[:, c, 0:1]).then_inc(copied, 1)


def normalise_rows(nc, name, H, mean, rstd, X):
    normed, added = nc.alloc_semaphore(name=f"{name}_normed"), nc.alloc_semaphore(name=f"{name}_added")
    with nc.Block() as block:

        @block.vector
        def _(dve):
            with dve.Fori(0, GROUPS) as g:
                for k in range(TT):
                    t = bass.ds(g * TT + k, 1)
                    dve.tensor_scalar(X[:, t, :].rearrange("p t d -> p (t d)"), H[:, t, :].rearrange("p t d -> p (t d)"),
                                      mean[:, t], rstd[:, t], ALU.subtract, ALU.mult).then_inc(normed, 1)
                dve.wait_ge(normed, g * TT + TT)
                four = bass.ds(g * TT, TT)
                dve.tensor_tensor(H[:, four, :], H[:, four, :], X[:, four, :], ALU.add).then_inc(added, 1)


def feed_forward(nc, name, H, xT, experts, hidden, w_in, w_out, func, bias=None, gates=None):
    M = hidden // P
    PAIRS = GROUPS // 2
    with ExitStack() as part:
        pt = Store(nc, part, name)
        copies = min(2, experts)
        w1 = pt.sb("w1", [C2, copies, 2, hidden])
        w2 = pt.sb("w2", [P, copies, M, D])
        hid = pt.sb("hid", [P, 2, M, SEQ])
        hid_ps = pt.ps("hid_ps", [P, 4, SEQ])
        out_ps = pt.ps("out_ps", [P, 2, 2, SEQ])
        w_in_sem = [pt.sem(f"weights_in{c}") for c in range(copies)]
        hid_done, func_done, out_done, added = (
            pt.sem("hid_done"), pt.sem("func_done"), pt.sem("out_done"), pt.sem("added"))
        with nc.Block() as block:

            def over_experts(eng, body):
                if experts == 1:
                    body(0, 0)
                else:
                    with eng.Fori(0, experts // 2) as pair:
                        for c in range(2):
                            body(pair * 2 + c, c)

            @block.sync
            def _(sp):
                def load(e, c):
                    sp.dma_start(w1[:, c, :, :], w_in(e)).then_inc(w_in_sem[c], 16)
                    sp.dma_start(w2[:, c, :, :], w_out(e)).then_inc(w_in_sem[c], 16)

                for c in range(copies):
                    load(c, c)
                if experts > 2:
                    with sp.Fori(0, experts // 2 - 1) as pair:
                        for c in range(2):
                            e = pair * 2 + c
                            sp.wait_ge(out_done, e * GROUPS + GROUPS + 1)
                            load(e + 2, c)

            @block.tensor
            def _(pe):
                def first(e, c, g, half):
                    n = e * GROUPS + g
                    for m in range(M):
                        at = (half * M + m) % 4
                        pe.wait_ge(func_done, n * M + m)
                        for k in range(2):
                            last = pe.matmul(hid_ps[:, at, :], w1[:, c, k, P * m:P * m + P], xT[:, k, bass.ds(g * SEQ, SEQ)],
                                             start=(k == 0), stop=(k == 1))
                        last.then_inc(hid_done, 1)

                def second(e, c, g, half):
                    n = e * GROUPS + g
                    pe.wait_ge(func_done, n * M + M + 3)
                    pe.wait_ge(added, n * TT)
                    for k in range(TT):
                        for m in range(M):
                            last = pe.matmul(out_ps[:, half, k // 2, D * (k % 2):D * (k % 2) + D], hid[:, half, m, P * k:P * k + P],
                                             w2[:, c, m, :], start=(m == 0), stop=(m == M - 1))
                    last.then_inc(out_done, 1)

                def expert(e, c):
                    pe.wait_ge(w_in_sem[c], (e - c) * 16 + 32 if experts > 1 else 32)
                    first(e, c, 0, 0)
                    with pe.Fori(0, PAIRS - 1) as it:
                        first(e, c, it * 2 + 1, 1)
                        second(e, c, it * 2, 0)
                        first(e, c, it * 2 + 2, 0)
                        second(e, c, it * 2 + 1, 1)
                    first(e, c, GROUPS - 1, 1)
                    second(e, c, GROUPS - 2, 0)
                    second(e, c, GROUPS - 1, 1)

                pe.sem_inc(out_done, 1)
                over_experts(pe, expert)

            @block.scalar
            def _(act):
                def group(n, half):
                    act.wait_ge(out_done, n)
                    for m in range(M):
                        act.wait_ge(hid_done, n * M + m + 1)
                        if bias is None:
                            act.activation(hid[:, half, m, :], hid_ps[:, (half * M + m) % 4, :], func).then_inc(func_done, 1)
                        else:
                            act.activation(hid[:, half, m, :], hid_ps[:, (half * M + m) % 4, :], func,
                                           bias=bias[:, m:m + 1]).then_inc(func_done, 1)

                act.sem_inc(func_done, 3)
                with act.Fori(0, experts * PAIRS) as it:
                    for half in range(2):
                        group(it * 2 + half, half)

            @block.vector
            def _(dve):
                def expert(e, c):
                    with dve.Fori(0, PAIRS) as it:
                        for half in range(2):
                            g = it * 2 + half
                            n = e * GROUPS + g
                            dve.wait_ge(out_done, n + 2)
                            for k in range(TT):
                                dst = H[:, bass.ds(g * TT + k, 1), :].rearrange("p t d -> p (t d)")
                                out = out_ps[:, half, k // 2, D * (k % 2):D * (k % 2) + D]
                                if gates is None:
                                    dve.tensor_tensor(dst, out, dst, ALU.add).then_inc(added, 1)
                                else:
                                    gate = gates[:, bass.ds((g * TT + k) * experts + e, 1)]
                                    dve.scalar_tensor_tensor(dst, out, gate, dst, ALU.mult, ALU.add).then_inc(added, 1)

                dve.sem_inc(added, TT)
                over_experts(dve, expert)


WIN = 5
COLS = P // NB
SPAN = COLS + WIN - 1
KEYS = NB * SPAN
HID = 96
HEADS, DH = 4, 24
RPB = 2 * WIN - 1
UROWS = 2 * NB - 1


def neighborhood_stage(nc, h1, h2, weights, turned, small, const, row_sems, turn_sems):
    fc1_b, convA_b, convB_b, qkv_b, rpb, proj_b, fc2_b = weights
    fc1_t, convA_t, convB_t, qkv_t, proj_t, fc2_t = turned
    shifts = small
    with ExitStack() as stage:
        st = Store(nc, stage, "near")
        H = st.sb("H", [P, TILES, D])
        idn = st.sb("idn", [P, P])
        xs = st.sb("xs", [HID + 1, NB, SEQ + WIN - 1])
        table = st.sb("table", [P, 3, HEADS, KEYS])
        in_sem, out_sem, zero_done = st.sem("in"), st.sem("out"), st.sem("zero_done")

        with ExitStack() as part:
            pt = Store(nc, part, "near_load")
            bias = pt.sb("bias", [P, HEADS, KEYS])
            mask = pt.sb("mask", [P, 3, KEYS])
            zeros = pt.sb("zeros", [HID, COLS * HEADS * UROWS * SPAN // HID])
            shifted = pt.sem("shifted")
            with nc.Block() as block:

                @block.gpsimd
                def _(pool):
                    pool.memset(zeros[:, :], 0.0).then_inc(zero_done, 1)
                    pool.memset(xs[0:HID, :, :].rearrange("p b w -> p (b w)"), 0.0).then_inc(zero_done, 1)
                    pool.memset(xs[HID:, :, :].rearrange("p b w -> p (b w)"), 1.0).then_inc(zero_done, 1)

                @block.sync
                def _(sp):
                    for b in range(NB):
                        sp.dma_start(H[COLS * b:COLS * b + COLS, :, :],
                                     h1[SEQ * b:SEQ * b + SEQ, :].rearrange("(j w) d -> w j d", w=COLS)).then_inc(in_sem, 16)
                    sp.dma_start(idn[:, :], const["ident"]).then_inc(in_sem, 16)
                    sp.dma_start(mask[:, :, :], const["near_mask"].rearrange("p (v k) -> p v k", v=3)).then_inc(in_sem, 16)
                    sp.wait_ge(zero_done, 1)
                    sp.dma_start(shifts.rearrange("w n u c -> (w n u c)").rearrange("(p k) -> p k", p=HID),
                                 zeros[:, :]).then_inc(shifted, 16)
                    sp.wait_ge(shifted, 16)
                    half = WIN // 2
                    for w in range(COLS):
                        c0, c1 = max(0, w - half), min(SPAN, w + half + WIN)
                        r0 = c0 - half - w + WIN - 1
                        sp.dma_start(shifts[w, :, NB - WIN:NB - WIN + RPB, c0:c1], rpb[:, :, r0:r0 + c1 - c0]).then_inc(shifted, 16)
                    sp.wait_ge(shifted, 16 * (1 + COLS))
                    for b in range(NB):
                        sp.dma_start(bias[COLS * b:COLS * b + COLS, :, :].rearrange("w n (b c) -> w n b c", b=NB),
                                     shifts[:, :, NB - 1 - b:2 * NB - 1 - b, :]).then_inc(in_sem, 16)
                    sp.wait_ge(in_sem, 16 * (2 * NB + 2))

                @block.vector
                def _(dve):
                    dve.wait_ge(in_sem, 16 * (2 * NB + 2))
                    for v in range(3):
                        dve.tensor_tensor(table[:, v, :, :], bias[:, :, :],
                                          mask[:, v, :].unsqueeze(1).to_broadcast([P, HEADS, KEYS]), ALU.add)

        with ExitStack() as part:
            pt = Store(nc, part, "near_in")
            mean = pt.sb("mean", [P, TILES])
            rstd = pt.sb("rstd", [P, TILES])
            xT = pt.sb("xT", [C2, 2, TOKENS])
            row_statistics(nc, row_sems, 0, H, mean, rstd)
            turn_rows(nc, turn_sems, 0, H, mean, rstd, idn, xT, add_to=H)
            CA = 64
            w1 = pt.sb("w1", [C2, 2, HID])
            wa = pt.sb("wa", [HID, CA])
            wb = pt.sb("wb", [CA, HID])
            b1 = pt.sb("b1", [HID, 1])
            ba = pt.sb("ba", [CA, 1])
            bb = pt.sb("bb", [HID, 1])
            x1 = pt.sb("x1", [HID, 2, SEQ])
            mid = pt.sb("mid", [CA, 2, SEQ])
            total = pt.sb("total", [HID, 2, SEQ])
            x1_ps = pt.ps("x1_ps", [HID, 2, SEQ])
            mid_ps = pt.ps("mid_ps", [CA, 2, SEQ])
            total_ps = pt.ps("total_ps", [HID, 2, SEQ])
            loaded, x1_done, x1_copied = pt.sem("loaded"), pt.sem("x1_done"), pt.sem("x1_copied")
            mid_done, mid_copied = pt.sem("mid_done"), pt.sem("mid_copied")
            total_done, summed, gelu_done = pt.sem("total_done"), pt.sem("summed"), pt.sem("gelu_done")
            nc.scalar.preload_act_table(ACT.Gelu)
            with nc.Block() as block:

                @block.sync
                def _(sp):
                    sp.dma_start(w1[:, :, :], fc1_t).then_inc(loaded, 16)
                    sp.dma_start(wa[:, :], convA_t.rearrange("p a n -> p (a n)")).then_inc(loaded, 16)
                    sp.dma_start(wb[:, :], convB_t.rearrange("p a n -> p (a n)")).then_inc(loaded, 16)
                    for dst, src in ((b1, fc1_b), (ba, convA_b), (bb, convB_b)):
                        sp.dma_start(dst[:, :], src.rearrange("(p a) -> p a", a=1)).then_inc(loaded, 16)
                    sp.wait_ge(loaded, 16 * 6)

                @block.tensor
                def _(pe):
                    def front(g, half):
                        pe.wait_ge(x1_copied, g)
                        for c in range(2):
                            last = pe.matmul(x1_ps[:, half, :], w1[:, c, :], xT[:, c, bass.ds(g * SEQ, SEQ)], start=(c == 0), stop=(c == 1))
                        last.then_inc(x1_done, 1)

                    def middle(g, half):
                        pe.wait_ge(x1_copied, g + 3)
                        pe.wait_ge(mid_copied, g)
                        pe.matmul(mid_ps[:, half, :], wa[:, :], x1[:, half, :], start=True, stop=True).then_inc(mid_done, 1)

                    def back(g, half):
                        pe.wait_ge(mid_copied, g + 3)
                        pe.wait_ge(summed, g)
                        pe.matmul(total_ps[:, half, :], wb[:, :], mid[:, half, :], start=True, stop=True).then_inc(total_done, 1)

                    pe.wait_ge(loaded, 16 * 6)
                    front(0, 0)
                    middle(0, 0)
                    with pe.Fori(0, GROUPS // 2 - 1) as it:
                        for half in (1, 0):
                            g = it * 2 + (1 if half else 2)
                            front(g, half)
                            back(it * 2 + (0 if half else 1), 1 - half)
                            middle(g, half)
                    front(GROUPS - 1, 1)
                    back(GROUPS - 2, 0)
                    middle(GROUPS - 1, 1)
                    back(GROUPS - 1, 1)

                @block.scalar
                def _(act):
                    act.wait_ge(loaded, 16 * 6)
                    act.sem_inc(x1_copied, 2)
                    act.sem_inc(gelu_done, 2)

                    def front(g, half):
                        act.wait_ge(x1_done, g + 1)
                        act.wait_ge(summed, g)
                        act.activation(x1[:, half, :], x1_ps[:, half, :], ACT.Identity, bias=b1[:, :]).then_inc(x1_copied, 1)

                    def last(g, half):
                        act.wait_ge(summed, g + 3)
                        act.activation(xs[0:HID, :, bass.ds(g * (TT * COLS) + WIN // 2, TT * COLS)].rearrange("p b (k w) -> p k b w", k=TT),
                                       total[:, half, :].rearrange("p (k b w) -> p k b w", k=TT, b=NB), ACT.Gelu).then_inc(gelu_done, 1)

                    front(0, 0)
                    with act.Fori(0, GROUPS // 2 - 1) as it:
                        for half in (1, 0):
                            front(it * 2 + (1 if half else 2), half)
                            last(it * 2 + (0 if half else 1), 1 - half)
                    front(GROUPS - 1, 1)
                    last(GROUPS - 2, 0)
                    last(GROUPS - 1, 1)

                @block.vector
                def _(dve):
                    dve.wait_ge(loaded, 16 * 6)
                    dve.sem_inc(mid_copied, 2)
                    dve.sem_inc(summed, 2)

                    def middle(g, half):
                        dve.wait_ge(mid_done, g + 1)
                        dve.tensor_scalar(mid[:, half, :], mid_ps[:, half, :], ba[:, :], None, ALU.add).then_inc(mid_copied, 1)

                    def last(g, half):
                        dve.wait_ge(total_done, g + 1)
                        dve.wait_ge(gelu_done, g)
                        dve.scalar_tensor_tensor(total[:, half, :], total_ps[:, half, :], bb[:, :], x1[:, half, :],
                                                 ALU.add, ALU.add).then_inc(summed, 1)

                    middle(0, 0)
                    with dve.Fori(0, GROUPS // 2 - 1) as it:
                        for half in (1, 0):
                            last(it * 2 + (0 if half else 1), 1 - half)
                            middle(it * 2 + (1 if half else 2), half)
                    last(GROUPS - 2, 0)
                    middle(GROUPS - 1, 1)
                    last(GROUPS - 1, 1)

        with ExitStack() as part:
            pt = Store(nc, part, "near_att")
            wq = pt.sb("wq", [HID + 1, HEADS, PAD])
            wk = pt.sb("wk", [HID + 1, HEADS, PAD])
            wv = pt.sb("wv", [HID + 1, HEADS, DH + 1])
            wp = pt.sb("wp", [HID + 1, HID])
            w2 = pt.sb("w2", [HID + 1, D])
            xw = pt.sb("xw", [HID + 1, 2, KEYS])
            q_t = pt.sb("q_t", [P, 2, P])
            k_diag = pt.sb("k_diag", [P, 2, HEADS, KEYS])
            v = pt.sb("v", [KEYS // 2, 2, 2, HEADS * (DH + 1)])
            logits = pt.sb("logits", [P, HEADS, KEYS])
            shifted = pt.sb("shifted", [P, HEADS, KEYS])
            probs = pt.sb("probs", [P, 2, HEADS, KEYS])
            high = pt.sb("high", [P, HEADS])
            recip = pt.sb("recip", [P, HEADS])
            probs_t = pt.sb("probs_t", [KEYS // 2, 2, TT, P])
            att = pt.sb("att", [P, HEADS, DH])
            att_t = pt.sb("att_t", [HID + 1, P])
            proj = pt.sb("proj", [HID + 1, P])
            qk_ps = pt.ps("qk_ps", [P, SEQ])
            v_ps = pt.ps("v_ps", [P, SEQ])
            logits_ps = pt.ps("logits_ps", [P, 2, SEQ])
            turned_ps = pt.ps("turned_ps", [KEYS // 2, 2, SEQ])
            att_ps = pt.ps("att_ps", [P, SEQ])
            out_ps = pt.ps("out_ps", [P, SEQ])
            loaded, zeroed = pt.sem("loaded"), pt.sem("zeroed")
            xw_done, qkv_done, qkv_copied = pt.sem("xw_done"), pt.sem("qkv_done"), pt.sem("qkv_copied")
            logits_done, logits_read = pt.sem("logits_done"), pt.sem("logits_read")
            max_done, shifted_done, exp_done = pt.sem("max_done"), pt.sem("shifted_done"), pt.sem("exp_done")
            turned_done, turned_copied = pt.sem("turned_done"), pt.sem("turned_copied")
            pv_done, att_done, own = pt.sem("pv_done"), pt.sem("att_done"), pt.sem("own")
            end_done, end_copied, added = pt.sem("end_done"), pt.sem("end_copied"), pt.sem("added")
            SCALE = DH ** -0.5
            LOADS = 10
            HALF = KEYS // 2
            with nc.Block() as block:

                @block.sync
                def _(sp):
                    sp.wait_ge(zeroed, 5)
                    for m, dst in enumerate((wq, wk, wv)):
                        sp.dma_start(dst[0:HID, :, 0:DH], qkv_t[:, 0, HID * m:HID * m + HID].rearrange("p (h c) -> p h c", h=HEADS)).then_inc(loaded, 16)
                        sp.dma_start(dst[HID:, :, 0:DH], qkv_b[HID * m:HID * m + HID].rearrange("(a h c) -> a h c", a=1, h=HEADS)).then_inc(loaded, 16)
                    sp.dma_start(wp[0:HID, :], proj_t.rearrange("p a n -> p (a n)")).then_inc(loaded, 16)
                    sp.dma_start(wp[HID:, :], proj_b.rearrange("(a n) -> a n", a=1)).then_inc(loaded, 16)
                    sp.dma_start(w2[0:HID, :], fc2_t.rearrange("p a n -> p (a n)")).then_inc(loaded, 16)
                    sp.dma_start(w2[HID:, :], fc2_b.rearrange("(a n) -> a n", a=1)).then_inc(loaded, 16)
                    sp.wait_ge(loaded, 16 * LOADS)

                @block.gpsimd
                def _(pool):
                    for w in (wq, wk):
                        pool.memset(w[:, :, :].rearrange("p h c -> p (h c)"), 0.0).then_inc(zeroed, 1)
                    pool.memset(wv[:, :, :].rearrange("p h c -> p (h c)"), 0.0).then_inc(zeroed, 1)
                    pool.memset(k_diag[:, :, :, :].rearrange("p a h k -> p (a h k)"), 0.0).then_inc(zeroed, 1)
                    pool.wait_ge(zeroed, 4)
                    pool.memset(wv[HID:, :, DH:], 1.0).then_inc(zeroed, 1)
                    pool.memset(att_t[HID:, :], 1.0).then_inc(zeroed, 1)
                    pool.memset(proj[HID:, :], 1.0).then_inc(zeroed, 1)

            with nc.Block() as block:

                def turns(eng, turn):
                    turn(0, 0, 0)
                    with eng.Fori(0, TILES // 2 - 1) as it:
                        turn(it * 2 + 1, 1, 1)
                        turn(it * 2 + 2, 0, 1)
                    turn(TILES - 1, 1, 2)

                @block.gpsimd
                def _(pool):
                    def turn(j, half, variant):
                        pool.wait_ge(qkv_done, j)
                        pool.tensor_copy(xw[:, half, :].rearrange("p (b c) -> p b c", b=NB), xs[:, :, bass.ds(j * COLS, SPAN)]).then_inc(xw_done, 1)
                        pool.wait_ge(max_done, j + 1)
                        pool.wait_ge(exp_done, j + 1)
                        pool.tensor_tensor(shifted[:, :, :], logits[:, :, :],
                                           high[:, :].unsqueeze(2).to_broadcast([P, HEADS, KEYS]), ALU.subtract).then_inc(shifted_done, 1)

                    turns(pool, turn)

                @block.tensor
                def _(pe):
                    def turn(j, half, variant):
                        pe.wait_ge(xw_done, j + 1)
                        pe.wait_ge(qkv_copied, j * 4)
                        inner = xw[:, half, :].rearrange("p (b c) -> p b c", b=NB)[:, :, WIN // 2:WIN // 2 + COLS]
                        pe.matmul(qk_ps[:, 0:P], wq[:, :, :].rearrange("p h c -> p (h c)"), inner, start=True, stop=True)
                        pe.matmul(qk_ps[:, P:P + KEYS], wk[:, :, :].rearrange("p h c -> p (h c)"), xw[:, half, :], start=True, stop=True)
                        for m in range(2):
                            last = pe.matmul(v_ps[0:HALF, 128 * m:128 * m + HEADS * (DH + 1)], xw[:, half, HALF * m:HALF * m + HALF],
                                             wv[:, :, :].rearrange("p h c -> p (h c)"), start=True, stop=True)
                        last.then_inc(qkv_done, 1)
                        pe.wait_ge(qkv_copied, j * 4 + 4)
                        pe.wait_ge(logits_read, j)
                        for m in range(2):
                            last = pe.matmul(logits_ps[:, m, 0:2 * KEYS], q_t[:, half, :],
                                             k_diag[:, half, 2 * m:2 * m + 2, :].rearrange("p h k -> p (h k)"), start=True, stop=True)
                        last.then_inc(logits_done, 1)
                        pe.wait_ge(exp_done, j + 2)
                        for m in range(2):
                            pe.wait_ge(turned_copied, j * 2 + m)
                            for h in range(HEADS):
                                last = pe.transpose(turned_ps[:, m, P * h:P * h + P], probs[:, half, h, HALF * m:HALF * m + HALF], idn[:, :])
                            last.then_inc(turned_done, 1)
                        pe.wait_ge(att_done, j)
                        pe.wait_ge(end_copied, j * 2)
                        pe.wait_ge(turned_copied, j * 2 + 2)
                        for h in range(HEADS):
                            for m in range(2):
                                last = pe.matmul(att_ps[:, 32 * h:32 * h + DH + 1], probs_t[:, m, h, :],
                                                 v[:, half, m, (DH + 1) * h:(DH + 1) * h + DH + 1], start=(m == 0), stop=(m == 1))
                        last.then_inc(pv_done, 1)
                        pe.wait_ge(att_done, j + 1)
                        pe.transpose(att_ps[0:HID, 128:128 + P], att[:, :, :].rearrange("p h c -> p (h c)"), idn[:, :]).then_inc(end_done, 1)
                        pe.wait_ge(end_copied, j * 2 + 1)
                        pe.wait_ge(added, j)
                        pe.matmul(out_ps[0:HID, 0:P], wp[:, :], att_t[:, :], start=True, stop=True).then_inc(end_done, 1)
                        pe.wait_ge(end_copied, j * 2 + 2)
                        pe.matmul(out_ps[:, 128:128 + D], proj[:, :], w2[:, :], start=True, stop=True).then_inc(end_done, 1)

                    turns(pe, turn)

                @block.scalar
                def _(act):
                    act.sem_inc(exp_done, 1)

                    def turn(j, half, variant):
                        act.wait_ge(qkv_done, j + 1)
                        act.wait_ge(logits_done, j)
                        act.activation(q_t[:, half, :], qk_ps[:, 0:P], ACT.Copy).then_inc(qkv_copied, 1)
                        for h in range(HEADS):
                            rows_h = slice(PAD * h, PAD * h + PAD)
                            ins = act.activation(k_diag[rows_h, half, h, :], qk_ps[rows_h, P:P + KEYS], ACT.Copy)
                            if h % 2:
                                ins.then_inc(qkv_copied, 1)
                        act.activation(v[:, half, :, :], v_ps[0:HALF, 0:256].rearrange("p (m c) -> p m c", m=2)[:, :, 0:HEADS * (DH + 1)],
                                       ACT.Copy).then_inc(qkv_copied, 1)
                        act.wait_ge(shifted_done, j + 1)
                        act.activation(probs[:, half, :, :], shifted[:, :, :], ACT.Exp).then_inc(exp_done, 1)
                        act.wait_ge(pv_done, j)
                        for m in range(2):
                            act.wait_ge(turned_done, j * 2 + m + 1)
                            act.activation(probs_t[:, m, :, :].rearrange("p h q -> p (h q)"), turned_ps[:, m, :], ACT.Copy).then_inc(turned_copied, 1)
                        act.wait_ge(end_done, j * 3 + 1)
                        act.activation(att_t[0:HID, :], att_ps[0:HID, 128:128 + P], ACT.Copy).then_inc(end_copied, 1)
                        act.wait_ge(end_done, j * 3 + 2)
                        act.activation(proj[0:HID, :], out_ps[0:HID, 0:P], ACT.Copy).then_inc(end_copied, 1)

                    turns(act, turn)

                @block.vector
                def _(dve):
                    def turn(j, half, variant):
                        chain = Chain(dve, own, 1, j)
                        dve.wait_ge(logits_done, j + 1)
                        dve.wait_ge(shifted_done, j)
                        dve.scalar_tensor_tensor(logits[:, :, :].rearrange("p (m h) k -> p m (h k)", m=2), logits_ps[:, :, 0:2 * KEYS], SCALE,
                                                 table[:, variant, :, :].rearrange("p (m h) k -> p m (h k)", m=2),
                                                 ALU.mult, ALU.add).then_inc(logits_read, 1)
                        dve.wait_ge(logits_read, j + 1)
                        dve.tensor_reduce(high[:, :], logits[:, :, :], AX.X, ALU.max).then_inc(max_done, 1)
                        dve.wait_ge(pv_done, j + 1)
                        sums = att_ps[:, 0:P].rearrange("p (h c) -> p h c", h=HEADS)
                        chain(dve.reciprocal(recip[:, :], sums[:, :, DH]))
                        chain.wait()
                        dve.tensor_tensor(att[:, :, :], sums[:, :, 0:DH], recip[:, :].unsqueeze(2).to_broadcast([P, HEADS, DH]),
                                          ALU.mult).then_inc(att_done, 1)
                        dve.wait_ge(end_done, j * 3 + 3)
                        dst = H[:, bass.ds(j, 1), :].rearrange("p t d -> p (t d)")
                        dve.tensor_tensor(dst, out_ps[:, 128:128 + D], dst, ALU.add).then_inc(added, 1)

                    turns(dve, turn)

                @block.sync
                def _(sp):
                    sp.wait_ge(added, TILES)
                    for b in range(NB):
                        sp.dma_start(h2[SEQ * b:SEQ * b + SEQ, :].rearrange("(j w) d -> w j d", w=COLS),
                                     H[COLS * b:COLS * b + COLS, :, :]).then_inc(out_sem, 16)
                    sp.wait_ge(out_sem, 16 * NB)


def dense_stage(nc, H, idn, in_weight_t, in_bias, out_weight, mean, rstd, row_sems, turn_sems):
    hidden = in_bias.shape[0]
    with ExitStack() as stage:
        st = Store(nc, stage, "dense_ffn")
        xT = st.sb("xT", [C2, 2, TOKENS])
        bias = st.sb("bias", [P, hidden // P])
        row_statistics(nc, row_sems, 1, H, mean, rstd)
        turn_rows(nc, turn_sems, 1, H, mean, rstd, idn, xT)
        bias_in = st.sem("bias_in")
        with nc.Block() as block:

            @block.sync
            def _(sp):
                with nc.allow_non_contiguous_dma(reason="one bias per partition"):
                    sp.dma_start(bias[:, :], in_bias.rearrange("(m p) -> p m", p=P)).then_inc(bias_in, 16)
                sp.wait_ge(bias_in, 16)

        feed_forward(nc, "ffn", H, xT, 1, hidden, lambda e: in_weight_t,
                     lambda e: out_weight.rearrange("(m p) d -> p m d", p=P), ACT.Gelu, bias=bias)


def turned_weights(nc, weights, ident):
    steps, outs = [], []
    with ExitStack() as part:
        pt = Store(nc, part, "turn_weights")
        idn = pt.sb("idn", [P, P])
        for i, weight in enumerate(weights):
            rows, cols = weight.shape
            n = max(1, -(-cols // P))
            size = cols // n
            out = nc.dram_tensor(f"turned_weight{i}", (size, n, rows), F32).ap()
            tiles = [(r, min(P, rows - r)) for r in range(0, rows, P)]
            w = pt.sb(f"w{i}", [P, len(tiles), cols])
            wT = pt.sb(f"wT{i}", [size, n, rows])
            steps += [(w, wT, t, r, m, c, size) for t, (r, m) in enumerate(tiles) for c in range(n)]
            outs.append((weight, w, wT, out, tiles, len(steps)))
        ps = pt.ps("ps", [P, 2, SEQ])
        loaded, turned, copied, stored = pt.sem("loaded"), pt.sem("turned"), pt.sem("copied"), pt.sem("stored")
        loads = 1 + sum(len(tiles) for *_, tiles, _ in outs)
        with nc.Block() as block:

            @block.sync
            def _(sp):
                sp.dma_start(idn[:, :], ident).then_inc(loaded, 16)
                for weight, w, _, _, tiles, _ in outs:
                    for t, (r, m) in enumerate(tiles):
                        sp.dma_start(w[0:m, t, :], weight[r:r + m, :]).then_inc(loaded, 16)
                for _, _, wT, out, _, end in outs:
                    sp.wait_ge(copied, end)
                    sp.dma_start(out, wT[:, :, :]).then_inc(stored, 16)
                sp.wait_ge(stored, 16 * len(outs))

            @block.tensor
            def _(pe):
                pe.wait_ge(loaded, 16 * loads)
                for j, (w, _, t, _, m, c, size) in enumerate(steps):
                    if j >= 2:
                        pe.wait_ge(copied, j - 1)
                    pe.transpose(ps[0:size, j % 2, 0:m], w[0:m, t, size * c:size * c + size], idn[0:m, 0:m]).then_inc(turned, 1)

            @block.vector
            def _(dve):
                for j, (_, wT, _, r, m, c, size) in enumerate(steps):
                    dve.wait_ge(turned, j + 1)
                    dve.tensor_copy(wT[:, c, r:r + m], ps[0:size, j % 2, 0:m]).then_inc(copied, 1)
    return [out for _, _, _, out, _, _ in outs]


SETS = 64


def sets_stage(nc, H, idn, wqkv_t, wproj_t, wv_t, bv, const, mean, rstd, row_sems):
    HH = HD * HD
    SCALE = 0.25
    assert SCALE == HD ** -0.5
    BATCHES = NH // 2
    X, QT, OT, PT, OUT, TURN = 0, 1, (2, 3, 4, 7, 8, 9), (5, 6), 10, 11
    KSUM, VSUM = TT * TURN, TT * TURN + 1
    PER_SEQ = TT * TURN + 2
    DVE_BATCHES = 4
    with ExitStack() as stage:
        st = Store(nc, stage, "sets")
        wqkv = st.sb("wqkv", [C2, 2, 3 * D])
        wproj = st.sb("wproj", [C2, 2, D])
        wv = st.sb("wv", [P, 2, HD])
        bias = st.sb("bias", [P, HD])
        setm = st.sb("setm", [P, TT, P])
        tri = st.sb("tri", [P, P])
        mask = st.sb("mask", [P, TT, SETS])
        rows = st.sb("rows", [P, 2, D])
        xs = st.sb("xs", [C2, 2, 2, P])
        qk = st.sb("qk", [P, 2, TT, 2, NH, PAD])
        v0 = st.sb("v0", [P, 2, NH, HD])
        v = st.sb("v", [P, 2, TT, D])
        outer = st.sb("outer", [P, 2, NH, HH])
        outer_t = st.sb("outer_t", [P, 2, 2 * NH, P])
        k_diag = st.sb("k_diag", [P, 2, NG, GH * SETS])
        v_diag = st.sb("v_diag", [P, 2, NH // 2, 2, HD + 1])
        q_t = st.sb("q_t", [P, 2, NG, P])
        logits = st.sb("logits", [P, NH, SETS])
        shifted = st.sb("shifted", [P, NH, SETS])
        probs = st.sb("probs", [P, 2, NH, SETS])
        probs_t = st.sb("probs_t", [P, NH // 2, P])
        q_tail = st.sb("q_tail", [P, NH, HD])
        tail = st.sb("tail", [P, NH])
        high = st.sb("high", [P, NH])
        recip = st.sb("recip", [P, NH])
        out = st.sb("out", [P, NH, HD])
        out_n = st.sb("out_n", [P, NH, HD])
        out_t = st.sb("out_t", [C2, 2, P])
        row_statistics(nc, row_sems, 2, H, mean, rstd)
        logits_ps = st.ps("logits_ps", [P, 2, SEQ])
        tails_ps = st.ps("tails_ps", [P, SEQ])
        qk_ps = st.ps("qk_ps", [P, SEQ])
        v_ps = st.ps("v_ps", [P, 2, SEQ // 2])
        ring = st.ps("ring", [P, 2, SEQ])
        out_ps = st.ps("out_ps", [P, 2, SEQ // 2])
        loaded, zeroed = st.sem("loaded"), st.sem("zeroed")
        rows_done, ring_done, ring_copied = st.sem("rows_done"), st.sem("ring_done"), st.sem("ring_copied")
        qkv_done, qkv_copied = st.sem("qkv_done"), st.sem("qkv_copied")
        outer_done = {"dve": st.sem("outer_dve"), "pool": st.sem("outer_pool")}
        v_done, v_copied = st.sem("v_done"), st.sem("v_copied")
        tails_done, logits_done, logits_read = st.sem("tails_done"), st.sem("logits_done"), st.sem("logits_read")
        max_done, shifted_done, exp_done = st.sem("max_done"), st.sem("shifted_done"), st.sem("exp_done")
        pv_done, combined, proj_done, added = (
            st.sem("pv_done"), st.sem("combined"), st.sem("proj_done"), st.sem("added"))
        own = st.sem("own")

        with nc.Block() as block:

            @block.sync
            def _(sp):
                sp.dma_start(wqkv[:, :, :], wqkv_t).then_inc(loaded, 16)
                sp.dma_start(wproj[:, :, :], wproj_t).then_inc(loaded, 16)
                sp.dma_start(wv[:, :, :], wv_t).then_inc(loaded, 16)
                sp.dma_start(bias[:, :], bv.rearrange("(a e) -> a e", a=1).to_broadcast([P, HD])).then_inc(loaded, 16)
                sp.dma_start(setm[:, :, :], const["sets"].rearrange("(q p) s -> p q s", p=P)).then_inc(loaded, 16)
                sp.dma_start(tri[:, :], const["tail_sums"]).then_inc(loaded, 16)
                sp.dma_start(mask[:, :, :], const["sets_mask"].rearrange("(q p) s -> p q s", p=P)).then_inc(loaded, 16)
                sp.wait_ge(loaded, 16 * 7)

            @block.gpsimd
            def _(pool):
                pool.memset(qk[:, :, :, :, :, :].rearrange("p a q m h c -> p (a q m h c)"), 0.0).then_inc(zeroed, 1)
                pool.memset(k_diag[:, :, :, :].rearrange("p a g s -> p (a g s)"), 0.0).then_inc(zeroed, 1)
                pool.memset(v_diag[:, :, :, :, :].rearrange("p a h m c -> p (a h m c)"), 0.0).then_inc(zeroed, 1)
                pool.wait_ge(zeroed, 3)
                pool.memset(v_diag[0:SETS, :, :, 0, HD:], 1.0).then_inc(zeroed, 1)
                pool.memset(v_diag[SETS:P, :, :, 1, HD:], 1.0).then_inc(zeroed, 1)
                pool.wait_ge(zeroed, 5)

        def at(s, q, use):
            return s * PER_SEQ + (q * TURN + use)

        def bank(q, use):
            return ring[:, (q * TURN + use) % 2, :]

        def counted(use, has1, has2):
            if has1 and has2:
                return 1
            uses = (X, *OT) if has1 else (QT, *PT, OUT)
            return [u for u in (*uses, uses[0] + TURN) if u > use][0] - use

        with nc.Block() as block:

            def steps(eng, turn, sums):
                for q in range(TT):
                    turn(0, 0, q, True, False)
                sums(0, 0)
                with eng.Fori(0, (NB - 2) // 2) as it:
                    for par in (1, 0):
                        s = it * 2 + (1 if par else 2)
                        for q in range(TT):
                            turn(s, par, q, True, True)
                        sums(s, par)
                for q in range(TT):
                    turn(NB - 1, 1, q, True, True)
                sums(NB - 1, 1)
                for q in range(TT):
                    turn(NB, 0, q, False, True)

            @block.tensor
            def _(pe):
                def claim(s, q, use):
                    if not (isinstance(s, int) and s == 0 and q * TURN + use < 2):
                        pe.wait_ge(ring_copied, at(s, q, use) - 1)

                def batch(s, q, T1, k, has2):
                    claim(s, q, OT[k])
                    pe.wait_ge(outer_done["dve" if k < DVE_BATCHES else "pool"], T1 + 1)
                    for m in range(4):
                        last = pe.transpose(bank(q, OT[k])[:, P * m:P * m + P],
                                            outer[:, q % 2, 2 * k + m // 2, P * (m % 2):P * (m % 2) + P], idn[:, :])
                    last.then_inc(ring_done, counted(OT[k], True, has2))

                def value(s, q, T1, k):
                    pe.wait_ge(ring_copied, at(s, q, OT[k]) + 1)
                    for h in (2 * k, 2 * k + 1):
                        for m in range(2):
                            last = pe.matmul(v_ps[:, 1, HD * h:HD * h + HD], outer_t[:, q % 2, 2 * h + m, :], wv[:, m, :],
                                             start=(m == 0), stop=(m == 1))
                    if k == BATCHES - 1:
                        last.then_inc(v_done, 1)

                def turn(s, par, q, has1, has2):
                    T1 = s * TT + q
                    T2 = T1 - TT
                    if has1:
                        pe.wait_ge(rows_done, T1 + 1)
                        claim(s, q, X)
                        for c in range(2):
                            last = pe.transpose(bank(q, X)[0:C2, P * c:P * c + P], rows[:, q % 2, C2 * c:C2 * c + C2], idn[:, :])
                        last.then_inc(ring_done, counted(X, has1, has2))
                    if has2:
                        claim(s, q, QT)
                        for g in range(NG):
                            last = pe.transpose(bank(q, QT)[:, P * g:P * g + P],
                                                qk[:, 1 - par, q, 0, GH * g:GH * g + GH, :].rearrange("p h c -> p (h c)"), idn[:, :])
                        last.then_inc(ring_done, counted(QT, has1, has2))
                        pe.wait_ge(combined, T2)
                        pe.matmul(tails_ps[:, 0:D], tri[:, :], qk[:, 1 - par, q, 1, :, 0:HD], start=True, stop=True)
                        pe.matmul(tails_ps[:, D:2 * D], tri[:, :], v[:, 1 - par, q, :], start=True, stop=True).then_inc(tails_done, 1)
                    if has1:
                        pe.wait_ge(ring_copied, at(s, q, X) + 1)
                        pe.wait_ge(qkv_copied, T1 * 2)
                        pe.wait_ge(v_copied, T1)
                        for c in range(2):
                            pe.matmul(qk_ps[:, 0:2 * D], xs[:, q % 2, c, :], wqkv[:, c, 0:2 * D], start=(c == 0), stop=(c == 1))
                        for c in range(2):
                            last = pe.matmul(v_ps[:, 0, 0:D], xs[:, q % 2, c, :], wqkv[:, c, 2 * D:], start=(c == 0), stop=(c == 1))
                        last.then_inc(qkv_done, 1)
                    if has2:
                        pe.wait_ge(ring_copied, at(s, q, QT) + 1)
                        pe.wait_ge(logits_read, T2)
                        for g in range(NG):
                            last = pe.matmul(logits_ps[:, g // 2, 256 * (g % 2):256 * (g % 2) + 256], q_t[:, q % 2, g, :],
                                             k_diag[:, 1 - par, g, :], start=True, stop=True)
                        last.then_inc(logits_done, 1)
                    if has1:
                        batch(s, q, T1, 0, has2)
                        batch(s, q, T1, 1, has2)
                        value(s, q, T1, 0)
                        batch(s, q, T1, 2, has2)
                        value(s, q, T1, 1)
                    if has2:
                        pe.wait_ge(exp_done, T2 + 1)
                        for k in range(2):
                            claim(s, q, PT[k])
                            for m in range(3):
                                h = 2 * (3 * k + m)
                                last = pe.transpose(bank(q, PT[k])[:, P * m:P * m + P],
                                                    probs[:, q % 2, h:h + 2, :].rearrange("p h s -> p (h s)"), idn[:, :])
                            last.then_inc(ring_done, counted(PT[k], has1, has2))
                    if has1:
                        value(s, q, T1, 2)
                        batch(s, q, T1, 3, has2)
                    if has2:
                        pe.wait_ge(ring_copied, at(s, q, PT[1]) + 1)
                        pe.wait_ge(added, T2)
                        for m in range(NH // 2):
                            last = pe.matmul(out_ps[:, 0, 34 * m:34 * m + 34], probs_t[:, m, :],
                                             v_diag[:, 1 - par, m, :, :].rearrange("p h c -> p (h c)"), start=True, stop=True)
                        last.then_inc(pv_done, 1)
                    if has1:
                        batch(s, q, T1, 4, has2)
                        value(s, q, T1, 3)
                        batch(s, q, T1, 5, has2)
                        value(s, q, T1, 4)
                        value(s, q, T1, 5)
                    if has2:
                        pe.wait_ge(combined, T2 + 1)
                        claim(s, q, OUT)
                        for c in range(2):
                            last = pe.transpose(bank(q, OUT)[0:C2, P * c:P * c + P],
                                                out_n[:, :, :].rearrange("p h c -> p (h c)")[:, C2 * c:C2 * c + C2], idn[:, :])
                        last.then_inc(ring_done, counted(OUT, has1, has2))
                        pe.wait_ge(ring_copied, at(s, q, OUT) + 1)
                        for c in range(2):
                            last = pe.matmul(out_ps[:, 1, 0:D], out_t[:, c, :], wproj[:, c, :], start=(c == 0), stop=(c == 1))
                        last.then_inc(proj_done, 1)

                def sums(s, par):
                    pe.wait_ge(v_copied, s * TT + TT)
                    claim(s, 0, KSUM)
                    for g in range(NG):
                        for q in range(TT):
                            last = pe.matmul(bank(0, KSUM)[:, SETS * g:SETS * g + SETS],
                                             qk[:, par, q, 1, GH * g:GH * g + GH, :].rearrange("p h c -> p (h c)"),
                                             setm[:, q, 0:SETS], start=(q == 0), stop=(q == TT - 1))
                    last.then_inc(ring_done, 1)
                    claim(s, 0, VSUM)
                    for q in range(TT):
                        last = pe.matmul(bank(0, VSUM)[:, 0:D], setm[:, q, :], v[:, par, q, :], start=(q == 0), stop=(q == TT - 1))
                    last.then_inc(ring_done, 2 if isinstance(s, int) and s == NB - 1 else 1)

                steps(pe, turn, sums)

            @block.scalar
            def _(act):
                def copy(s, q, use, dst, src, has1, has2):
                    act.wait_ge(ring_done, at(s, q, use) + 1)
                    act.activation(dst, src, ACT.Copy).then_inc(ring_copied, counted(use, has1, has2))

                def turn(s, par, q, has1, has2):
                    T1 = s * TT + q
                    T2 = T1 - TT
                    early = isinstance(s, int) and s == 0 and q < 2

                    def batches(ks):
                        for k in ks:
                            if k == 0 and not early:
                                act.wait_ge(v_done, T1 - 1)
                            copy(s, q, OT[k], outer_t[:, q % 2, 4 * k:4 * k + 4, :].rearrange("p m t -> p (m t)"), bank(q, OT[k]), has1, has2)

                    if has1:
                        if not early:
                            act.wait_ge(qkv_done, T1 - 1)
                        copy(s, q, X, xs[:, q % 2, :, :].rearrange("p c t -> p (c t)"), bank(q, X)[0:C2, 0:2 * P], has1, has2)
                    if has2:
                        act.wait_ge(logits_done, T2)
                        copy(s, q, QT, q_t[:, q % 2, :, :].rearrange("p g t -> p (g t)"), bank(q, QT)[:, 0:NG * P], has1, has2)
                    if has1:
                        act.wait_ge(qkv_done, T1 + 1)
                        act.activation(qk[:, par, q, :, :, 0:HD].rearrange("p m h c -> p (m h) c"),
                                       qk_ps[:, 0:2 * D].rearrange("p (m c) -> p m c", c=HD), ACT.Copy).then_inc(qkv_copied, 1)
                        act.activation(v0[:, q % 2, :, :].rearrange("p h c -> p (h c)"), v_ps[:, 0, 0:D], ACT.Copy).then_inc(qkv_copied, 1)
                        batches((0, 1))
                    if has2:
                        act.wait_ge(shifted_done, T2 + 1)
                        act.activation(probs[:, q % 2, :, :], shifted[:, :, :], ACT.Exp).then_inc(exp_done, 1)
                    if has1:
                        batches((2,))
                    if has2:
                        act.wait_ge(pv_done, T2)
                        for k in range(2):
                            copy(s, q, PT[k], probs_t[:, 3 * k:3 * k + 3, :].rearrange("p m t -> p (m t)"), bank(q, PT[k])[:, 0:3 * P], has1, has2)
                    if has1:
                        batches((3, 4, 5))
                    if has2:
                        act.wait_ge(proj_done, T2)
                        copy(s, q, OUT, out_t[:, :, :].rearrange("p c t -> p (c t)"), bank(q, OUT)[0:C2, 0:2 * P], has1, has2)

                def sums(s, par):
                    act.wait_ge(ring_done, at(s, 0, KSUM) + 1)
                    for j in range(GH):
                        rows_j = slice(PAD * j, PAD * j + PAD)
                        ins = act.activation(k_diag[rows_j, par, :, SETS * j:SETS * j + SETS],
                                             bank(0, KSUM)[rows_j, 0:NG * SETS].rearrange("p (g s) -> p g s", g=NG), ACT.Copy)
                    ins.then_inc(ring_copied, 1)
                    act.wait_ge(ring_done, at(s, 0, VSUM) + 1)
                    for m in range(2):
                        rows_m = slice(SETS * m, SETS * m + SETS)
                        ins = act.activation(v_diag[rows_m, par, :, m, 0:HD],
                                             bank(0, VSUM)[rows_m, 0:D].rearrange("p (h m c) -> p h m c", m=2, c=HD)[:, :, m, :], ACT.Copy)
                    ins.then_inc(ring_copied, 2 if isinstance(s, int) and s == NB - 1 else 1)

                steps(act, turn, sums)

            def products(eng, which, s, par, q, heads):
                n = heads.stop - heads.start
                eng.wait_ge(qkv_copied, (s * TT + q) * 2 + 2)
                k = qk[:, par, q, 1, heads, 0:HD].unsqueeze(3).to_broadcast([P, n, HD, HD])
                w = v0[:, q % 2, heads, :].unsqueeze(2).to_broadcast([P, n, HD, HD])
                eng.tensor_tensor(outer[:, q % 2, heads, :].rearrange("p h (i j) -> p h i j", i=HD), k, w,
                                  ALU.mult).then_inc(outer_done[which], 1)

            @block.gpsimd
            def _(pool):
                def turn(s, par, q, has1, has2):
                    T2 = s * TT + (q - TT)
                    if has2:
                        pool.wait_ge(max_done, T2 + 1)
                        pool.wait_ge(exp_done, T2)
                        pool.tensor_tensor(shifted[:, :, :], logits[:, :, :],
                                           high[:, :].unsqueeze(2).to_broadcast([P, NH, SETS]), ALU.subtract).then_inc(shifted_done, 1)
                    if has1:
                        products(pool, "pool", s, par, q, slice(2 * DVE_BATCHES, NH))

                steps(pool, turn, lambda s, par: None)

            @block.vector
            def _(dve):
                def rows_of(s, q):
                    T = s * TT + q
                    if not (isinstance(s, int) and s == 0 and q < 2):
                        dve.wait_ge(ring_done, at(s, q - 2, X) + 1 if q >= 2 else at(s - 1, q + 2, X) + 1)
                    t = bass.ds(T, 1)
                    dve.tensor_scalar(rows[:, q % 2, :], H[:, t, :].rearrange("p t d -> p (t d)"),
                                      mean[:, t], rstd[:, t], ALU.subtract, ALU.mult).then_inc(rows_done, 1)

                def turn(s, par, q, has1, has2):
                    T1 = s * TT + q
                    T2 = T1 - TT
                    chain = Chain(dve, own, 6, T2) if has2 else None
                    if has2:
                        q_rows = qk[:, 1 - par, q, 0, :, 0:HD]
                        dve.wait_ge(tails_done, T2 + 1)
                        chain(dve.tensor_tensor(q_tail[:, :, :], q_rows, tails_ps[:, 0:D].rearrange("p (h c) -> p h c", h=NH), ALU.mult))
                        chain.wait()
                        chain(dve.tensor_reduce(tail[:, :], q_tail[:, :, :], AX.X, ALU.add))
                        dve.wait_ge(logits_done, T2 + 1)
                        dve.wait_ge(shifted_done, T2)
                        dve.scalar_tensor_tensor(logits[:, :, :],
                                                 logits_ps[:, :, :].rearrange("p b s -> p (b s)")[:, 0:NH * SETS].rearrange("p (h s) -> p h s", h=NH),
                                                 SCALE, mask[:, q, :].unsqueeze(1).to_broadcast([P, NH, SETS]),
                                                 ALU.mult, ALU.add).then_inc(logits_read, 1)
                        dve.wait_ge(logits_read, T2 + 1)
                        chain.wait()
                        chain(dve.tensor_scalar(logits[:, :, SETS - 1], tail[:, :], SCALE, None, ALU.mult))
                        chain.wait()
                        dve.tensor_reduce(high[:, :], logits[:, :, :], AX.X, ALU.max).then_inc(max_done, 1)
                    if has1:
                        products(dve, "dve", s, par, q, slice(0, 2 * DVE_BATCHES))
                        if q < TT - 1:
                            rows_of(s, q + 1)
                        elif not (isinstance(s, int) and s == NB - 1):
                            rows_of(s + 1, 0)
                    if has2:
                        dve.wait_ge(pv_done, T2 + 1)
                        pv = out_ps[:, 0, 0:NH * (HD + 1)].rearrange("p (h c) -> p h c", h=NH)
                        chain(dve.reciprocal(recip[:, :], pv[:, :, HD]))
                        chain(dve.tensor_tensor(out[:, :, :], tails_ps[:, D:2 * D].rearrange("p (h c) -> p h c", h=NH),
                                                probs[:, q % 2, :, SETS - 1:].to_broadcast([P, NH, HD]), ALU.mult))
                        chain.wait()
                        chain(dve.tensor_tensor(out[:, :, :], out[:, :, :], pv[:, :, 0:HD], ALU.add))
                        chain.wait()
                        dve.tensor_tensor(out_n[:, :, :], out[:, :, :], recip[:, :].unsqueeze(2).to_broadcast([P, NH, HD]),
                                          ALU.mult).then_inc(combined, 1)
                        chain.end()
                    if has1:
                        dve.wait_ge(v_done, T1 + 1)
                        dve.tensor_tensor(v[:, par, q, :].rearrange("p (h c) -> p h c", h=NH),
                                          v_ps[:, 1, 0:D].rearrange("p (h c) -> p h c", h=NH),
                                          bias[:, :].unsqueeze(1).to_broadcast([P, NH, HD]), ALU.add).then_inc(v_copied, 1)
                    if has2:
                        dve.wait_ge(proj_done, T2 + 1)
                        dst = H[:, bass.ds(T2, 1), :].rearrange("p t d -> p (t d)")
                        dve.tensor_tensor(dst, out_ps[:, 1, 0:D], dst, ALU.add).then_inc(added, 1)

                rows_of(0, 0)
                steps(dve, turn, lambda s, par: None)



def experts_stage(nc, H, idn, gamma, beta, router_w, w1, w2, mean, rstd, row_sems, turn_sems):
    E, hidden = w1.shape[0], w1.shape[2]
    with ExitStack() as stage:
        st = Store(nc, stage, "experts")
        xT = st.sb("xT", [C2, 2, TOKENS])
        gates = st.sb("gates", [P, TILES * E])
        gamma_beta = st.sb("gamma_beta", [C2, 2, 2])
        router = st.sb("router", [C2, 2, E])
        row_statistics(nc, row_sems, 3, H, mean, rstd)
        with ExitStack() as part:
            X = Store(nc, part, "moe").sb("X", [P, TILES, D])
            normalise_rows(nc, "moe_norm", H, mean, rstd, X)
            row_statistics(nc, row_sems, 4, X, mean, rstd)
            small_in = st.sem("small_in")
            with nc.Block() as block:

                @block.sync
                def _(sp):
                    with nc.allow_non_contiguous_dma(reason="one value per partition"):
                        sp.dma_start(gamma_beta[:, :, 0], gamma.rearrange("(c p) -> p c", c=2)).then_inc(small_in, 16)
                        sp.dma_start(gamma_beta[:, :, 1], beta.rearrange("(c p) -> p c", c=2)).then_inc(small_in, 16)
                    sp.dma_start(router[:, :, :], router_w.rearrange("(c p) e -> p c e", c=2)).then_inc(small_in, 16)
                    sp.wait_ge(small_in, 48)

            turn_rows(nc, turn_sems, 2, X, mean, rstd, idn, xT, gamma_beta=gamma_beta)
        route(nc, xT, router, idn, gates, E)
        feed_forward(nc, "moe_ffn", H, xT, E, hidden,
                     lambda e: w1[bass.ds(e, 1), :, :].rearrange("e (c p) f -> p (e c) f", c=2),
                     lambda e: w2[bass.ds(e, 1), :, :].rearrange("e (m p) d -> p (e m) d", p=P), ACT.Silu, gates=gates)


def route(nc, xT, router, idn, gates, E):
    with ExitStack() as part:
        pt = Store(nc, part, "route")
        logits_t = pt.sb("logits_t", [E, 2, SEQ])
        full = [P, TILES, E]
        probs = pt.sb("probs", full)
        left = pt.sb("left", full)
        equal = pt.sb("equal", full)
        first_mask = pt.sb("first_mask", full)
        number = pt.sb("number", full)
        number_i = pt.sb("number_i", full, I32)
        high = pt.sb("high", [P, TILES])
        top1 = pt.sb("top1", [P, TILES])
        index = pt.sb("index", [P, TILES])
        product = pt.ps("product", [E, 2, SEQ])
        turned = pt.ps("turned", [P, 2, SEQ])
        product_done, copied, turned_done, placed, numbered = (
            pt.sem("product_done"), pt.sem("copied"), pt.sem("turned_done"), pt.sem("placed"), pt.sem("numbered"))
        turn_begun = pt.sem("turn_begun")
        own, exp_ready, exp_done = pt.sem("own"), pt.sem("exp_ready"), pt.sem("exp_done")
        g3 = gates[:, :].rearrange("p (t e) -> p t e", e=E)

        def wide(x):
            return x[:, :].unsqueeze(2).to_broadcast(full)

        with nc.Block() as block:

            @block.gpsimd
            def _(pool):
                pool.iota(number_i[:, :, :], pattern=[[0, TILES], [1, E]], base=0, channel_multiplier=0).then_inc(numbered, 1)

            @block.tensor
            def _(pe):
                pe.sem_inc(turned_done, 1)
                with pe.Fori(0, GROUPS // 2) as it:
                    for half in range(2):
                        g = it * 2 + half
                        pe.wait_ge(copied, g)
                        for k in range(2):
                            last = pe.matmul(product[:, half, :], router[:, k, :], xT[:, k, bass.ds(g * SEQ, SEQ)],
                                             start=(k == 0), stop=(k == 1))
                        last.then_inc(product_done, 1)
                        pe.wait_ge(copied, g + 2)
                        pe.wait_ge(placed, g)
                        pe.sem_inc(turn_begun, 1)
                        for k in range(TT):
                            last = pe.transpose(turned[:, half, E * k:E * k + E], logits_t[:, half, P * k:P * k + P], idn[0:E, 0:E])
                        last.then_inc(turned_done, 1)

            @block.scalar
            def _(act):
                act.sem_inc(copied, 1)
                with act.Fori(0, GROUPS // 2) as it:
                    for half in range(2):
                        g = it * 2 + half
                        act.wait_ge(product_done, g + 1)
                        act.wait_ge(turned_done, g)
                        act.activation(logits_t[:, half, :], product[:, half, :], ACT.Copy).then_inc(copied, 1)
                act.wait_ge(exp_ready, 1)
                act.activation(equal[:, :, :], left[:, :, :], ACT.Exp).then_inc(exp_done, 1)

            @block.vector
            def _(dve):
                dve.sem_inc(placed, 1)
                with dve.Fori(0, GROUPS // 2) as it:
                    for half in range(2):
                        g = it * 2 + half
                        dve.wait_ge(turned_done, g + 2)
                        dve.tensor_copy(probs[:, bass.ds(g * TT, TT), :].rearrange("p t e -> p (t e)"),
                                        turned[:, half, 0:TT * E]).then_inc(placed, 1)
                dve.wait_ge(placed, GROUPS + 1)
                chain = Chain(dve, own)
                chain(dve.tensor_reduce(high[:, :], probs[:, :, :], AX.X, ALU.max))
                chain.wait()
                dve.tensor_tensor(left[:, :, :], probs[:, :, :], wide(high), ALU.subtract).then_inc(exp_ready, 1)
                dve.wait_ge(exp_done, 1)
                chain(dve.tensor_reduce(high[:, :], equal[:, :, :], AX.X, ALU.add))
                chain.wait()
                chain(dve.reciprocal(index[:, :], high[:, :]))
                chain.wait()
                chain(dve.tensor_tensor(probs[:, :, :], equal[:, :, :], wide(index), ALU.mult))
                dve.wait_ge(numbered, 1)
                chain(dve.tensor_copy(number[:, :, :], number_i[:, :, :]))
                chain.wait()

                def first_largest(values, top, mask):
                    chain(dve.tensor_reduce(top[:, :], values[:, :, :], AX.X, ALU.max))
                    chain.wait()
                    chain(dve.tensor_tensor(equal[:, :, :], values[:, :, :], wide(top), ALU.not_equal))
                    chain.wait()
                    chain(dve.scalar_tensor_tensor(equal[:, :, :], equal[:, :, :], float(E), number[:, :, :], ALU.mult, ALU.add))
                    chain.wait()
                    chain(dve.tensor_reduce(index[:, :], equal[:, :, :], AX.X, ALU.min))
                    chain.wait()
                    chain(dve.tensor_tensor(mask, number[:, :, :], wide(index), ALU.is_equal))
                    chain.wait()

                first_largest(probs, top1, first_mask[:, :, :])
                chain(dve.scalar_tensor_tensor(left[:, :, :], first_mask[:, :, :], -2.0, probs[:, :, :], ALU.mult, ALU.add))
                chain.wait()
                first_largest(left, high, g3)
                chain(dve.tensor_tensor(top1[:, :], top1[:, :], high[:, :], ALU.add))
                chain(dve.tensor_tensor(g3, g3, first_mask[:, :, :], ALU.add))
                chain.wait()
                chain(dve.reciprocal(top1[:, :], top1[:, :]))
                chain(dve.tensor_tensor(g3, g3, probs[:, :, :], ALU.mult))
                chain.wait()
                chain(dve.tensor_tensor(g3, g3, wide(top1), ALU.mult))


def constants():
    p, i = np.meshgrid(np.arange(SEQ), np.arange(D // 2))
    pos = np.zeros((SEQ, D), dtype=np.float32)
    pos[:, ::2] = np.sin(p / 2500 ** (2 * i / D)).T
    pos[:, 1::2] = np.cos(p / 2500 ** (2 * i / D)).T
    wv = np.zeros((P, NH, PAD), np.float32)
    wv[HD, :, HD:] = 1.0
    affine = np.zeros((P, NG, 4), np.float32)
    affine[HD, :, 1] = affine[HD, :, 3] = 1.0
    t = np.arange(SEQ)
    spans = [(i, i + size - 1) for size in (16 << n for n in range(6)) for i in range(0, SEQ, size)]
    sets = np.zeros((SEQ, 2, SETS), np.float32)
    sets_mask = np.zeros((SEQ, SETS), np.float32)
    for n, (first, last) in enumerate(spans):
        sets[first:last + 1, :, n] = 1.0
        sets_mask[:, n] = np.where(t >= last, 0.0, NEG)
    near_mask = np.full((NB, COLS, 3, NB, SPAN), NEG, np.float32)
    for v, column0 in enumerate((0, COLS, SEQ - COLS)):
        for b in range(NB):
            for w in range(COLS):
                top = min(max(b - WIN // 2, 0), NB - WIN)
                left = min(max(column0 + w - WIN // 2, 0), SEQ - WIN) - (column0 - WIN // 2)
                near_mask[b, w, v, top:top + WIN, left:left + WIN] = 0.0
    r = np.arange(P)
    tail_sums = ((r[:, None] // 16 == r[None, :] // 16) & (r[:, None] <= r[None, :])).astype(np.float32)
    return {
        "near_mask": near_mask.reshape(P, 3 * KEYS),
        "sets": sets.reshape(SEQ, 2 * SETS),
        "sets_mask": sets_mask,
        "tail_sums": tail_sums,
        "pos": pos,
        "pad_rows": np.concatenate([wv.reshape(P, -1), affine.reshape(P, -1)], axis=1),
        "ident": np.eye(P, dtype=np.float32),
    }


_CONSTANTS = constants()
_INS = [
    "x", "L0_tok_emb", "L0_tok_Wq", "L0_tok_bq", "L0_tok_Wk", "L0_tok_bk", "L0_tok_Wv", "L0_tok_bv", "L0_tok_Wf",
    "L0_tok_bf", "L0_tok_g1", "L0_tok_b1", "L0_tok_g2", "L0_tok_b2", "L0_attn_fc1_w", "L0_attn_fc1_b",
    "L0_attn_convA_w", "L0_attn_convA_b", "L0_attn_convB_w", "L0_attn_convB_b", "L0_attn_qkv_w", "L0_attn_qkv_b",
    "L0_attn_rpb", "L0_attn_proj_w", "L0_attn_proj_b", "L0_attn_fc2_w", "L0_attn_fc2_b", "L0_ffn_in_weight",
    "L0_ffn_in_bias", "L0_ffn_out_weight", "L1_attn_Wqkv", "L1_attn_Wproj", "L1_attn_Wv", "L1_attn_bv",
    "L1_ffn_ln_gamma", "L1_ffn_ln_beta", "L1_ffn_router_w", "L1_ffn_w1", "L1_ffn_w2",
]


def tower(nc, ins, const, out):

    def dram(name, shape, dt=F32):
        return nc.dram_tensor(name, shape, dt).ap()

    def group(prefix, names):
        return [ins[prefix + n] for n in names.split()]

    rows_out = out.rearrange("b s d -> (b s) d")
    h1, h2 = dram("h1", (TOKENS, D)), dram("h2", (TOKENS, D))
    scratch = dram("q_parts", (3 * NB * D, SEQ), BF16), dram("k_parts", (3 * NB * D, SEQ), BF16), dram("v_rows", (NB * NG * SEQ, P))
    shifts = dram("shifts", (COLS, HEADS, UROWS, SPAN))
    to_turn = group("L0_attn_", "fc1_w convA_w convB_w qkv_w proj_w fc2_w") + group("L0_ffn_", "in_weight") + group("L1_attn_", "Wqkv Wproj Wv")
    turned = turned_weights(nc, to_turn, const["ident"])
    row_sems, turn_sems = row_semaphores(nc)
    token_stage(nc, ins["x"], ins["L0_tok_emb"], group("L0_tok_", "Wq bq Wk bk Wv bv Wf bf g1 b1 g2 b2"),
                const["pos"], const["pad_rows"], const["ident"], h1, scratch)
    neighborhood_stage(nc, h1, h2, group("L0_attn_", "fc1_b convA_b convB_b qkv_b rpb proj_b fc2_b"), turned[0:6], shifts,
                       const, row_sems, turn_sems)
    with ExitStack() as ctx:
        st = Store(nc, ctx, "main")
        H = st.sb("H", [P, TILES, D])
        idn = st.sb("idn", [P, P])
        mean = st.sb("mean", [P, TILES])
        rstd = st.sb("rstd", [P, TILES])
        h_in, h_out = st.sem("h_in"), st.sem("h_out")
        with nc.Block() as block:

            @block.sync
            def _(sp):
                sp.dma_start(H[:, :, :], h2.rearrange("(t p) d -> p t d", p=P)).then_inc(h_in, 16)
                sp.dma_start(idn[:, :], const["ident"]).then_inc(h_in, 16)
                sp.wait_ge(h_in, 32)

        dense_stage(nc, H, idn, turned[6], ins["L0_ffn_in_bias"], ins["L0_ffn_out_weight"], mean, rstd, row_sems, turn_sems)
        sets_stage(nc, H, idn, turned[7], turned[8], turned[9], ins["L1_attn_bv"], const, mean, rstd, row_sems)
        experts_stage(nc, H, idn, *group("L1_ffn_", "ln_gamma ln_beta router_w w1 w2"), mean, rstd, row_sems, turn_sems)
        with nc.Block() as block:

            @block.sync
            def _(sp):
                sp.dma_start(rows_out.rearrange("(t p) d -> p t d", p=P), H[:, :, :]).then_inc(h_out, 16)
                sp.wait_ge(h_out, 16)


def kernel(**inputs):
    import numpy as _np
    import concourse.bacc as _bacc
    from concourse import mybir as _mybir
    from concourse.bass_utils import run_bass_kernel_spmd as _run

    nc = _bacc.Bacc("TRN2", target_bir_lowering=False, num_devices=1)
    arrays, ins, const = {}, {}, {}
    for group, names, values in ((ins, _INS, inputs), (const, list(_CONSTANTS), _CONSTANTS)):
        for name in names:
            a = _np.ascontiguousarray(values[name])
            arrays[f"in_{name}_dram"] = a
            group[name] = nc.dram_tensor(f"in_{name}_dram", a.shape, _mybir.dt.from_np(a.dtype), kind="ExternalInput").ap()
    out = nc.dram_tensor("out_0_dram", (NB, SEQ, D), F32, kind="ExternalOutput").ap()
    tower(nc, ins, const, out)
    r = _run(nc, [arrays], core_ids=[0])
    return r.results[0]["out_0_dram"]
```

```python
from contextlib import ExitStack

import concourse.bass as bass
import numpy as np
from concourse import mybir

F32 = mybir.dt.float32
BF16 = mybir.dt.bfloat16
I32 = mybir.dt.int32
U32 = mybir.dt.uint32
ALU = mybir.AluOpType
ACT = mybir.ActivationFunctionType
AX = mybir.AxisListType

P = 128
NB, SEQ, D = 16, 512, 192
TOKENS = NB * SEQ
VOCAB = 8000
NH, HD = 12, 16
PAD = 32
NG, GH = 3, 4
TT = SEQ // P
TILES = TOKENS // P
EPS = 1e-5
LAYERS = 2
NEG = -1.0e30


class Chain:

    def __init__(self, eng, sem, per=0, turn=0):
        self.eng, self.sem, self.base, self.per, self.n = eng, sem, turn * per, per, 0

    def __call__(self, ins):
        ins.then_inc(self.sem, 1)
        self.n += 1

    def wait(self):
        self.eng.wait_ge(self.sem, self.base + self.n)

    def end(self):
        assert self.n == self.per, (self.n, self.per)


class Store:

    def __init__(self, nc, ctx, stage):
        self.nc, self.ctx, self.stage = nc, ctx, stage

    def sb(self, name, shape, dt=F32):
        return self.ctx.enter_context(self.nc.sbuf_tensor(f"{self.stage}_{name}", shape, dt))

    def ps(self, name, shape, dt=F32):
        return self.ctx.enter_context(self.nc.psum_tensor(f"{self.stage}_{name}", shape, dt))

    def sem(self, name):
        return self.nc.alloc_semaphore(name=f"{self.stage}_{name}")




def token_stage(nc, x, emb, weights, pos, pad_rows, ident, h1, scratch):
    Wq, bq, Wk, bk, Wv, bv, Wf, bf, g1, b1, g2, b2 = weights
    q_parts, k_parts, v_rows = scratch
    SCALE = float(np.float32(1.0) / np.sqrt(np.float32(D)))
    UNITS = NB * NG
    SLOTS = 4

    with ExitStack() as stage:
        st = Store(nc, stage, "tok")
        hT = st.sb("hT", [P, NB, NG, SEQ])
        hT_u = hT[:, :, :, :].rearrange("p b g t -> p (b g) t")
        wq = st.sb("wq", [P, D])
        wk = st.sb("wk", [P, D])
        wv = st.sb("wv", [P, NH * PAD])
        wf = st.sb("wf", [P, NG, NH * PAD])
        affine = st.sb("affine", [P, NG, 4])
        norm = st.sb("norm", [P, 2, 2, NG])
        mean_var = st.sb("mean_var", [P, NG, 2])
        power = st.sb("power", [P, 2, NG])
        stats = st.sb("stats", [P, NG, NB, 6])
        idn = st.sb("idn", [P, P])
        idn_b = st.sb("idn_b", [P, P], BF16)

        with ExitStack() as part:
            pt = Store(nc, part, "emb")
            ids = pt.sb("ids", [P, TILES], I32)
            wrap = pt.sb("wrap", [P, TILES], I32)
            wrapped = pt.sb("wrapped", [P, TILES], I32)
            rows = pt.sb("rows", [P, TILES, D])
            posn = pt.sb("posn", [P, TT, D])
            tmp = pt.sb("tmp", [P, TT, D])
            padded = pt.sb("padded", [P, 2, TT, NH, PAD])
            turned = pt.ps("turned", [P, 2, 4, SEQ])
            ids_in, pos_in, idn_in = pt.sem("ids_in"), pt.sem("pos_in"), pt.sem("idn_in")
            zeroed, weights_in = pt.sem("zeroed"), pt.sem("weights_in")
            rows_in = [pt.sem("rows_in_even"), pt.sem("rows_in_odd")]
            own, idn_copied = pt.sem("own"), pt.sem("idn_copied")
            ready, padded_done, turned_done, copied = (
                pt.sem("ready"), pt.sem("padded_done"), pt.sem("turned_done"), pt.sem("copied"))
            with nc.Block() as block:

                @block.sync
                def _(sp):
                    with nc.allow_non_contiguous_dma(reason="one token number per partition"):
                        sp.dma_start(ids[:, :], x.rearrange("b (q p) -> p (b q)", p=P)).then_inc(ids_in, 16)
                    sp.dma_start(posn[:, :, :], pos.rearrange("(q p) d -> p q d", p=P)).then_inc(pos_in, 16)
                    sp.dma_start(idn[:, :], ident).then_inc(idn_in, 16)
                    sp.wait_ge(zeroed, 4)
                    sp.dma_start(wv[:, :], pad_rows[:, 0:NH * PAD]).then_inc(weights_in, 16)
                    sp.dma_start(affine[:, :, :], pad_rows[:, NH * PAD:].rearrange("p (g k) -> p g k", g=NG)).then_inc(weights_in, 16)
                    sp.wait_ge(weights_in, 32)
                    for j in range(GH):
                        rows_j = slice(PAD * j, PAD * j + HD)
                        in_j = slice(HD * j, HD * j + HD)
                        sp.dma_start(wq[rows_j, :], Wq[in_j, :]).then_inc(weights_in, 16)
                        sp.dma_start(wk[rows_j, :], Wk[in_j, :]).then_inc(weights_in, 16)
                        sp.dma_start(wv[rows_j, :].rearrange("p (h c) -> p h c", h=NH)[:, :, 0:HD],
                                     Wv[in_j, :].rearrange("p (h c) -> p h c", h=NH)).then_inc(weights_in, 16)
                        for g in range(NG):
                            c0 = HD * (GH * g + j)
                            sp.dma_start(wf[rows_j, g, :].rearrange("p (h c) -> p h c", h=NH)[:, :, 0:HD],
                                         Wf[c0:c0 + HD, :].rearrange("p (h c) -> p h c", h=NH)).then_inc(weights_in, 16)
                            for n, vec in enumerate((g1, b1, g2, b2)):
                                sp.dma_start(affine[rows_j, g, n:n + 1],
                                             vec[c0:c0 + HD].rearrange("(p a) -> p a", a=1)).then_inc(weights_in, 16)
                    one = slice(HD, HD + 1)
                    sp.dma_start(wq[one, :], bq.rearrange("(a n) -> a n", a=1)).then_inc(weights_in, 16)
                    sp.dma_start(wk[one, :], bk.rearrange("(a n) -> a n", a=1)).then_inc(weights_in, 16)
                    sp.dma_start(wv[one, :].rearrange("p (h c) -> p h c", h=NH)[:, :, 0:HD],
                                 bv.rearrange("(a h c) -> a h c", a=1, h=NH)).then_inc(weights_in, 16)
                    sp.dma_start(wf[one, 0, :].rearrange("p (h c) -> p h c", h=NH)[:, :, 0:HD],
                                 bf.rearrange("(a h c) -> a h c", a=1, h=NH)).then_inc(weights_in, 16)
                    sp.wait_ge(weights_in, 16 * (2 + GH * (3 + NG * 5) + 4))

                @block.gpsimd
                def _(pool):
                    pool.memset(wq[:, :], 0.0).then_inc(zeroed, 1)
                    pool.memset(wk[:, :], 0.0).then_inc(zeroed, 1)
                    pool.memset(wv[:, :], 0.0).then_inc(zeroed, 1)
                    pool.memset(wf[:, :, :], 0.0).then_inc(zeroed, 1)
                    pool.wait_ge(ready, 1)
                    for t in range(TILES):
                        b = t // TT
                        if t % TT == 0 and b >= 2:
                            pool.wait_ge(rows_in[b % 2], 16 * TT * (b // 2))
                        pool.indirect_dma_start(rows[:, t, :], None, emb[:, :],
                                                bass.IndirectOffsetOnAxis(ap=wrapped[:, t:t + 1].bitcast(U32), axis=0)
                                                ).then_inc(rows_in[b % 2], 16)

                @block.vector
                def _(dve):
                    chain = Chain(dve, own)
                    dve.wait_ge(ids_in, 16)
                    chain(dve.tensor_scalar(wrap[:, :], ids[:, :], 0.0, float(VOCAB), ALU.is_lt, ALU.mult))
                    chain.wait()
                    chain(dve.tensor_tensor(wrap[:, :], ids[:, :], wrap[:, :], ALU.add))
                    chain.wait()
                    dve.tensor_scalar(wrapped[:, :], wrap[:, :], 0.0, float(VOCAB - 1), ALU.max, ALU.min).then_inc(ready, 1)
                    chain(dve.memset(padded[:, :, :, :, :], 0.0))
                    chain.wait()
                    chain(dve.memset(padded[:, :, :, :, HD:HD + 1], 1.0))
                    chain(dve.memset(norm[:, 1, 0, :], 1.0))
                    chain(dve.memset(norm[:, 1, 1, :], 0.0))
                    chain.wait()
                    base = chain.n
                    dve.wait_ge(pos_in, 16)
                    with dve.Fori(0, NB // 2) as it:
                        for half in range(2):
                            b = it * 2 + half
                            dve.wait_ge(rows_in[half], it * (16 * TT) + 16 * TT)
                            e = rows[:, bass.ds(b * TT, TT), :]
                            dve.wait_ge(padded_done, b)
                            dve.tensor_tensor(tmp[:, :, :], e, posn[:, :, :], ALU.add).then_inc(own, 1)
                            dve.wait_ge(own, b + (base + 1))
                            dve.wait_ge(turned_done, b)
                            dve.tensor_tensor(padded[:, half, :, :, 0:HD],
                                              tmp[:, :, :].rearrange("p q (h c) -> p q h c", h=NH),
                                              e.rearrange("p q (h c) -> p q h c", h=NH), ALU.add).then_inc(padded_done, 1)

                @block.tensor
                def _(pe):
                    pe.wait_ge(idn_in, 16)
                    pe.sem_inc(turned_done, 1)
                    with pe.Fori(0, NB // 2) as it:
                        for half in range(2):
                            b = it * 2 + half
                            pe.wait_ge(padded_done, b + 1)
                            pe.wait_ge(copied, b)
                            for g in range(NG):
                                for q in range(TT):
                                    last = pe.transpose(turned[:, half, g, P * q:P * q + P],
                                                        padded[:, half, q, GH * g:GH * g + GH, :].rearrange("p h c -> p (h c)"),
                                                        idn[:, :])
                            last.then_inc(turned_done, 1)

                @block.scalar
                def _(act):
                    act.wait_ge(idn_in, 16)
                    act.activation(idn_b[:, :], idn[:, :], ACT.Copy).then_inc(idn_copied, 1)
                    act.sem_inc(copied, 1)
                    with act.Fori(0, NB // 2) as it:
                        for half in range(2):
                            b = it * 2 + half
                            act.wait_ge(turned_done, b + 2)
                            act.activation(hT[:, bass.ds(b, 1), :, :].rearrange("p b g t -> p (b g) t"),
                                           turned[:, half, 0:NG, :], ACT.Copy).then_inc(copied, 1)

        with nc.Fori(0, LAYERS) as layer:
            token_project(nc, layer, hT, wq, wk, wv, norm, q_parts, k_parts, v_rows)
            token_attention(nc, layer, hT_u, idn, idn_b, stats, q_parts, k_parts, v_rows, SCALE, UNITS, SLOTS)
            token_norm(nc, layer, 0, stats, mean_var, power, affine, norm)
            token_dense(nc, layer, hT, wf, norm, stats)
            token_norm(nc, layer, 1, stats, mean_var, power, affine, norm)

        with ExitStack() as part:
            pt = Store(nc, part, "end")
            staged = pt.sb("staged", [P, 2, NG, SEQ])
            out_rows = pt.sb("out_rows", [P, 2, TT, D])
            turned = pt.ps("turned", [P, TT, SEQ])
            staged_done, turned_done, out_done = pt.sem("staged_done"), pt.sem("turned_done"), pt.sem("out_done")
            stored = [pt.sem("stored_even"), pt.sem("stored_odd")]
            with nc.Block() as block:

                @block.scalar
                def _(act):
                    with act.Fori(0, NB // 2) as it:
                        for half in range(2):
                            b = it * 2 + half
                            act.wait_ge(turned_done, b)
                            for g in range(NG):
                                act.activation(staged[:, half, g, :], hT[:, bass.ds(b, 1), g, :].rearrange("p b t -> p (b t)"),
                                               ACT.Identity, bias=norm[:, 1, 1, g:g + 1],
                                               scale=norm[:, 1, 0, g:g + 1]).then_inc(staged_done, 1)

                @block.tensor
                def _(pe):
                    pe.sem_inc(turned_done, 1)
                    with pe.Fori(0, NB // 2) as it:
                        for half in range(2):
                            b = it * 2 + half
                            pe.wait_ge(staged_done, b * NG + NG)
                            pe.wait_ge(out_done, b * 2)
                            for q in range(TT):
                                for g in range(NG):
                                    last = pe.transpose(turned[:, q, P * g:P * g + P], staged[:, half, g, P * q:P * q + P], idn[:, :])
                            last.then_inc(turned_done, 1)

                @block.vector
                def _(dve):
                    with dve.Fori(0, NB // 2) as it:
                        for half in range(2):
                            b = it * 2 + half
                            dve.wait_ge(turned_done, b + 2)
                            dve.wait_ge(stored[half], it * 16)
                            for n in range(2):
                                dve.tensor_copy(
                                    out_rows[:, half, 2 * n:2 * n + 2, :].rearrange("p q (h c) -> p q h c", h=NH),
                                    turned[:, 2 * n:2 * n + 2, 0:NH * PAD].rearrange("p q (h c) -> p q h c", h=NH)[:, :, :, 0:HD]
                                ).then_inc(out_done, 1)

                @block.sync
                def _(sp):
                    with sp.Fori(0, NB // 2) as it:
                        for half in range(2):
                            b = it * 2 + half
                            sp.wait_ge(out_done, b * 2 + 2)
                            sp.dma_start(h1[bass.ds(b * SEQ, SEQ), :].rearrange("(q p) d -> p q d", p=P),
                                         out_rows[:, half, :, :]).then_inc(stored[half], 16)
                    for half in range(2):
                        sp.wait_ge(stored[half], 16 * NB // 2)


def token_project(nc, layer, hT, wq, wk, wv, norm, q_parts, k_parts, v_rows):
    with ExitStack() as part:
        pt = Store(nc, part, "proj")
        staged = pt.sb("staged", [P, 2, NG, SEQ])
        full = [pt.sb(f"full_{n}", [96, 2, SEQ]) for n in "qk"]
        rest = [pt.sb(f"rest_{n}", [96, 2, SEQ]) for n in "qk"]
        parts = [pt.sb(f"parts_{n}", [96, 3, 2, SEQ], BF16) for n in "qk"]
        v_sb = pt.sb("v_sb", [P, TT, NH * PAD])
        qk_ps = [pt.ps(f"{n}_ps", [96, 2, SEQ]) for n in "qk"]
        v_ps = pt.ps("v_ps", [P, TT, SEQ])
        staged_done, restored = pt.sem("staged_done"), pt.sem("restored")
        qk_done, v_done = pt.sem("qk_done"), pt.sem("v_done")
        full_done = pt.sem("full_done")
        v_copied = pt.sem("v_copied")
        split = [pt.sem(f"split_{n}") for n in "qk"]
        stored, v_stored = [pt.sem(f"stored_{n}") for n in "qk"], pt.sem("v_stored")
        all_stored = pt.sem("all_stored")
        STORES = 3
        with nc.Block() as block:

            @block.scalar
            def _(act):
                with act.Fori(0, NB // 2) as it:
                    for half in range(2):
                        n = layer * NB + it * 2 + half
                        b = it * 2 + half
                        act.wait_ge(v_done, layer * (NB + 1) + b)
                        act.wait_ge(restored, layer * (NB + 1) + b)
                        for g in range(NG):
                            act.activation(staged[:, half, g, :], hT[:, bass.ds(b, 1), g, :].rearrange("p b t -> p (b t)"),
                                           ACT.Identity, bias=norm[:, 1, 1, g:g + 1],
                                           scale=norm[:, 1, 0, g:g + 1]).then_inc(staged_done, 1)
                        act.wait_ge(qk_done, n + 1)
                        for m in range(2):
                            act.wait_ge(split[m], n * 3)
                            act.wait_ge(stored[m], n * (16 * STORES))
                            act.activation(full[m][:, :, :], qk_ps[m][:, :, :], ACT.Relu).then_inc(full_done, 1)
                            act.activation(parts[m][:, 0, :, :], qk_ps[m][:, :, :], ACT.Relu).then_inc(full_done, 1)

            @block.tensor
            def _(pe):
                pe.sem_inc(v_done, 1)
                with pe.Fori(0, NB // 2) as it:
                    for half in range(2):
                        n = layer * NB + it * 2 + half
                        pe.wait_ge(staged_done, n * NG + NG)
                        pe.wait_ge(full_done, n * 4)
                        for m, w in enumerate((wq, wk)):
                            for c in range(2):
                                last = pe.matmul(qk_ps[m][:, c, :], w[:, 96 * c:96 * c + 96], staged[:, half, m, :],
                                                 start=True, stop=True)
                        last.then_inc(qk_done, 1)
                        pe.wait_ge(v_copied, n)
                        for q in range(TT):
                            last = pe.matmul(v_ps[:, q, 0:NH * PAD], staged[:, half, 2, P * q:P * q + P], wv[:, :],
                                             start=True, stop=True)
                        last.then_inc(v_done, 1)

            def split_parts(eng, m, n):
                eng.wait_ge(full_done, n * 4 + 2 * m + 2)
                eng.tensor_tensor(rest[m][:, :, :], full[m][:, :, :], parts[m][:, 0, :, :], ALU.subtract).then_inc(split[m], 1)
                eng.tensor_tensor(parts[m][:, 1, :, :], full[m][:, :, :], parts[m][:, 0, :, :], ALU.subtract).then_inc(split[m], 1)
                eng.wait_ge(split[m], n * 3 + 2)
                eng.tensor_tensor(parts[m][:, 2, :, :], rest[m][:, :, :], parts[m][:, 1, :, :], ALU.subtract).then_inc(split[m], 1)

            @block.gpsimd
            def _(pool):
                with pool.Fori(0, NB) as b:
                    split_parts(pool, 0, layer * NB + b)

            @block.vector
            def _(dve):
                dve.sem_inc(restored, 1)
                with dve.Fori(0, NB // 2) as it:
                    for half in range(2):
                        n = layer * NB + it * 2 + half
                        b = it * 2 + half
                        dve.wait_ge(staged_done, n * NG + NG)
                        dve.tensor_copy(hT[:, bass.ds(b, 1), :, :].rearrange("p b g t -> p (b g) t"),
                                        staged[:, half, :, :]).then_inc(restored, 1)
                        dve.wait_ge(v_done, layer * (NB + 1) + b + 2)
                        dve.wait_ge(v_stored, n * (16 * NG))
                        dve.tensor_scalar(v_sb[:, :, :], v_ps[:, :, 0:NH * PAD], 0.0, None, ALU.max).then_inc(v_copied, 1)
                        split_parts(dve, 1, n)

            @block.sync
            def _(sp):
                with sp.Fori(0, NB) as b:
                    n = layer * NB + b
                    sp.wait_ge(v_copied, n + 1)
                    for g in range(NG):
                        sp.dma_start(v_rows[bass.ds(b * (NG * SEQ) + g * SEQ, SEQ), :].rearrange("(q p) c -> p q c", p=P),
                                     v_sb[:, :, P * g:P * g + P]).then_inc(v_stored, 16)
                    for m, dram in enumerate((q_parts, k_parts)):
                        sp.wait_ge(split[m], n * 3 + 3)
                        for k in range(3):
                            sp.dma_start(dram[bass.ds(b * D + k * (NB * D), D), :].rearrange("(c p) t -> p c t", c=2),
                                         parts[m][:, k, :, :]).then_inc(stored[m], 16)
                sp.wait_ge(stored[0], (layer + 1) * (16 * STORES * NB))
                sp.wait_ge(stored[1], (layer + 1) * (16 * STORES * NB))
                sp.wait_ge(v_stored, (layer + 1) * (16 * NG * NB))
                sp.sem_inc(all_stored, 1)


def token_attention(nc, layer, hT_u, idn, idn_b, stats, q_parts, k_parts, v_rows, SCALE, UNITS, SLOTS):
    ROWS = 96 + 3
    with ExitStack() as part:
        pt = Store(nc, part, "att")
        q_sb = pt.sb("q_sb", [ROWS, SLOTS, GH, SEQ], BF16)
        k_sb = pt.sb("k_sb", [ROWS, SLOTS, GH, SEQ], BF16)
        v_sb = pt.sb("v_sb", [P, SLOTS, TT, P])
        probs = pt.sb("probs", [P, 2, GH, SEQ])
        neg_max = pt.sb("neg_max", [P, 2, GH, TT])
        max_rest = pt.sb("max_rest", [P, GH, TT])
        max_parts = pt.sb("max_parts", [P, 2, 3, GH, TT], BF16)
        max_rows = pt.sb("max_rows", [3 * GH, SEQ], BF16)
        o_raw = pt.sb("o_raw", [P, SEQ])
        o_norm = pt.sb("o_norm", [P, TT, GH, PAD])
        recip = pt.sb("recip", [P, TT, GH])
        s_ps = pt.ps("s_ps", [P, 2, SEQ])
        st_ps = pt.ps("st_ps", [P, GH, SEQ])
        o_ps = pt.ps("o_ps", [P, SEQ])
        misc = pt.ps("misc", [P, SEQ])
        misc_b = misc[0:3 * GH, :].bitcast(BF16)[:, 0:SEQ]
        loaded = [pt.sem(f"loaded{s}") for s in range(SLOTS)]
        s_done, s_read = pt.sem("s_done"), pt.sem("s_read")
        st_done, exp_done, pv_done = pt.sem("st_done"), pt.sem("exp_done"), pt.sem("pv_done")
        o_copied, o_turned, o_normed, o_back, h_added = (
            pt.sem("o_copied"), pt.sem("o_turned"), pt.sem("o_normed"), pt.sem("o_back"), pt.sem("h_added"))
        max_split, rows_turned, rows_copied, rows_sent = (
            pt.sem("max_split"), pt.sem("rows_turned"), pt.sem("rows_copied"), pt.sem("rows_sent"))
        all_sent = pt.sem("all_sent")
        own, ones_set, recip_done = pt.sem("own"), pt.sem("ones_set"), pt.sem("recip_done")
        LOADS = 13
        TURNS = UNITS // SLOTS

        with nc.Block() as block:

            def load(sp, s, u):
                for dst, src, order in ((q_sb, q_parts, (0, 1, 2, 0, 1, 0)), (k_sb, k_parts, (0, 0, 0, 1, 1, 2))):
                    for at, k in enumerate(order):
                        rows = src[bass.ds(u * (GH * HD) + k * (NB * D), GH * HD), :]
                        sp.dma_start(dst[HD * at:HD * at + HD, s, :, :],
                                     rows.rearrange("(h r) t -> r h t", h=GH)).then_inc(loaded[s], 16)
                sp.dma_start(v_sb[:, s, :, :], v_rows[bass.ds(u * SEQ, SEQ), :].rearrange("(q p) c -> p q c", p=P)
                             ).then_inc(loaded[s], 16)

            @block.sync
            def _(sp):
                for s in range(SLOTS):
                    load(sp, s, s)

                def send(s, u):
                    n = layer * UNITS + u
                    sp.wait_ge(rows_copied, n + 1)
                    sp.dma_start(q_sb[96:99, s % SLOTS, :, :], max_rows[:, :]).then_inc(rows_sent, 16)

                send(0, 0)
                with sp.Fori(0, TURNS - 1) as turn:
                    for s in range(SLOTS):
                        u = turn * SLOTS + s
                        send(s + 1, u + 1)
                        sp.wait_ge(pv_done, (layer * UNITS + u) * TT + TT)
                        load(sp, s, u + SLOTS)
                for s in range(SLOTS - 1):
                    send(s + 1, (TURNS - 1) * SLOTS + s + 1)
                sp.wait_ge(rows_sent, (layer + 1) * (16 * UNITS))
                sp.sem_inc(all_sent, 1)

            def score_rows(pe, s, u, q):
                n = layer * UNITS + u
                for h in range(GH):
                    m = 4 * q + h
                    pe.wait_ge(s_read, n * 16 + max(m - 1, 0))
                    pe.matmul(s_ps[:, m % 2, :], q_sb[0:96, s, h, P * q:P * q + P], k_sb[0:96, s, h, :],
                              start=True, stop=True).then_inc(s_done, 1)

            def turn_maxima(pe, s, u):
                n = layer * UNITS + u
                pe.wait_ge(max_split, n + 1)
                for q in range(TT):
                    last = pe.transpose(misc_b[:, P * q:P * q + P],
                                        max_parts[:, s % 2, :, :, q].rearrange("p k h -> p (k h)"), idn_b[:, :])
                last.then_inc(rows_turned, 1)

            @block.tensor
            def _(pe):
                for s in range(2):
                    pe.wait_ge(loaded[s], (layer * TURNS + 1) * (16 * LOADS))
                    for q in range(TT):
                        score_rows(pe, s, s, q)
                turn_maxima(pe, 0, 0)
                pe.wait_ge(ones_set, layer * 2 + 2)

                def turn_out(n, rows):
                    pe.wait_ge(o_copied, n + 1)
                    pe.wait_ge(rows_copied, rows)
                    for q in range(TT):
                        last = pe.transpose(misc[:, P * q:P * q + P], o_raw[:, P * q:P * q + P], idn[:, :])
                    last.then_inc(o_turned, 1)

                def turn_back(n):
                    pe.wait_ge(o_normed, n + 1)
                    for q in range(TT):
                        last = pe.transpose(misc[:, P * q:P * q + P],
                                            o_norm[:, q, :, :].rearrange("p h c -> p (h c)"), idn[:, :])
                    last.then_inc(o_back, 1)

                def unit(s, u, turn, ahead, following, first):
                    n = layer * UNITS + u
                    s2, s1 = (s + 2) % SLOTS, (s + 1) % SLOTS
                    pe.wait_ge(rows_sent, n * 16 + 16)
                    if ahead:
                        pe.wait_ge(loaded[s2], (layer * TURNS + turn + (2 if s + 2 >= SLOTS else 1)) * (16 * LOADS))

                    def scores(t):
                        for half in range(2):
                            pe.wait_ge(exp_done, n * 8 + (2 * t + half - 1 if t else 0))
                            for h in (2 * half, 2 * half + 1):
                                last = pe.matmul(st_ps[:, h, :], k_sb[0:ROWS, s, h, P * t:P * t + P], q_sb[0:ROWS, s, h, :],
                                                 start=True, stop=True)
                            last.then_inc(st_done, 1)

                    def values(t):
                        pe.wait_ge(exp_done, n * 8 + 2 * t + 2)
                        if t == 0:
                            pe.wait_ge(o_copied, n)
                        for h in range(GH):
                            last = pe.matmul(o_ps[PAD * h:PAD * h + PAD, :], v_sb[:, s, t, PAD * h:PAD * h + PAD],
                                             probs[:, t % 2, h, :], start=(t == 0), stop=(t == TT - 1))
                        last.then_inc(pv_done, 1)

                    scores(0)
                    if ahead:
                        score_rows(pe, s2, u + 2, 0)
                    if not first:
                        turn_out(n - 1, n + 1)
                    scores(1)
                    values(0)
                    if ahead:
                        score_rows(pe, s2, u + 2, 1)
                    if not first:
                        turn_back(n - 1)
                    scores(2)
                    values(1)
                    if ahead:
                        score_rows(pe, s2, u + 2, 2)
                    if following:
                        if not first:
                            pe.wait_ge(h_added, n)
                        turn_maxima(pe, s1, u + 1)
                    scores(3)
                    values(2)
                    if ahead:
                        score_rows(pe, s2, u + 2, 3)
                    values(3)

                for s in range(SLOTS):
                    unit(s, s, 0, True, True, s == 0)
                with pe.Fori(1, TURNS - 1) as turn:
                    for s in range(SLOTS):
                        unit(s, turn * SLOTS + s, turn, True, True, False)
                for s in range(SLOTS):
                    unit(s, (TURNS - 1) * SLOTS + s, TURNS - 1, s < SLOTS - 2, s < SLOTS - 1, False)
                end = (layer + 1) * UNITS
                pe.wait_ge(h_added, end - 1)
                turn_out(end - 1, end)
                turn_back(end - 1)

            @block.scalar
            def _(act):
                def copy_out(n):
                    act.wait_ge(pv_done, n * TT + TT)
                    act.wait_ge(o_turned, n)
                    act.activation(o_raw[:, :], o_ps[:, :], ACT.Copy).then_inc(o_copied, 1)

                def unit(s, u, first):
                    n = layer * UNITS + u
                    for t in range(TT):
                        for half in range(2):
                            act.wait_ge(st_done, n * 8 + 2 * t + half + 1)
                            if t >= 2:
                                act.wait_ge(pv_done, n * TT + t - 1)
                            else:
                                act.wait_ge(pv_done, n * TT if t == 1 or first else n * TT - 1)
                            act.activation(probs[:, t % 2, 2 * half:2 * half + 2, :], st_ps[:, 2 * half:2 * half + 2, :],
                                           ACT.Exp, scale=SCALE).then_inc(exp_done, 1)
                        if t == 0 and not first:
                            copy_out(n - 1)

                for s in range(SLOTS):
                    unit(s, s, s == 0)
                with act.Fori(1, TURNS) as turn:
                    for s in range(SLOTS):
                        unit(s, turn * SLOTS + s, False)
                copy_out(layer * UNITS + UNITS - 1)

            @block.gpsimd
            def _(pool):
                pool.memset(k_sb[96:99, :, :, :].rearrange("p s h t -> p (s h t)"), 1.0).then_inc(ones_set, 1)

            @block.vector
            def _(dve):
                def maxima(s, u, q):
                    n = layer * UNITS + u
                    for h in range(GH):
                        m = 4 * q + h
                        dve.wait_ge(s_done, n * 16 + m + 1)
                        dve.tensor_reduce(neg_max[:, s % 2, h, q:q + 1], s_ps[:, m % 2, :], AX.X, ALU.max,
                                          negate=True).then_inc(s_read, 1)

                def split_maxima(s, u):
                    n = layer * UNITS + u
                    dve.wait_ge(s_read, n * 16 + 16)
                    if isinstance(u, int) and u < 2:
                        dve.wait_ge(rows_turned, layer * UNITS)
                    else:
                        dve.wait_ge(rows_turned, n - 1)
                    mp = max_parts[:, s % 2, :, :, :]
                    nm = neg_max[:, s % 2, :, :]
                    dve.tensor_copy(mp[:, 0, :, :], nm).then_inc(own, 1)
                    dve.wait_ge(own, n * 3 + 1)
                    dve.tensor_tensor(max_rest[:, :, :], nm, mp[:, 0, :, :], ALU.subtract).then_inc(own, 1)
                    dve.wait_ge(own, n * 3 + 2)
                    dve.tensor_copy(mp[:, 1, :, :], max_rest[:, :, :]).then_inc(own, 1)
                    dve.wait_ge(own, n * 3 + 3)
                    dve.tensor_tensor(mp[:, 2, :, :], max_rest[:, :, :], mp[:, 1, :, :], ALU.subtract).then_inc(max_split, 1)

                def copy_rows(s, u):
                    n = layer * UNITS + u
                    dve.wait_ge(rows_turned, n + 1)
                    dve.wait_ge(rows_sent, n * 16)
                    dve.tensor_copy(max_rows[:, :], misc_b).then_inc(rows_copied, 1)

                def normalise(n):
                    dve.wait_ge(o_turned, n + 1)
                    o = misc[:, :].rearrange("p (q h c) -> p q h c", q=TT, h=GH)
                    dve.reciprocal(recip[:, :, :], o[:, :, :, HD]).then_inc(recip_done, 1)
                    dve.wait_ge(recip_done, n + 1)
                    dve.wait_ge(ones_set, layer * 2 + 2)
                    dve.wait_ge(o_back, n)
                    for q in range(TT):
                        ins = dve.tensor_tensor(o_norm[:, q, :, 0:HD], o[:, q, :, 0:HD],
                                                recip[:, q, :].unsqueeze(2).to_broadcast([P, GH, HD]), ALU.mult)
                    ins.then_inc(o_normed, 1)

                def add(n, u):
                    dve.wait_ge(o_back, n + 1)
                    dst = hT_u[:, bass.ds(u, 1), :].rearrange("p u t -> p (u t)")
                    dve.tensor_tensor(dst, dst, misc[:, :], ALU.add).then_inc(h_added, 1)

                dve.memset(o_norm[:, :, :, :], 0.0).then_inc(ones_set, 1)
                for s in range(2):
                    for q in range(TT):
                        maxima(s, s, q)
                    split_maxima(s, s)
                copy_rows(0, 0)

                def unit(s, u, ahead, following, first):
                    n = layer * UNITS + u
                    if ahead:
                        maxima(s + 2, u + 2, 0)
                    if not first:
                        normalise(n - 1)
                    if ahead:
                        maxima(s + 2, u + 2, 1)
                    if not first:
                        add(n - 1, u - 1)
                    if ahead:
                        maxima(s + 2, u + 2, 2)
                    if following:
                        copy_rows(s + 1, u + 1)
                    if ahead:
                        maxima(s + 2, u + 2, 3)
                        split_maxima(s + 2, u + 2)

                for s in range(SLOTS):
                    unit(s, s, True, True, s == 0)
                with dve.Fori(1, TURNS - 1) as turn:
                    for s in range(SLOTS):
                        unit(s, turn * SLOTS + s, True, True, False)
                for s in range(SLOTS):
                    unit(s, (TURNS - 1) * SLOTS + s, s < SLOTS - 2, s < SLOTS - 1, False)
                normalise(layer * UNITS + UNITS - 1)
                add(layer * UNITS + UNITS - 1, UNITS - 1)
                with dve.Fori(0, NB) as b:
                    dve.wait_ge(h_added, (layer + 1) * UNITS)
                    for g in range(NG):
                        dve.bn_stats(stats[:, g, bass.ds(b, 1), :].rearrange("p b k -> p (b k)"),
                                     hT_u[:, bass.ds(b * NG + g, 1), :].rearrange("p u t -> p (u t)"))


def token_norm(nc, layer, which, stats, mean_var, power, affine, norm):
    with ExitStack() as part:
        pt = Store(nc, part, f"norm{which}")
        own, var_done, pow_done = pt.sem("own"), pt.sem("var_done"), pt.sem("pow_done")
        scale, shift = norm[:, which, 0, :], norm[:, which, 1, :]
        with nc.Block() as block:

            @block.vector
            def _(dve):
                for g in range(NG):
                    dve.bn_aggr(mean_var[:, g, :], stats[:, g, :, :].rearrange("p b k -> p (b k)")).then_inc(own, 1)
                dve.wait_ge(own, layer * 5 + 3)
                dve.memset(power[:, 1, :], -0.5).then_inc(var_done, 1)
                dve.tensor_scalar(power[:, 0, :], mean_var[:, :, 1], EPS, None, ALU.add).then_inc(var_done, 1)
                dve.wait_ge(pow_done, layer + 1)
                dve.tensor_tensor(scale, power[:, 0, :], affine[:, :, 2 * which], ALU.mult).then_inc(own, 1)
                dve.wait_ge(own, layer * 5 + 4)
                dve.tensor_tensor(shift, mean_var[:, :, 0], scale, ALU.mult).then_inc(own, 1)
                dve.wait_ge(own, layer * 5 + 5)
                dve.tensor_tensor(shift, affine[:, :, 2 * which + 1], shift, ALU.subtract)

            @block.gpsimd
            def _(pool):
                pool.wait_ge(var_done, layer * 2 + 2)
                pool.tensor_tensor(power[:, 0, :], power[:, 0, :], power[:, 1, :], ALU.pow).then_inc(pow_done, 1)


def token_dense(nc, layer, hT, wf, norm, stats):
    with ExitStack() as part:
        pt = Store(nc, part, "dense")
        staged = pt.sb("staged", [P, 2, NG, SEQ])
        out_ps = pt.ps("out_ps", [P, 2, 4, SEQ])
        staged_done, product_done, added, stats_done = (
            pt.sem("staged_done"), pt.sem("product_done"), pt.sem("added"), pt.sem("stats_done"))
        with nc.Block() as block:

            @block.scalar
            def _(act):
                with act.Fori(0, NB // 2) as it:
                    for half in range(2):
                        b = it * 2 + half
                        n = layer * NB + b
                        act.wait_ge(added, layer * (NB + 1) + b)
                        for g in range(NG):
                            act.activation(staged[:, half, g, :], hT[:, bass.ds(b, 1), g, :].rearrange("p b t -> p (b t)"),
                                           ACT.Identity, bias=norm[:, 0, 1, g:g + 1],
                                           scale=norm[:, 0, 0, g:g + 1]).then_inc(staged_done, 1)

            @block.tensor
            def _(pe):
                with pe.Fori(0, NB // 2) as it:
                    for half in range(2):
                        b = it * 2 + half
                        pe.wait_ge(staged_done, (layer * NB + b) * NG + NG)
                        pe.wait_ge(added, layer * (NB + 1) + b)
                        for m in range(NG):
                            for g in range(NG):
                                last = pe.matmul(out_ps[:, half, m, :], wf[:, g, P * m:P * m + P], staged[:, half, g, :],
                                                 start=(g == 0), stop=(g == NG - 1))
                        last.then_inc(product_done, 1)

            @block.vector
            def _(dve):
                dve.sem_inc(added, 1)
                with dve.Fori(0, NB // 2) as it:
                    for half in range(2):
                        b = it * 2 + half
                        n = layer * NB + b
                        dve.wait_ge(product_done, n + 1)
                        dve.tensor_tensor(hT[:, bass.ds(b, 1), :, :].rearrange("p b g t -> p (b g) t"),
                                          out_ps[:, half, 0:NG, :], staged[:, half, :, :], ALU.add).then_inc(added, 1)
                        dve.wait_ge(added, layer * (NB + 1) + b + 2)
                        for g in range(NG):
                            ins = dve.bn_stats(stats[:, g, bass.ds(b, 1), :].rearrange("p b k -> p (b k)"),
                                               hT[:, bass.ds(b, 1), g, :].rearrange("p b t -> p (b t)"))
                        ins.then_inc(stats_done, 1)


C2 = D // 2
GROUPS = TILES // TT


def row_semaphores(nc):
    rows = [nc.alloc_semaphore(name=f"row_{n}") for n in ("stats_done", "aggr_done", "var_done", "pow_done")]
    turns = [nc.alloc_semaphore(name=f"turn_{n}") for n in ("rows_done", "turned_done", "copied", "added")]
    return rows, turns


def row_statistics(nc, sems, call, H, mean, rstd):
    with ExitStack() as part:
        pt = Store(nc, part, f"row_stats{call}")
        stats = pt.sb("stats", [P, TILES, 6])
        mean_var = pt.sb("mean_var", [P, TILES, 2])
        var = pt.sb("var", [P, TILES])
        half = pt.sb("half", [P, TILES])
        stats_done, aggr_done, var_done, pow_done = sems
        before = call * TILES
        with nc.Block() as block:

            @block.vector
            def _(dve):
                with dve.Fori(0, TILES // TT) as i:
                    for k in range(TT):
                        t = bass.ds(i * TT + k, 1)
                        dve.bn_stats(stats[:, t, :].rearrange("p t k -> p (t k)"),
                                     H[:, t, :].rearrange("p t d -> p (t d)")).then_inc(stats_done, 1)
                for t in range(TILES):
                    if t % 16 == 0:
                        dve.wait_ge(stats_done, before + t + 16)
                    dve.bn_aggr(mean_var[:, t, :], stats[:, t, :]).then_inc(aggr_done, 1)
                dve.wait_ge(aggr_done, before + TILES)
                dve.memset(half[:, :], -0.5).then_inc(var_done, 1)
                dve.tensor_copy(mean[:, :], mean_var[:, :, 0])
                dve.tensor_scalar(var[:, :], mean_var[:, :, 1], EPS, None, ALU.add).then_inc(var_done, 1)

            @block.gpsimd
            def _(pool):
                pool.wait_ge(var_done, call * 2 + 2)
                pool.tensor_tensor(rstd[:, :], var[:, :], half[:, :], ALU.pow).then_inc(pow_done, 1)


def turn_rows(nc, sems, call, X, mean, rstd, idn, xT, add_to=None, gamma_beta=None):
    with ExitStack() as part:
        pt = Store(nc, part, f"turn_rows{call}")
        rows = pt.sb("rows", [P, 2, TT, D])
        turned = pt.ps("turned", [C2, 2, 2, SEQ])
        rows_done, turned_done, copied, added = sems
        turns = call * (GROUPS + 1)
        with nc.Block() as block:

            @block.vector
            def _(dve):
                with dve.Fori(0, GROUPS // 2) as it:
                    for half in range(2):
                        g = it * 2 + half
                        dve.wait_ge(turned_done, turns + g)
                        for k in range(TT):
                            t = bass.ds(g * TT + k, 1)
                            dve.tensor_scalar(rows[:, half, k, :], X[:, t, :].rearrange("p t d -> p (t d)"),
                                              mean[:, t], rstd[:, t], ALU.subtract, ALU.mult).then_inc(rows_done, 1)
                        if add_to is not None:
                            dve.wait_ge(rows_done, call * TILES + g * TT + TT)
                            dst = add_to[:, bass.ds(g * TT, TT), :]
                            dve.tensor_tensor(dst, dst, rows[:, half, :, :], ALU.add).then_inc(added, 1)

            @block.tensor
            def _(pe):
                pe.sem_inc(turned_done, 1)
                with pe.Fori(0, GROUPS // 2) as it:
                    for half in range(2):
                        g = it * 2 + half
                        pe.wait_ge(rows_done, call * TILES + g * TT + TT)
                        pe.wait_ge(copied, turns * 2 + g * 2)
                        for c in range(2):
                            for k in range(TT):
                                last = pe.transpose(turned[:, half, c, P * k:P * k + P], rows[:, half, k, C2 * c:C2 * c + C2],
                                                    idn[:, :])
                        last.then_inc(turned_done, 1)

            @block.scalar
            def _(act):
                act.sem_inc(copied, 2)
                with act.Fori(0, GROUPS // 2) as it:
                    for half in range(2):
                        g = it * 2 + half
                        act.wait_ge(turned_done, turns + g + 2)
                        for c in range(2):
                            dst = xT[:, c, bass.ds(g * SEQ, SEQ)]
                            if gamma_beta is None:
                                act.activation(dst, turned[:, half, c, :], ACT.Copy).then_inc(copied, 1)
                            else:
                                act.activation(dst, turned[:, half, c, :], ACT.Identity, bias=gamma_beta[:, c, 1:2],
                                               scale=gamma_beta[:, c, 0:1]).then_inc(copied, 1)


def normalise_rows(nc, name, H, mean, rstd, X):
    normed, added = nc.alloc_semaphore(name=f"{name}_normed"), nc.alloc_semaphore(name=f"{name}_added")
    with nc.Block() as block:

        @block.vector
        def _(dve):
            with dve.Fori(0, GROUPS) as g:
                for k in range(TT):
                    t = bass.ds(g * TT + k, 1)
                    dve.tensor_scalar(X[:, t, :].rearrange("p t d -> p (t d)"), H[:, t, :].rearrange("p t d -> p (t d)"),
                                      mean[:, t], rstd[:, t], ALU.subtract, ALU.mult).then_inc(normed, 1)
                dve.wait_ge(normed, g * TT + TT)
                four = bass.ds(g * TT, TT)
                dve.tensor_tensor(H[:, four, :], H[:, four, :], X[:, four, :], ALU.add).then_inc(added, 1)


def feed_forward(nc, name, H, xT, experts, hidden, w_in, w_out, func, bias=None, gates=None):
    M = hidden // P
    PAIRS = GROUPS // 2
    with ExitStack() as part:
        pt = Store(nc, part, name)
        copies = min(2, experts)
        w1 = pt.sb("w1", [C2, copies, 2, hidden])
        w2 = pt.sb("w2", [P, copies, M, D])
        hid = pt.sb("hid", [P, 2, M, SEQ])
        hid_ps = pt.ps("hid_ps", [P, 4, SEQ])
        out_ps = pt.ps("out_ps", [P, 2, 2, SEQ])
        w_in_sem = [pt.sem(f"weights_in{c}") for c in range(copies)]
        hid_done, func_done, out_done, added = (
            pt.sem("hid_done"), pt.sem("func_done"), pt.sem("out_done"), pt.sem("added"))
        with nc.Block() as block:

            def over_experts(eng, body):
                if experts == 1:
                    body(0, 0)
                else:
                    with eng.Fori(0, experts // 2) as pair:
                        for c in range(2):
                            body(pair * 2 + c, c)

            @block.sync
            def _(sp):
                def load(e, c):
                    sp.dma_start(w1[:, c, :, :], w_in(e)).then_inc(w_in_sem[c], 16)
                    sp.dma_start(w2[:, c, :, :], w_out(e)).then_inc(w_in_sem[c], 16)

                for c in range(copies):
                    load(c, c)
                if experts > 2:
                    with sp.Fori(0, experts // 2 - 1) as pair:
                        for c in range(2):
                            e = pair * 2 + c
                            sp.wait_ge(out_done, e * GROUPS + GROUPS + 1)
                            load(e + 2, c)

            @block.tensor
            def _(pe):
                def first(e, c, g, half):
                    n = e * GROUPS + g
                    for m in range(M):
                        at = (half * M + m) % 4
                        pe.wait_ge(func_done, n * M + m)
                        for k in range(2):
                            last = pe.matmul(hid_ps[:, at, :], w1[:, c, k, P * m:P * m + P], xT[:, k, bass.ds(g * SEQ, SEQ)],
                                             start=(k == 0), stop=(k == 1))
                        last.then_inc(hid_done, 1)

                def second(e, c, g, half):
                    n = e * GROUPS + g
                    pe.wait_ge(func_done, n * M + M + 3)
                    pe.wait_ge(added, n * TT)
                    for k in range(TT):
                        for m in range(M):
                            last = pe.matmul(out_ps[:, half, k // 2, D * (k % 2):D * (k % 2) + D], hid[:, half, m, P * k:P * k + P],
                                             w2[:, c, m, :], start=(m == 0), stop=(m == M - 1))
                    last.then_inc(out_done, 1)

                def expert(e, c):
                    pe.wait_ge(w_in_sem[c], (e - c) * 16 + 32 if experts > 1 else 32)
                    first(e, c, 0, 0)
                    with pe.Fori(0, PAIRS - 1) as it:
                        first(e, c, it * 2 + 1, 1)
                        second(e, c, it * 2, 0)
                        first(e, c, it * 2 + 2, 0)
                        second(e, c, it * 2 + 1, 1)
                    first(e, c, GROUPS - 1, 1)
                    second(e, c, GROUPS - 2, 0)
                    second(e, c, GROUPS - 1, 1)

                pe.sem_inc(out_done, 1)
                over_experts(pe, expert)

            @block.scalar
            def _(act):
                def group(n, half):
                    act.wait_ge(out_done, n)
                    for m in range(M):
                        act.wait_ge(hid_done, n * M + m + 1)
                        if bias is None:
                            act.activation(hid[:, half, m, :], hid_ps[:, (half * M + m) % 4, :], func).then_inc(func_done, 1)
                        else:
                            act.activation(hid[:, half, m, :], hid_ps[:, (half * M + m) % 4, :], func,
                                           bias=bias[:, m:m + 1]).then_inc(func_done, 1)

                act.sem_inc(func_done, 3)
                with act.Fori(0, experts * PAIRS) as it:
                    for half in range(2):
                        group(it * 2 + half, half)

            @block.vector
            def _(dve):
                def expert(e, c):
                    with dve.Fori(0, PAIRS) as it:
                        for half in range(2):
                            g = it * 2 + half
                            n = e * GROUPS + g
                            dve.wait_ge(out_done, n + 2)
                            for k in range(TT):
                                dst = H[:, bass.ds(g * TT + k, 1), :].rearrange("p t d -> p (t d)")
                                out = out_ps[:, half, k // 2, D * (k % 2):D * (k % 2) + D]
                                if gates is None:
                                    dve.tensor_tensor(dst, out, dst, ALU.add).then_inc(added, 1)
                                else:
                                    gate = gates[:, bass.ds((g * TT + k) * experts + e, 1)]
                                    dve.scalar_tensor_tensor(dst, out, gate, dst, ALU.mult, ALU.add).then_inc(added, 1)

                dve.sem_inc(added, TT)
                over_experts(dve, expert)


WIN = 5
COLS = P // NB
SPAN = COLS + WIN - 1
KEYS = NB * SPAN
HID = 96
HEADS, DH = 4, 24
RPB = 2 * WIN - 1
UROWS = 2 * NB - 1


def neighborhood_stage(nc, h1, h2, weights, turned, small, const, row_sems, turn_sems):
    fc1_b, convA_b, convB_b, qkv_b, rpb, proj_b, fc2_b = weights
    fc1_t, convA_t, convB_t, qkv_t, proj_t, fc2_t = turned
    shifts = small
    with ExitStack() as stage:
        st = Store(nc, stage, "near")
        H = st.sb("H", [P, TILES, D])
        idn = st.sb("idn", [P, P])
        xs = st.sb("xs", [HID + 1, NB, SEQ + WIN - 1])
        table = st.sb("table", [P, 3, HEADS, KEYS])
        in_sem, out_sem, zero_done = st.sem("in"), st.sem("out"), st.sem("zero_done")

        with ExitStack() as part:
            pt = Store(nc, part, "near_load")
            bias = pt.sb("bias", [P, HEADS, KEYS])
            mask = pt.sb("mask", [P, 3, KEYS])
            zeros = pt.sb("zeros", [HID, COLS * HEADS * UROWS * SPAN // HID])
            shifted = pt.sem("shifted")
            with nc.Block() as block:

                @block.gpsimd
                def _(pool):
                    pool.memset(zeros[:, :], 0.0).then_inc(zero_done, 1)
                    pool.memset(xs[0:HID, :, :].rearrange("p b w -> p (b w)"), 0.0).then_inc(zero_done, 1)
                    pool.memset(xs[HID:, :, :].rearrange("p b w -> p (b w)"), 1.0).then_inc(zero_done, 1)

                @block.sync
                def _(sp):
                    for b in range(NB):
                        sp.dma_start(H[COLS * b:COLS * b + COLS, :, :],
                                     h1[SEQ * b:SEQ * b + SEQ, :].rearrange("(j w) d -> w j d", w=COLS)).then_inc(in_sem, 16)
                    sp.dma_start(idn[:, :], const["ident"]).then_inc(in_sem, 16)
                    sp.dma_start(mask[:, :, :], const["near_mask"].rearrange("p (v k) -> p v k", v=3)).then_inc(in_sem, 16)
                    sp.wait_ge(zero_done, 1)
                    sp.dma_start(shifts.rearrange("w n u c -> (w n u c)").rearrange("(p k) -> p k", p=HID),
                                 zeros[:, :]).then_inc(shifted, 16)
                    sp.wait_ge(shifted, 16)
                    half = WIN // 2
                    for w in range(COLS):
                        c0, c1 = max(0, w - half), min(SPAN, w + half + WIN)
                        r0 = c0 - half - w + WIN - 1
                        sp.dma_start(shifts[w, :, NB - WIN:NB - WIN + RPB, c0:c1], rpb[:, :, r0:r0 + c1 - c0]).then_inc(shifted, 16)
                    sp.wait_ge(shifted, 16 * (1 + COLS))
                    for b in range(NB):
                        sp.dma_start(bias[COLS * b:COLS * b + COLS, :, :].rearrange("w n (b c) -> w n b c", b=NB),
                                     shifts[:, :, NB - 1 - b:2 * NB - 1 - b, :]).then_inc(in_sem, 16)
                    sp.wait_ge(in_sem, 16 * (2 * NB + 2))

                @block.vector
                def _(dve):
                    dve.wait_ge(in_sem, 16 * (2 * NB + 2))
                    for v in range(3):
                        dve.tensor_tensor(table[:, v, :, :], bias[:, :, :],
                                          mask[:, v, :].unsqueeze(1).to_broadcast([P, HEADS, KEYS]), ALU.add)

        with ExitStack() as part:
            pt = Store(nc, part, "near_in")
            mean = pt.sb("mean", [P, TILES])
            rstd = pt.sb("rstd", [P, TILES])
            xT = pt.sb("xT", [C2, 2, TOKENS])
            row_statistics(nc, row_sems, 0, H, mean, rstd)
            turn_rows(nc, turn_sems, 0, H, mean, rstd, idn, xT, add_to=H)
            CA = 64
            w1 = pt.sb("w1", [C2, 2, HID])
            wa = pt.sb("wa", [HID, CA])
            wb = pt.sb("wb", [CA, HID])
            b1 = pt.sb("b1", [HID, 1])
            ba = pt.sb("ba", [CA, 1])
            bb = pt.sb("bb", [HID, 1])
            x1 = pt.sb("x1", [HID, 2, SEQ])
            mid = pt.sb("mid", [CA, 2, SEQ])
            total = pt.sb("total", [HID, 2, SEQ])
            x1_ps = pt.ps("x1_ps", [HID, 2, SEQ])
            mid_ps = pt.ps("mid_ps", [CA, 2, SEQ])
            total_ps = pt.ps("total_ps", [HID, 2, SEQ])
            loaded, x1_done, x1_copied = pt.sem("loaded"), pt.sem("x1_done"), pt.sem("x1_copied")
            mid_done, mid_copied = pt.sem("mid_done"), pt.sem("mid_copied")
            total_done, summed, gelu_done = pt.sem("total_done"), pt.sem("summed"), pt.sem("gelu_done")
            nc.scalar.preload_act_table(ACT.Gelu)
            with nc.Block() as block:

                @block.sync
                def _(sp):
                    sp.dma_start(w1[:, :, :], fc1_t).then_inc(loaded, 16)
                    sp.dma_start(wa[:, :], convA_t.rearrange("p a n -> p (a n)")).then_inc(loaded, 16)
                    sp.dma_start(wb[:, :], convB_t.rearrange("p a n -> p (a n)")).then_inc(loaded, 16)
                    for dst, src in ((b1, fc1_b), (ba, convA_b), (bb, convB_b)):
                        sp.dma_start(dst[:, :], src.rearrange("(p a) -> p a", a=1)).then_inc(loaded, 16)
                    sp.wait_ge(loaded, 16 * 6)

                @block.tensor
                def _(pe):
                    def front(g, half):
                        pe.wait_ge(x1_copied, g)
                        for c in range(2):
                            last = pe.matmul(x1_ps[:, half, :], w1[:, c, :], xT[:, c, bass.ds(g * SEQ, SEQ)], start=(c == 0), stop=(c == 1))
                        last.then_inc(x1_done, 1)

                    def middle(g, half):
                        pe.wait_ge(x1_copied, g + 3)
                        pe.wait_ge(mid_copied, g)
                        pe.matmul(mid_ps[:, half, :], wa[:, :], x1[:, half, :], start=True, stop=True).then_inc(mid_done, 1)

                    def back(g, half):
                        pe.wait_ge(mid_copied, g + 3)
                        pe.wait_ge(summed, g)
                        pe.matmul(total_ps[:, half, :], wb[:, :], mid[:, half, :], start=True, stop=True).then_inc(total_done, 1)

                    pe.wait_ge(loaded, 16 * 6)
                    front(0, 0)
                    middle(0, 0)
                    with pe.Fori(0, GROUPS // 2 - 1) as it:
                        for half in (1, 0):
                            g = it * 2 + (1 if half else 2)
                            front(g, half)
                            back(it * 2 + (0 if half else 1), 1 - half)
                            middle(g, half)
                    front(GROUPS - 1, 1)
                    back(GROUPS - 2, 0)
                    middle(GROUPS - 1, 1)
                    back(GROUPS - 1, 1)

                @block.scalar
                def _(act):
                    act.wait_ge(loaded, 16 * 6)
                    act.sem_inc(x1_copied, 2)
                    act.sem_inc(gelu_done, 2)

                    def front(g, half):
                        act.wait_ge(x1_done, g + 1)
                        act.wait_ge(summed, g)
                        act.activation(x1[:, half, :], x1_ps[:, half, :], ACT.Identity, bias=b1[:, :]).then_inc(x1_copied, 1)

                    def last(g, half):
                        act.wait_ge(summed, g + 3)
                        act.activation(xs[0:HID, :, bass.ds(g * (TT * COLS) + WIN // 2, TT * COLS)].rearrange("p b (k w) -> p k b w", k=TT),
                                       total[:, half, :].rearrange("p (k b w) -> p k b w", k=TT, b=NB), ACT.Gelu).then_inc(gelu_done, 1)

                    front(0, 0)
                    with act.Fori(0, GROUPS // 2 - 1) as it:
                        for half in (1, 0):
                            front(it * 2 + (1 if half else 2), half)
                            last(it * 2 + (0 if half else 1), 1 - half)
                    front(GROUPS - 1, 1)
                    last(GROUPS - 2, 0)
                    last(GROUPS - 1, 1)

                @block.vector
                def _(dve):
                    dve.wait_ge(loaded, 16 * 6)
                    dve.sem_inc(mid_copied, 2)
                    dve.sem_inc(summed, 2)

                    def middle(g, half):
                        dve.wait_ge(mid_done, g + 1)
                        dve.tensor_scalar(mid[:, half, :], mid_ps[:, half, :], ba[:, :], None, ALU.add).then_inc(mid_copied, 1)

                    def last(g, half):
                        dve.wait_ge(total_done, g + 1)
                        dve.wait_ge(gelu_done, g)
                        dve.scalar_tensor_tensor(total[:, half, :], total_ps[:, half, :], bb[:, :], x1[:, half, :],
                                                 ALU.add, ALU.add).then_inc(summed, 1)

                    middle(0, 0)
                    with dve.Fori(0, GROUPS // 2 - 1) as it:
                        for half in (1, 0):
                            last(it * 2 + (0 if half else 1), 1 - half)
                            middle(it * 2 + (1 if half else 2), half)
                    last(GROUPS - 2, 0)
                    middle(GROUPS - 1, 1)
                    last(GROUPS - 1, 1)

        with ExitStack() as part:
            pt = Store(nc, part, "near_att")
            wq = pt.sb("wq", [HID + 1, HEADS, PAD])
            wk = pt.sb("wk", [HID + 1, HEADS, PAD])
            wv = pt.sb("wv", [HID + 1, HEADS, PAD])
            wp = pt.sb("wp", [HID + 1, HID])
            w2 = pt.sb("w2", [HID + 1, D])
            xw = pt.sb("xw", [HID + 1, 2, KEYS])
            q_t = pt.sb("q_t", [P, 2, P])
            k_diag = pt.sb("k_diag", [P, 2, HEADS, KEYS])
            v = pt.sb("v", [KEYS // 2, 2, 2, HEADS * PAD])
            logits = pt.sb("logits", [P, HEADS, KEYS])
            shifted = pt.sb("shifted", [P, HEADS, KEYS])
            probs = pt.sb("probs", [P, 2, HEADS, KEYS])
            high = pt.sb("high", [P, HEADS])
            recip = pt.sb("recip", [P, HEADS])
            probs_t = pt.sb("probs_t", [KEYS // 2, 2, TT, P])
            raw = pt.sb("raw", [P, P])
            att = pt.sb("att", [P, HEADS, DH])
            att_t = pt.sb("att_t", [HID + 1, P])
            proj = pt.sb("proj", [HID + 1, P])
            qk_ps = pt.ps("qk_ps", [P, SEQ])
            v_ps = pt.ps("v_ps", [P, SEQ])
            logits_ps = pt.ps("logits_ps", [P, 2, SEQ])
            turned_ps = pt.ps("turned_ps", [KEYS // 2, 2, SEQ])
            att_ps = pt.ps("att_ps", [P, 4, P])
            out_ps = pt.ps("out_ps", [P, SEQ])
            loaded, zeroed = pt.sem("loaded"), pt.sem("zeroed")
            xw_done, qkv_done, qkv_copied = pt.sem("xw_done"), pt.sem("qkv_done"), pt.sem("qkv_copied")
            logits_done, logits_read = pt.sem("logits_done"), pt.sem("logits_read")
            max_done, shifted_done, exp_done = pt.sem("max_done"), pt.sem("shifted_done"), pt.sem("exp_done")
            turned_done, turned_copied = pt.sem("turned_done"), pt.sem("turned_copied")
            pv_done, att_done, own = pt.sem("pv_done"), pt.sem("att_done"), pt.sem("own")
            raw_copied, end_done, end_copied, added = (
                pt.sem("raw_copied"), pt.sem("end_done"), pt.sem("end_copied"), pt.sem("added"))
            SCALE = DH ** -0.5
            LOADS = 10
            HALF = KEYS // 2
            with nc.Block() as block:

                @block.sync
                def _(sp):
                    sp.wait_ge(zeroed, 5)
                    for m, dst in enumerate((wq, wk, wv)):
                        sp.dma_start(dst[0:HID, :, 0:DH], qkv_t[:, 0, HID * m:HID * m + HID].rearrange("p (h c) -> p h c", h=HEADS)).then_inc(loaded, 16)
                        sp.dma_start(dst[HID:, :, 0:DH], qkv_b[HID * m:HID * m + HID].rearrange("(a h c) -> a h c", a=1, h=HEADS)).then_inc(loaded, 16)
                    sp.dma_start(wp[0:HID, :], proj_t.rearrange("p a n -> p (a n)")).then_inc(loaded, 16)
                    sp.dma_start(wp[HID:, :], proj_b.rearrange("(a n) -> a n", a=1)).then_inc(loaded, 16)
                    sp.dma_start(w2[0:HID, :], fc2_t.rearrange("p a n -> p (a n)")).then_inc(loaded, 16)
                    sp.dma_start(w2[HID:, :], fc2_b.rearrange("(a n) -> a n", a=1)).then_inc(loaded, 16)
                    sp.wait_ge(loaded, 16 * LOADS)

                @block.gpsimd
                def _(pool):
                    for w in (wq, wk):
                        pool.memset(w[:, :, :].rearrange("p h c -> p (h c)"), 0.0).then_inc(zeroed, 1)
                    pool.memset(wv[:, :, :].rearrange("p h c -> p (h c)"), 0.0).then_inc(zeroed, 1)
                    pool.memset(k_diag[:, :, :, :].rearrange("p a h k -> p (a h k)"), 0.0).then_inc(zeroed, 1)
                    pool.wait_ge(zeroed, 4)
                    pool.memset(wv[HID:, :, DH:DH + 1], 1.0).then_inc(zeroed, 1)
                    pool.memset(att_t[HID:, :], 1.0).then_inc(zeroed, 1)
                    pool.memset(proj[HID:, :], 1.0).then_inc(zeroed, 1)

            with nc.Block() as block:

                def turns(eng, front, turn):
                    front(0, 0, 0)
                    turn(0, 0, 1, False, True)
                    with eng.Fori(0, TILES // 2 - 2) as it:
                        turn(it * 2 + 1, 1, 1, True, True)
                        turn(it * 2 + 2, 0, 1, True, True)
                    turn(TILES - 3, 1, 1, True, True)
                    turn(TILES - 2, 0, 2, True, True)
                    turn(TILES - 1, 1, None, True, False)

                @block.gpsimd
                def _(pool):
                    def window(j, half):
                        pool.tensor_copy(xw[:, half, :].rearrange("p (b c) -> p b c", b=NB), xs[:, :, bass.ds(j * COLS, SPAN)]).then_inc(xw_done, 1)

                    def subtract(j, half, variant):
                        pool.wait_ge(max_done, j + 1)
                        pool.wait_ge(exp_done, j)
                        pool.tensor_tensor(shifted[:, :, :], logits[:, :, :],
                                           high[:, :].unsqueeze(2).to_broadcast([P, HEADS, KEYS]), ALU.subtract).then_inc(shifted_done, 1)

                    def turn(j, half, variant, has_end, has_front):
                        if has_front:
                            if variant != 2:
                                pool.wait_ge(qkv_done, j + 1)
                                window(j + 2, half)
                            subtract(j + 1, 1 - half, variant)

                    def front(j, half, variant):
                        window(0, 0)
                        window(1, 1)
                        subtract(j, half, variant)

                    turns(pool, front, turn)

                @block.tensor
                def _(pe):
                    def project(j, half):
                        pe.wait_ge(xw_done, j + 1)
                        pe.wait_ge(qkv_copied, j * 4)
                        inner = xw[:, half, :].rearrange("p (b c) -> p b c", b=NB)[:, :, WIN // 2:WIN // 2 + COLS]
                        pe.matmul(qk_ps[:, 0:P], wq[:, :, :].rearrange("p h c -> p (h c)"), inner, start=True, stop=True)
                        pe.matmul(qk_ps[:, P:P + KEYS], wk[:, :, :].rearrange("p h c -> p (h c)"), xw[:, half, :], start=True, stop=True)
                        for m in range(2):
                            last = pe.matmul(v_ps[0:HALF, P * m:P * m + P], xw[:, half, HALF * m:HALF * m + HALF],
                                             wv[:, :, :].rearrange("p h c -> p (h c)"), start=True, stop=True)
                        last.then_inc(qkv_done, 1)

                    def scores(j, half):
                        pe.wait_ge(qkv_copied, j * 4 + 4)
                        pe.wait_ge(logits_read, j)
                        for m in range(2):
                            last = pe.matmul(logits_ps[:, m, 0:2 * KEYS], q_t[:, half, :],
                                             k_diag[:, half, 2 * m:2 * m + 2, :].rearrange("p h k -> p (h k)"), start=True, stop=True)
                        last.then_inc(logits_done, 1)

                    def front(j, half, variant):
                        project(j, half)
                        scores(j, half)

                    def turn(j, half, variant, has_end, has_front):
                        if has_end:
                            pe.wait_ge(raw_copied, j)
                            pe.transpose(att_ps[:, 1, :], raw[:, :], idn[:, :]).then_inc(end_done, 1)
                        if has_front:
                            project(j + 1, 1 - half)
                        pe.wait_ge(exp_done, j + 1)
                        for m in range(2):
                            pe.wait_ge(turned_copied, j * 2 + m)
                            for h in range(HEADS):
                                last = pe.transpose(turned_ps[:, m, P * h:P * h + P], probs[:, half, h, HALF * m:HALF * m + HALF], idn[:, :])
                            last.then_inc(turned_done, 1)
                        if has_end:
                            pe.wait_ge(att_done, j)
                            pe.transpose(att_ps[0:HID, 2, :], att[:, :, :].rearrange("p h c -> p (h c)"), idn[:, :]).then_inc(end_done, 1)
                        if has_front:
                            scores(j + 1, 1 - half)
                        if has_end:
                            pe.wait_ge(end_copied, j * 2 - 1)
                            pe.wait_ge(added, j - 1)
                            pe.matmul(out_ps[0:HID, 0:P], wp[:, :], att_t[:, :], start=True, stop=True).then_inc(end_done, 1)
                        pe.wait_ge(turned_copied, j * 2 + 2)
                        for m in range(2):
                            for h in range(HEADS):
                                last = pe.matmul(att_ps[PAD * h:PAD * h + PAD, 0, :], v[:, half, m, PAD * h:PAD * h + PAD],
                                                 probs_t[:, m, h, :], start=(m == 0), stop=(m == 1))
                        last.then_inc(pv_done, 1)
                        if has_end:
                            end(j)

                    def end(j):
                        pe.wait_ge(end_copied, j * 2)
                        pe.matmul(out_ps[:, P:P + D], proj[:, :], w2[:, :], start=True, stop=True).then_inc(end_done, 1)

                    turns(pe, front, turn)
                    j = TILES
                    pe.wait_ge(raw_copied, j)
                    pe.transpose(att_ps[:, 1, :], raw[:, :], idn[:, :]).then_inc(end_done, 1)
                    pe.wait_ge(att_done, j)
                    pe.transpose(att_ps[0:HID, 2, :], att[:, :, :].rearrange("p h c -> p (h c)"), idn[:, :]).then_inc(end_done, 1)
                    pe.wait_ge(end_copied, j * 2 - 1)
                    pe.wait_ge(added, j - 1)
                    pe.matmul(out_ps[0:HID, 0:P], wp[:, :], att_t[:, :], start=True, stop=True).then_inc(end_done, 1)
                    end(j)

                @block.scalar
                def _(act):
                    def copies(j, half):
                        act.wait_ge(qkv_done, j + 1)
                        act.activation(q_t[:, half, :], qk_ps[:, 0:P], ACT.Copy).then_inc(qkv_copied, 1)
                        for h in range(HEADS):
                            rows_h = slice(PAD * h, PAD * h + PAD)
                            ins = act.activation(k_diag[rows_h, half, h, :], qk_ps[rows_h, P:P + KEYS], ACT.Copy)
                            if h % 2:
                                ins.then_inc(qkv_copied, 1)
                        act.activation(v[:, half, :, :].rearrange("p m c -> p (m c)"), v_ps[0:HALF, 0:2 * P], ACT.Copy).then_inc(qkv_copied, 1)

                    def exponentials(j, half):
                        act.wait_ge(shifted_done, j + 1)
                        act.activation(probs[:, half, :, :], shifted[:, :, :], ACT.Exp).then_inc(exp_done, 1)

                    def front(j, half, variant):
                        copies(j, half)
                        exponentials(j, half)

                    def end(j):
                        act.wait_ge(end_done, j * 4 - 2)
                        act.activation(att_t[0:HID, :], att_ps[0:HID, 2, :], ACT.Copy).then_inc(end_copied, 1)
                        act.wait_ge(end_done, j * 4 - 1)
                        act.activation(proj[0:HID, :], out_ps[0:HID, 0:P], ACT.Copy).then_inc(end_copied, 1)

                    def turn(j, half, variant, has_end, has_front):
                        if has_front:
                            copies(j + 1, 1 - half)
                        for m in range(2):
                            act.wait_ge(turned_done, j * 2 + m + 1)
                            act.activation(probs_t[:, m, :, :].rearrange("p h q -> p (h q)"), turned_ps[:, m, :], ACT.Copy).then_inc(turned_copied, 1)
                        if has_end:
                            end(j)
                        act.wait_ge(pv_done, j + 1)
                        act.activation(raw[:, :], att_ps[:, 0, :], ACT.Copy).then_inc(raw_copied, 1)
                        if has_front:
                            exponentials(j + 1, 1 - half)

                    turns(act, front, turn)
                    end(TILES)

                @block.vector
                def _(dve):
                    def scores(j, half, variant):
                        dve.wait_ge(logits_done, j + 1)
                        dve.wait_ge(shifted_done, j)
                        dve.scalar_tensor_tensor(logits[:, :, :].rearrange("p (m h) k -> p m (h k)", m=2), logits_ps[:, :, 0:2 * KEYS], SCALE,
                                                 table[:, variant, :, :].rearrange("p (m h) k -> p m (h k)", m=2),
                                                 ALU.mult, ALU.add).then_inc(logits_read, 1)
                        dve.wait_ge(logits_read, j + 1)
                        dve.tensor_reduce(high[:, :], logits[:, :, :], AX.X, ALU.max).then_inc(max_done, 1)

                    def normalise(j):
                        dve.wait_ge(end_done, j * 4 - 3)
                        sums = att_ps[:, 1, :].rearrange("p (h c) -> p h c", h=HEADS)
                        dve.reciprocal(recip[:, :], sums[:, :, DH]).then_inc(own, 1)
                        dve.wait_ge(own, j)
                        dve.tensor_tensor(att[:, :, :], sums[:, :, 0:DH], recip[:, :].unsqueeze(2).to_broadcast([P, HEADS, DH]),
                                          ALU.mult).then_inc(att_done, 1)

                    def add(j):
                        dve.wait_ge(end_done, j * 4)
                        dst = H[:, bass.ds(j - 1, 1), :].rearrange("p t d -> p (t d)")
                        dve.tensor_tensor(dst, out_ps[:, P:P + D], dst, ALU.add).then_inc(added, 1)

                    def turn(j, half, variant, has_end, has_front):
                        if has_end:
                            normalise(j)
                        if has_front:
                            scores(j + 1, 1 - half, variant)
                        if has_end:
                            add(j)

                    turns(dve, scores, turn)
                    normalise(TILES)
                    add(TILES)

                @block.sync
                def _(sp):
                    sp.wait_ge(added, TILES)
                    for b in range(NB):
                        sp.dma_start(h2[SEQ * b:SEQ * b + SEQ, :].rearrange("(j w) d -> w j d", w=COLS),
                                     H[COLS * b:COLS * b + COLS, :, :]).then_inc(out_sem, 16)
                    sp.wait_ge(out_sem, 16 * NB)


def dense_stage(nc, H, idn, in_weight_t, in_bias, out_weight, mean, rstd, row_sems, turn_sems):
    hidden = in_bias.shape[0]
    with ExitStack() as stage:
        st = Store(nc, stage, "dense_ffn")
        xT = st.sb("xT", [C2, 2, TOKENS])
        bias = st.sb("bias", [P, hidden // P])
        row_statistics(nc, row_sems, 1, H, mean, rstd)
        turn_rows(nc, turn_sems, 1, H, mean, rstd, idn, xT)
        bias_in = st.sem("bias_in")
        with nc.Block() as block:

            @block.sync
            def _(sp):
                with nc.allow_non_contiguous_dma(reason="one bias per partition"):
                    sp.dma_start(bias[:, :], in_bias.rearrange("(m p) -> p m", p=P)).then_inc(bias_in, 16)
                sp.wait_ge(bias_in, 16)

        feed_forward(nc, "ffn", H, xT, 1, hidden, lambda e: in_weight_t,
                     lambda e: out_weight.rearrange("(m p) d -> p m d", p=P), ACT.Gelu, bias=bias)


def turned_weights(nc, weights, ident):
    steps, outs = [], []
    with ExitStack() as part:
        pt = Store(nc, part, "turn_weights")
        idn = pt.sb("idn", [P, P])
        for i, weight in enumerate(weights):
            rows, cols = weight.shape
            n = max(1, -(-cols // P))
            size = cols // n
            out = nc.dram_tensor(f"turned_weight{i}", (size, n, rows), F32).ap()
            tiles = [(r, min(P, rows - r)) for r in range(0, rows, P)]
            w = pt.sb(f"w{i}", [P, len(tiles), cols])
            wT = pt.sb(f"wT{i}", [size, n, rows])
            steps += [(w, wT, t, r, m, c, size) for t, (r, m) in enumerate(tiles) for c in range(n)]
            outs.append((weight, w, wT, out, tiles, len(steps)))
        ps = pt.ps("ps", [P, 2, SEQ])
        loaded, turned, copied, stored = pt.sem("loaded"), pt.sem("turned"), pt.sem("copied"), pt.sem("stored")
        loads = 1 + sum(len(tiles) for *_, tiles, _ in outs)
        with nc.Block() as block:

            @block.sync
            def _(sp):
                sp.dma_start(idn[:, :], ident).then_inc(loaded, 16)
                for weight, w, _, _, tiles, _ in outs:
                    for t, (r, m) in enumerate(tiles):
                        sp.dma_start(w[0:m, t, :], weight[r:r + m, :]).then_inc(loaded, 16)
                for _, _, wT, out, _, end in outs:
                    sp.wait_ge(copied, end)
                    sp.dma_start(out, wT[:, :, :]).then_inc(stored, 16)
                sp.wait_ge(stored, 16 * len(outs))

            @block.tensor
            def _(pe):
                pe.wait_ge(loaded, 16 * loads)
                for j, (w, _, t, _, m, c, size) in enumerate(steps):
                    if j >= 2:
                        pe.wait_ge(copied, j - 1)
                    pe.transpose(ps[0:size, j % 2, 0:m], w[0:m, t, size * c:size * c + size], idn[0:m, 0:m]).then_inc(turned, 1)

            @block.vector
            def _(dve):
                for j, (_, wT, _, r, m, c, size) in enumerate(steps):
                    dve.wait_ge(turned, j + 1)
                    dve.tensor_copy(wT[:, c, r:r + m], ps[0:size, j % 2, 0:m]).then_inc(copied, 1)
    return [out for _, _, _, out, _, _ in outs]


SETS = 64


def sets_stage(nc, H, idn, wqkv_t, wproj_t, wv_t, bv, const, mean, rstd, row_sems):
    HH = HD * HD
    SCALE = 0.25
    assert SCALE == HD ** -0.5
    BATCHES = NH // 2
    X, QT, OUT, OT, PT, VT, TURN = 0, 1, 2, (3, 4, 5, 6, 7, 8), (9, 10), 11, 12
    KSUM, VSUM = TT * TURN, TT * TURN + 1
    PER_SEQ = TT * TURN + 2
    DVE_BATCHES = 4
    with ExitStack() as stage:
        st = Store(nc, stage, "sets")
        wqkv = st.sb("wqkv", [C2, 2, 3 * D])
        wproj = st.sb("wproj", [C2, 2, D])
        wv = st.sb("wv", [P, 2, PAD])
        bias = st.sb("bias", [P, 1])
        setm = st.sb("setm", [P, TT, P])
        tri = st.sb("tri", [P, P])
        mask = st.sb("mask", [P, TT, SETS])
        rows = st.sb("rows", [P, 2, D])
        xs = st.sb("xs", [C2, 2, 2, P])
        qk = st.sb("qk", [P, 2, TT, 2, NH, PAD])
        v0 = st.sb("v0", [P, 2, NH, HD])
        v = st.sb("v", [P, 2, TT, NH, PAD])
        v_t = st.sb("v_t", [P, NG, P])
        outer = st.sb("outer", [P, 2, NH, HH])
        outer_t = st.sb("outer_t", [P, 2, 2 * NH, P])
        k_diag = st.sb("k_diag", [P, 2, NG, GH * SETS])
        v_diag = st.sb("v_diag", [P, 2, NH // 2, 2, HD + 1])
        q_t = st.sb("q_t", [P, 2, NG, P])
        logits = st.sb("logits", [P, NH, SETS])
        shifted = st.sb("shifted", [P, NH, SETS])
        probs = st.sb("probs", [P, 2, NH, SETS])
        probs_t = st.sb("probs_t", [P, NH // 2, P])
        q_tail = st.sb("q_tail", [P, NH, HD])
        tail = st.sb("tail", [P, NH])
        high = st.sb("high", [P, NH])
        recip = st.sb("recip", [P, NH])
        out = st.sb("out", [P, NH, HD])
        out_n = st.sb("out_n", [P, NH, HD])
        out_t = st.sb("out_t", [C2, 2, P])
        row_statistics(nc, row_sems, 2, H, mean, rstd)
        logits_ps = st.ps("logits_ps", [P, 2, SEQ])
        tails_ps = st.ps("tails_ps", [P, SEQ])
        qk_ps = st.ps("qk_ps", [P, SEQ])
        v0_ps = logits_ps[:, 1, 256:256 + D]
        v_ps = st.ps("v_ps", [P, 4, P])[:, 0:NG, :]
        ring = st.ps("ring", [P, 2, SEQ])
        out_ps = st.ps("out_ps", [P, 2, SEQ // 2])
        loaded, zeroed = st.sem("loaded"), st.sem("zeroed")
        rows_done, ring_done, ring_copied = st.sem("rows_done"), st.sem("ring_done"), st.sem("ring_copied")
        qkv_done, qkv_copied = st.sem("qkv_done"), st.sem("qkv_copied")
        outer_done = {"dve": st.sem("outer_dve"), "pool": st.sem("outer_pool")}
        v_done, v_turned = st.sem("v_done"), st.sem("v_turned")
        tails_done, logits_done, logits_read = st.sem("tails_done"), st.sem("logits_done"), st.sem("logits_read")
        max_done, shifted_done, exp_done = st.sem("max_done"), st.sem("shifted_done"), st.sem("exp_done")
        pv_done, combined, proj_done, added = (
            st.sem("pv_done"), st.sem("combined"), st.sem("proj_done"), st.sem("added"))
        own, tail_steps = st.sem("own"), st.sem("tail_steps")

        with nc.Block() as block:

            @block.sync
            def _(sp):
                sp.dma_start(wqkv[:, :, :], wqkv_t).then_inc(loaded, 16)
                sp.dma_start(wproj[:, :, :], wproj_t).then_inc(loaded, 16)
                sp.wait_ge(zeroed, 7)
                sp.dma_start(wv[:, :, 0:HD], wv_t).then_inc(loaded, 16)
                for j in range(GH):
                    sp.dma_start(bias[PAD * j:PAD * j + HD, :], bv.rearrange("(e a) -> e a", a=1)).then_inc(loaded, 16)
                sp.dma_start(setm[:, :, :], const["sets"].rearrange("(q p) s -> p q s", p=P)).then_inc(loaded, 16)
                sp.dma_start(tri[:, :], const["tail_sums"]).then_inc(loaded, 16)
                sp.dma_start(mask[:, :, :], const["sets_mask"].rearrange("(q p) s -> p q s", p=P)).then_inc(loaded, 16)
                sp.wait_ge(loaded, 16 * (6 + GH))

            @block.gpsimd
            def _(pool):
                pool.memset(qk[:, :, :, :, :, :].rearrange("p a q m h c -> p (a q m h c)"), 0.0).then_inc(zeroed, 1)
                pool.memset(k_diag[:, :, :, :].rearrange("p a g s -> p (a g s)"), 0.0).then_inc(zeroed, 1)
                pool.memset(v_diag[:, :, :, :, :].rearrange("p a h m c -> p (a h m c)"), 0.0).then_inc(zeroed, 1)
                pool.wait_ge(zeroed, 3)
                pool.memset(v_diag[0:SETS, :, :, 0, HD:], 1.0).then_inc(zeroed, 1)
                pool.memset(v_diag[SETS:P, :, :, 1, HD:], 1.0).then_inc(zeroed, 1)
                pool.wait_ge(zeroed, 5)
                pool.memset(wv[:, :, :].rearrange("p m c -> p (m c)"), 0.0).then_inc(zeroed, 1)
                pool.memset(bias[:, :], 0.0).then_inc(zeroed, 1)

        def at(s, q, use):
            return s * PER_SEQ + (TURN + q * TURN + use)

        def bank(use):
            return ring[:, use % 2, :]

        def present(s, q, use):
            t1 = s * TT + q
            if use == X:
                return t1 < TILES - 1
            if use in (QT, *PT):
                return TT <= t1 < TILES + TT
            if use == OUT:
                return t1 > TT
            if use in (KSUM, VSUM):
                return s < NB
            return t1 < TILES

        ORDER = [at(0, 0, X) - TURN]
        for s in range(NB + 2):
            for q in range(TT if s <= NB else 1):
                ORDER += [at(s, q, use) for use in range(TURN) if present(s, q, use)]
            if s < NB:
                ORDER += [at(s, 0, KSUM), at(s, 0, VSUM)]
        NEXT = dict(zip(ORDER, ORDER[1:] + [ORDER[-1] + 1]))

        def counted(number):
            return NEXT[number] - number if isinstance(number, int) else 1

        with nc.Block() as block:

            def steps(eng, turn, sums):
                def one(s, par, q, fixed=None):
                    t1 = fixed * TT + q if fixed is not None else None
                    if t1 is None:
                        turn(s, par, q, True, True, True, True)
                    else:
                        turn(s, par, q, t1 < TILES - 1, t1 < TILES, TT <= t1 < TILES + TT, t1 > TT)

                for s in (0, 1):
                    for q in range(TT):
                        one(s, s % 2, q, s)
                    sums(s, s % 2)
                with eng.Fori(0, (NB - 4) // 2) as it:
                    for par in range(2):
                        for q in range(TT):
                            one(it * 2 + (2 + par), par, q)
                        sums(it * 2 + (2 + par), par)
                for s in (NB - 2, NB - 1):
                    for q in range(TT):
                        one(s, s % 2, q, s)
                    sums(s, s % 2)
                for q in range(TT):
                    one(NB, 0, q, NB)
                one(NB + 1, 1, 0, NB + 1)

            @block.tensor
            def _(pe):
                def claim(number):
                    if not (isinstance(number, int) and number <= at(0, 0, X)):
                        pe.wait_ge(ring_copied, number - 1)

                def rows_turned(number, at_q, T):
                    pe.wait_ge(rows_done, T + 1)
                    claim(number)
                    for c in range(2):
                        last = pe.transpose(bank(X)[0:C2, P * c:P * c + P], rows[:, at_q, C2 * c:C2 * c + C2], idn[:, :])
                    last.then_inc(ring_done, counted(number))

                def projections(number, at_q, T):
                    pe.wait_ge(ring_copied, number + 1)
                    pe.wait_ge(qkv_copied, T * 2)
                    for c in range(2):
                        pe.matmul(qk_ps[:, 0:2 * D], xs[:, at_q, c, :], wqkv[:, c, 0:2 * D], start=(c == 0), stop=(c == 1))
                    for c in range(2):
                        last = pe.matmul(v0_ps, xs[:, at_q, c, :], wqkv[:, c, 2 * D:], start=(c == 0), stop=(c == 1))
                    last.then_inc(qkv_done, 1)

                def batch(s, q, T1, k):
                    number = at(s, q, OT[k])
                    claim(number)
                    pe.wait_ge(outer_done["dve" if k < DVE_BATCHES else "pool"], T1 + 1)
                    for m in range(4):
                        last = pe.transpose(bank(OT[k])[:, P * m:P * m + P],
                                            outer[:, q % 2, 2 * k + m // 2, P * (m % 2):P * (m % 2) + P], idn[:, :])
                    last.then_inc(ring_done, counted(number))

                def value(s, q, T1, k):
                    pe.wait_ge(ring_copied, at(s, q, OT[k]) + 1)
                    if k == 0:
                        pe.wait_ge(v_turned, T1)
                    for m in range(2):
                        for h in (2 * k, 2 * k + 1):
                            j, g = PAD * (h % GH), h // GH
                            last = pe.matmul(v_ps[j:j + PAD, g, :], wv[:, m, :], outer_t[:, q % 2, 2 * h + m, :],
                                             start=(m == 0), stop=(m == 1))
                    if k == BATCHES - 1:
                        last.then_inc(v_done, 1)

                def turn(s, par, q, following, values, scores, end):
                    T1 = s * TT + q
                    T2 = T1 - TT
                    if following:
                        rows_turned(at(s, q, X), 1 - q % 2, T1 + 1)
                    if scores:
                        claim(at(s, q, QT))
                        for g in range(NG):
                            last = pe.transpose(bank(QT)[:, P * g:P * g + P],
                                                qk[:, 1 - par, q, 0, GH * g:GH * g + GH, :].rearrange("p h c -> p (h c)"), idn[:, :])
                        last.then_inc(ring_done, counted(at(s, q, QT)))
                    if following:
                        if scores:
                            pe.wait_ge(logits_read, T2)
                        projections(at(s, q, X), 1 - q % 2, T1 + 1)
                    if end:
                        pe.wait_ge(combined, T2)
                        claim(at(s, q, OUT))
                        for c in range(2):
                            last = pe.transpose(bank(OUT)[0:C2, P * c:P * c + P],
                                                out_n[:, :, :].rearrange("p h c -> p (h c)")[:, C2 * c:C2 * c + C2], idn[:, :])
                        last.then_inc(ring_done, counted(at(s, q, OUT)))
                    if scores:
                        pe.matmul(tails_ps[:, 0:D], tri[:, :], qk[:, 1 - par, q, 1, :, 0:HD], start=True, stop=True)
                        pe.matmul(tails_ps[:, D:2 * D], tri[:, :], v[:, 1 - par, q, :, 0:HD], start=True, stop=True).then_inc(tails_done, 1)
                        pe.wait_ge(ring_copied, at(s, q, QT) + 1)
                        pe.wait_ge(logits_read, T2)
                        if following:
                            pe.wait_ge(qkv_copied, T1 * 2 + 4)
                        for g in range(NG):
                            last = pe.matmul(logits_ps[:, g // 2, 256 * (g % 2):256 * (g % 2) + 256], q_t[:, q % 2, g, :],
                                             k_diag[:, 1 - par, g, :], start=True, stop=True)
                        last.then_inc(logits_done, 1)
                    if values:
                        batch(s, q, T1, 0)
                        for k in range(1, BATCHES):
                            batch(s, q, T1, k)
                            value(s, q, T1, k - 1)
                    if end:
                        pe.wait_ge(ring_copied, at(s, q, OUT) + 1)
                        for c in range(2):
                            last = pe.matmul(out_ps[:, 1, 0:D], out_t[:, c, :], wproj[:, c, :], start=(c == 0), stop=(c == 1))
                        last.then_inc(proj_done, 1)
                    if values:
                        value(s, q, T1, BATCHES - 1)
                    if scores:
                        pe.wait_ge(exp_done, T2 + 1)
                        for k in range(2):
                            claim(at(s, q, PT[k]))
                            for m in range(3):
                                h = 2 * (3 * k + m)
                                last = pe.transpose(bank(PT[k])[:, P * m:P * m + P],
                                                    probs[:, q % 2, h:h + 2, :].rearrange("p h s -> p (h s)"), idn[:, :])
                            last.then_inc(ring_done, counted(at(s, q, PT[k])))
                    if values:
                        pe.wait_ge(v_turned, T1 + 1)
                        claim(at(s, q, VT))
                        for g in range(NG):
                            last = pe.transpose(bank(VT)[:, P * g:P * g + P], v_t[:, g, :], idn[:, :])
                        last.then_inc(ring_done, counted(at(s, q, VT)))
                    if scores:
                        pe.wait_ge(ring_copied, at(s, q, PT[1]) + 1)
                        pe.wait_ge(added, T2)
                        for m in range(NH // 2):
                            last = pe.matmul(out_ps[:, 0, 34 * m:34 * m + 34], probs_t[:, m, :],
                                             v_diag[:, 1 - par, m, :, :].rearrange("p h c -> p (h c)"), start=True, stop=True)
                        last.then_inc(pv_done, 1)

                def sums(s, par):
                    claim(at(s, 0, KSUM))
                    for g in range(NG):
                        for q in range(TT):
                            last = pe.matmul(bank(KSUM)[:, SETS * g:SETS * g + SETS],
                                             qk[:, par, q, 1, GH * g:GH * g + GH, :].rearrange("p h c -> p (h c)"),
                                             setm[:, q, 0:SETS], start=(q == 0), stop=(q == TT - 1))
                    last.then_inc(ring_done, counted(at(s, 0, KSUM)))
                    pe.wait_ge(ring_copied, at(s, TT - 1, VT) + 1)
                    claim(at(s, 0, VSUM))
                    for q in range(TT):
                        last = pe.matmul(bank(VSUM)[:, 0:D], setm[:, q, :], v[:, par, q, :, 0:HD], start=(q == 0), stop=(q == TT - 1))
                    last.then_inc(ring_done, counted(at(s, 0, VSUM)))

                rows_turned(at(0, 0, X) - TURN, 0, 0)
                projections(at(0, 0, X) - TURN, 0, 0)
                steps(pe, turn, sums)

            @block.scalar
            def _(act):
                def copy(number, dst, src):
                    act.wait_ge(ring_done, number + 1)
                    act.activation(dst, src, ACT.Copy).then_inc(ring_copied, counted(number))

                def rows_copied(number, at_q):
                    copy(number, xs[:, at_q, :, :].rearrange("p c t -> p (c t)"), bank(X)[0:C2, 0:2 * P])

                def qkv(par, q, T):
                    act.wait_ge(qkv_done, T + 1)
                    act.activation(qk[:, par, q, :, :, 0:HD].rearrange("p m h c -> p (m h) c"),
                                   qk_ps[:, 0:2 * D].rearrange("p (m c) -> p m c", c=HD), ACT.Copy).then_inc(qkv_copied, 1)
                    act.activation(v0[:, q % 2, :, :].rearrange("p h c -> p (h c)"), v0_ps, ACT.Copy).then_inc(qkv_copied, 1)

                def turn(s, par, q, following, values, scores, end):
                    T1 = s * TT + q
                    T2 = T1 - TT
                    if following:
                        act.wait_ge(qkv_done, T1)
                        rows_copied(at(s, q, X), 1 - q % 2)
                    if scores:
                        act.wait_ge(logits_done, T2)
                        copy(at(s, q, QT), q_t[:, q % 2, :, :].rearrange("p g t -> p (g t)"), bank(QT)[:, 0:NG * P])
                    if following:
                        if q < TT - 1:
                            qkv(par, q + 1, T1 + 1)
                        else:
                            qkv(1 - par, 0, T1 + 1)
                    if end:
                        act.wait_ge(proj_done, T2 - 1)
                        copy(at(s, q, OUT), out_t[:, :, :].rearrange("p c t -> p (c t)"), bank(OUT)[0:C2, 0:2 * P])
                    if values:
                        act.wait_ge(v_done, T1)
                        for k in range(BATCHES):
                            copy(at(s, q, OT[k]), outer_t[:, q % 2, 4 * k:4 * k + 4, :].rearrange("p m t -> p (m t)"), bank(OT[k]))
                    if scores:
                        act.wait_ge(shifted_done, T2 + 1)
                        act.activation(probs[:, q % 2, :, :], shifted[:, :, :], ACT.Exp).then_inc(exp_done, 1)
                    if values:
                        act.wait_ge(v_done, T1 + 1)
                        act.activation(v_t[:, :, :], v_ps[:, :, :], ACT.Identity, bias=bias[:, :]).then_inc(v_turned, 1)
                    if scores:
                        act.wait_ge(pv_done, T2)
                        for k in range(2):
                            copy(at(s, q, PT[k]), probs_t[:, 3 * k:3 * k + 3, :].rearrange("p m t -> p (m t)"), bank(PT[k])[:, 0:3 * P])
                    if values:
                        copy(at(s, q, VT), v[:, par, q, :, :].rearrange("p h c -> p (h c)"), bank(VT)[:, 0:NG * P])

                def sums(s, par):
                    act.wait_ge(ring_done, at(s, 0, KSUM) + 1)
                    for j in range(GH):
                        rows_j = slice(PAD * j, PAD * j + PAD)
                        ins = act.activation(k_diag[rows_j, par, :, SETS * j:SETS * j + SETS],
                                             bank(KSUM)[rows_j, 0:NG * SETS].rearrange("p (g s) -> p g s", g=NG), ACT.Copy)
                    ins.then_inc(ring_copied, counted(at(s, 0, KSUM)))
                    act.wait_ge(ring_done, at(s, 0, VSUM) + 1)
                    for m in range(2):
                        rows_m = slice(SETS * m, SETS * m + SETS)
                        ins = act.activation(v_diag[rows_m, par, :, m, 0:HD],
                                             bank(VSUM)[rows_m, 0:D].rearrange("p (h m c) -> p h m c", m=2, c=HD)[:, :, m, :], ACT.Copy)
                    ins.then_inc(ring_copied, counted(at(s, 0, VSUM)))

                rows_copied(at(0, 0, X) - TURN, 0)
                qkv(0, 0, 0)
                steps(act, turn, sums)

            def products(eng, which, par, q, T, heads):
                n = heads.stop - heads.start
                eng.wait_ge(qkv_copied, T * 2 + 2)
                if not (isinstance(T, int) and T < 2):
                    eng.wait_ge(v_done, T - 1)
                k = qk[:, par, q, 1, heads, 0:HD].unsqueeze(3).to_broadcast([P, n, HD, HD])
                w = v0[:, q % 2, heads, :].unsqueeze(2).to_broadcast([P, n, HD, HD])
                eng.tensor_tensor(outer[:, q % 2, heads, :].rearrange("p h (i j) -> p h i j", i=HD), k, w,
                                  ALU.mult).then_inc(outer_done[which], 1)

            def next_products(eng, which, par, q, T1, heads):
                if q < TT - 1:
                    products(eng, which, par, q + 1, T1 + 1, heads)
                else:
                    products(eng, which, 1 - par, 0, T1 + 1, heads)

            @block.gpsimd
            def _(pool):
                heads = slice(2 * DVE_BATCHES, NH)

                def turn(s, par, q, following, values, scores, end):
                    T2 = s * TT + (q - TT)
                    if scores:
                        pool.wait_ge(max_done, T2 + 1)
                        pool.wait_ge(exp_done, T2)
                        pool.tensor_tensor(shifted[:, :, :], logits[:, :, :],
                                           high[:, :].unsqueeze(2).to_broadcast([P, NH, SETS]), ALU.subtract).then_inc(shifted_done, 1)
                    if following:
                        next_products(pool, "pool", par, q, s * TT + q, heads)

                products(pool, "pool", 0, 0, 0, heads)
                steps(pool, turn, lambda s, par: None)

            @block.vector
            def _(dve):
                heads = slice(0, 2 * DVE_BATCHES)

                def rows_of(T, at_q):
                    if not (isinstance(T, int) and T < 2):
                        dve.wait_ge(qkv_done, T - 1)
                    t = bass.ds(T, 1)
                    dve.tensor_scalar(rows[:, at_q, :], H[:, t, :].rearrange("p t d -> p (t d)"),
                                      mean[:, t], rstd[:, t], ALU.subtract, ALU.mult).then_inc(rows_done, 1)

                def combine(T, at_q):
                    dve.wait_ge(pv_done, T + 1)
                    pv = out_ps[:, 0, 0:NH * (HD + 1)].rearrange("p (h c) -> p h c", h=NH)
                    dve.reciprocal(recip[:, :], pv[:, :, HD]).then_inc(own, 1)
                    dve.tensor_tensor(out[:, :, :], tails_ps[:, D:2 * D].rearrange("p (h c) -> p h c", h=NH),
                                      probs[:, at_q, :, SETS - 1:].to_broadcast([P, NH, HD]), ALU.mult).then_inc(own, 1)
                    dve.wait_ge(own, T * 3 + 2)
                    dve.tensor_tensor(out[:, :, :], out[:, :, :], pv[:, :, 0:HD], ALU.add).then_inc(own, 1)
                    dve.wait_ge(own, T * 3 + 3)
                    dve.tensor_tensor(out_n[:, :, :], out[:, :, :], recip[:, :].unsqueeze(2).to_broadcast([P, NH, HD]),
                                      ALU.mult).then_inc(combined, 1)

                def turn(s, par, q, following, values, scores, end):
                    T1 = s * TT + q
                    T2 = T1 - TT
                    if end:
                        combine(T2 - 1, 1 - q % 2)
                    if scores:
                        dve.wait_ge(tails_done, T2 + 1)
                        dve.tensor_tensor(q_tail[:, :, :], qk[:, 1 - par, q, 0, :, 0:HD],
                                          tails_ps[:, 0:D].rearrange("p (h c) -> p h c", h=NH), ALU.mult).then_inc(tail_steps, 1)
                        dve.wait_ge(tail_steps, T2 * 3 + 1)
                        dve.tensor_reduce(tail[:, :], q_tail[:, :, :], AX.X, ALU.add).then_inc(tail_steps, 1)
                        dve.wait_ge(logits_done, T2 + 1)
                        dve.wait_ge(shifted_done, T2)
                        dve.scalar_tensor_tensor(logits[:, :, :],
                                                 logits_ps[:, :, :].rearrange("p b s -> p (b s)")[:, 0:NH * SETS].rearrange("p (h s) -> p h s", h=NH),
                                                 SCALE, mask[:, q, :].unsqueeze(1).to_broadcast([P, NH, SETS]),
                                                 ALU.mult, ALU.add).then_inc(logits_read, 1)
                        dve.wait_ge(logits_read, T2 + 1)
                        dve.wait_ge(tail_steps, T2 * 3 + 2)
                        dve.tensor_scalar(logits[:, :, SETS - 1], tail[:, :], SCALE, None, ALU.mult).then_inc(tail_steps, 1)
                        dve.wait_ge(tail_steps, T2 * 3 + 3)
                        dve.tensor_reduce(high[:, :], logits[:, :, :], AX.X, ALU.max).then_inc(max_done, 1)
                    if following:
                        next_products(dve, "dve", par, q, T1, heads)
                        if not (isinstance(T1, int) and T1 + 2 >= TILES):
                            rows_of(T1 + 2, q % 2)
                    if end:
                        dve.wait_ge(proj_done, T2)
                        dst = H[:, bass.ds(T2 - 1, 1), :].rearrange("p t d -> p (t d)")
                        dve.tensor_tensor(dst, out_ps[:, 1, 0:D], dst, ALU.add).then_inc(added, 1)

                rows_of(0, 0)
                products(dve, "dve", 0, 0, 0, heads)
                rows_of(1, 1)
                steps(dve, turn, lambda s, par: None)


def experts_stage(nc, H, idn, gamma, beta, router_w, w1, w2, mean, rstd, row_sems, turn_sems):
    E, hidden = w1.shape[0], w1.shape[2]
    with ExitStack() as stage:
        st = Store(nc, stage, "experts")
        xT = st.sb("xT", [C2, 2, TOKENS])
        gates = st.sb("gates", [P, TILES * E])
        gamma_beta = st.sb("gamma_beta", [C2, 2, 2])
        router = st.sb("router", [C2, 2, E])
        row_statistics(nc, row_sems, 3, H, mean, rstd)
        with ExitStack() as part:
            X = Store(nc, part, "moe").sb("X", [P, TILES, D])
            normalise_rows(nc, "moe_norm", H, mean, rstd, X)
            row_statistics(nc, row_sems, 4, X, mean, rstd)
            small_in = st.sem("small_in")
            with nc.Block() as block:

                @block.sync
                def _(sp):
                    with nc.allow_non_contiguous_dma(reason="one value per partition"):
                        sp.dma_start(gamma_beta[:, :, 0], gamma.rearrange("(c p) -> p c", c=2)).then_inc(small_in, 16)
                        sp.dma_start(gamma_beta[:, :, 1], beta.rearrange("(c p) -> p c", c=2)).then_inc(small_in, 16)
                    sp.dma_start(router[:, :, :], router_w.rearrange("(c p) e -> p c e", c=2)).then_inc(small_in, 16)
                    sp.wait_ge(small_in, 48)

            turn_rows(nc, turn_sems, 2, X, mean, rstd, idn, xT, gamma_beta=gamma_beta)
        route(nc, xT, router, idn, gates, E)
        feed_forward(nc, "moe_ffn", H, xT, E, hidden,
                     lambda e: w1[bass.ds(e, 1), :, :].rearrange("e (c p) f -> p (e c) f", c=2),
                     lambda e: w2[bass.ds(e, 1), :, :].rearrange("e (m p) d -> p (e m) d", p=P), ACT.Silu, gates=gates)


def route(nc, xT, router, idn, gates, E):
    with ExitStack() as part:
        pt = Store(nc, part, "route")
        logits_t = pt.sb("logits_t", [E, 2, SEQ])
        full = [P, TILES, E]
        probs = pt.sb("probs", full)
        left = pt.sb("left", full)
        equal = pt.sb("equal", full)
        first_mask = pt.sb("first_mask", full)
        number = pt.sb("number", full)
        number_i = pt.sb("number_i", full, I32)
        high = pt.sb("high", [P, TILES])
        top1 = pt.sb("top1", [P, TILES])
        index = pt.sb("index", [P, TILES])
        product = pt.ps("product", [E, 2, SEQ])
        turned = pt.ps("turned", [P, 2, SEQ])
        product_done, copied, turned_done, placed, numbered = (
            pt.sem("product_done"), pt.sem("copied"), pt.sem("turned_done"), pt.sem("placed"), pt.sem("numbered"))
        turn_begun = pt.sem("turn_begun")
        own, exp_ready, exp_done = pt.sem("own"), pt.sem("exp_ready"), pt.sem("exp_done")
        g3 = gates[:, :].rearrange("p (t e) -> p t e", e=E)

        def wide(x):
            return x[:, :].unsqueeze(2).to_broadcast(full)

        with nc.Block() as block:

            @block.gpsimd
            def _(pool):
                pool.iota(number_i[:, :, :], pattern=[[0, TILES], [1, E]], base=0, channel_multiplier=0).then_inc(numbered, 1)

            @block.tensor
            def _(pe):
                pe.sem_inc(turned_done, 1)
                with pe.Fori(0, GROUPS // 2) as it:
                    for half in range(2):
                        g = it * 2 + half
                        pe.wait_ge(copied, g)
                        for k in range(2):
                            last = pe.matmul(product[:, half, :], router[:, k, :], xT[:, k, bass.ds(g * SEQ, SEQ)],
                                             start=(k == 0), stop=(k == 1))
                        last.then_inc(product_done, 1)
                        pe.wait_ge(copied, g + 2)
                        pe.wait_ge(placed, g)
                        pe.sem_inc(turn_begun, 1)
                        for k in range(TT):
                            last = pe.transpose(turned[:, half, E * k:E * k + E], logits_t[:, half, P * k:P * k + P], idn[0:E, 0:E])
                        last.then_inc(turned_done, 1)

            @block.scalar
            def _(act):
                act.sem_inc(copied, 1)
                with act.Fori(0, GROUPS // 2) as it:
                    for half in range(2):
                        g = it * 2 + half
                        act.wait_ge(product_done, g + 1)
                        act.wait_ge(turned_done, g)
                        act.activation(logits_t[:, half, :], product[:, half, :], ACT.Copy).then_inc(copied, 1)
                act.wait_ge(exp_ready, 1)
                act.activation(equal[:, :, :], left[:, :, :], ACT.Exp).then_inc(exp_done, 1)

            @block.vector
            def _(dve):
                dve.sem_inc(placed, 1)
                with dve.Fori(0, GROUPS // 2) as it:
                    for half in range(2):
                        g = it * 2 + half
                        dve.wait_ge(turned_done, g + 2)
                        dve.tensor_copy(probs[:, bass.ds(g * TT, TT), :].rearrange("p t e -> p (t e)"),
                                        turned[:, half, 0:TT * E]).then_inc(placed, 1)
                dve.wait_ge(placed, GROUPS + 1)
                chain = Chain(dve, own)
                chain(dve.tensor_reduce(high[:, :], probs[:, :, :], AX.X, ALU.max))
                chain.wait()
                dve.tensor_tensor(left[:, :, :], probs[:, :, :], wide(high), ALU.subtract).then_inc(exp_ready, 1)
                dve.wait_ge(exp_done, 1)
                chain(dve.tensor_reduce(high[:, :], equal[:, :, :], AX.X, ALU.add))
                chain.wait()
                chain(dve.reciprocal(index[:, :], high[:, :]))
                chain.wait()
                chain(dve.tensor_tensor(probs[:, :, :], equal[:, :, :], wide(index), ALU.mult))
                dve.wait_ge(numbered, 1)
                chain(dve.tensor_copy(number[:, :, :], number_i[:, :, :]))
                chain.wait()

                def first_largest(values, top, mask):
                    chain(dve.tensor_reduce(top[:, :], values[:, :, :], AX.X, ALU.max))
                    chain.wait()
                    chain(dve.tensor_tensor(equal[:, :, :], values[:, :, :], wide(top), ALU.not_equal))
                    chain.wait()
                    chain(dve.scalar_tensor_tensor(equal[:, :, :], equal[:, :, :], float(E), number[:, :, :], ALU.mult, ALU.add))
                    chain.wait()
                    chain(dve.tensor_reduce(index[:, :], equal[:, :, :], AX.X, ALU.min))
                    chain.wait()
                    chain(dve.tensor_tensor(mask, number[:, :, :], wide(index), ALU.is_equal))
                    chain.wait()

                first_largest(probs, top1, first_mask[:, :, :])
                chain(dve.scalar_tensor_tensor(left[:, :, :], first_mask[:, :, :], -2.0, probs[:, :, :], ALU.mult, ALU.add))
                chain.wait()
                first_largest(left, high, g3)
                chain(dve.tensor_tensor(top1[:, :], top1[:, :], high[:, :], ALU.add))
                chain(dve.tensor_tensor(g3, g3, first_mask[:, :, :], ALU.add))
                chain.wait()
                chain(dve.reciprocal(top1[:, :], top1[:, :]))
                chain(dve.tensor_tensor(g3, g3, probs[:, :, :], ALU.mult))
                chain.wait()
                chain(dve.tensor_tensor(g3, g3, wide(top1), ALU.mult))


def constants():
    p, i = np.meshgrid(np.arange(SEQ), np.arange(D // 2))
    pos = np.zeros((SEQ, D), dtype=np.float32)
    pos[:, ::2] = np.sin(p / 2500 ** (2 * i / D)).T
    pos[:, 1::2] = np.cos(p / 2500 ** (2 * i / D)).T
    wv = np.zeros((P, NH, PAD), np.float32)
    wv[HD, :, HD:] = 1.0
    affine = np.zeros((P, NG, 4), np.float32)
    affine[HD, :, 1] = affine[HD, :, 3] = 1.0
    t = np.arange(SEQ)
    spans = [(i, i + size - 1) for size in (16 << n for n in range(6)) for i in range(0, SEQ, size)]
    sets = np.zeros((SEQ, 2, SETS), np.float32)
    sets_mask = np.zeros((SEQ, SETS), np.float32)
    for n, (first, last) in enumerate(spans):
        sets[first:last + 1, :, n] = 1.0
        sets_mask[:, n] = np.where(t >= last, 0.0, NEG)
    near_mask = np.full((NB, COLS, 3, NB, SPAN), NEG, np.float32)
    for v, column0 in enumerate((0, COLS, SEQ - COLS)):
        for b in range(NB):
            for w in range(COLS):
                top = min(max(b - WIN // 2, 0), NB - WIN)
                left = min(max(column0 + w - WIN // 2, 0), SEQ - WIN) - (column0 - WIN // 2)
                near_mask[b, w, v, top:top + WIN, left:left + WIN] = 0.0
    r = np.arange(P)
    tail_sums = ((r[:, None] // 16 == r[None, :] // 16) & (r[:, None] <= r[None, :])).astype(np.float32)
    return {
        "near_mask": near_mask.reshape(P, 3 * KEYS),
        "sets": sets.reshape(SEQ, 2 * SETS),
        "sets_mask": sets_mask,
        "tail_sums": tail_sums,
        "pos": pos,
        "pad_rows": np.concatenate([wv.reshape(P, -1), affine.reshape(P, -1)], axis=1),
        "ident": np.eye(P, dtype=np.float32),
    }


_CONSTANTS = constants()
_INS = [
    "x", "L0_tok_emb", "L0_tok_Wq", "L0_tok_bq", "L0_tok_Wk", "L0_tok_bk", "L0_tok_Wv", "L0_tok_bv", "L0_tok_Wf",
    "L0_tok_bf", "L0_tok_g1", "L0_tok_b1", "L0_tok_g2", "L0_tok_b2", "L0_attn_fc1_w", "L0_attn_fc1_b",
    "L0_attn_convA_w", "L0_attn_convA_b", "L0_attn_convB_w", "L0_attn_convB_b", "L0_attn_qkv_w", "L0_attn_qkv_b",
    "L0_attn_rpb", "L0_attn_proj_w", "L0_attn_proj_b", "L0_attn_fc2_w", "L0_attn_fc2_b", "L0_ffn_in_weight",
    "L0_ffn_in_bias", "L0_ffn_out_weight", "L1_attn_Wqkv", "L1_attn_Wproj", "L1_attn_Wv", "L1_attn_bv",
    "L1_ffn_ln_gamma", "L1_ffn_ln_beta", "L1_ffn_router_w", "L1_ffn_w1", "L1_ffn_w2",
]


def tower(nc, ins, const, out):

    def dram(name, shape, dt=F32):
        return nc.dram_tensor(name, shape, dt).ap()

    def group(prefix, names):
        return [ins[prefix + n] for n in names.split()]

    rows_out = out.rearrange("b s d -> (b s) d")
    h1, h2 = dram("h1", (TOKENS, D)), dram("h2", (TOKENS, D))
    scratch = dram("q_parts", (3 * NB * D, SEQ), BF16), dram("k_parts", (3 * NB * D, SEQ), BF16), dram("v_rows", (NB * NG * SEQ, P))
    shifts = dram("shifts", (COLS, HEADS, UROWS, SPAN))
    to_turn = group("L0_attn_", "fc1_w convA_w convB_w qkv_w proj_w fc2_w") + group("L0_ffn_", "in_weight") + group("L1_attn_", "Wqkv Wproj Wv")
    turned = turned_weights(nc, to_turn, const["ident"])
    row_sems, turn_sems = row_semaphores(nc)
    token_stage(nc, ins["x"], ins["L0_tok_emb"], group("L0_tok_", "Wq bq Wk bk Wv bv Wf bf g1 b1 g2 b2"),
                const["pos"], const["pad_rows"], const["ident"], h1, scratch)
    neighborhood_stage(nc, h1, h2, group("L0_attn_", "fc1_b convA_b convB_b qkv_b rpb proj_b fc2_b"), turned[0:6], shifts,
                       const, row_sems, turn_sems)
    with ExitStack() as ctx:
        st = Store(nc, ctx, "main")
        H = st.sb("H", [P, TILES, D])
        idn = st.sb("idn", [P, P])
        mean = st.sb("mean", [P, TILES])
        rstd = st.sb("rstd", [P, TILES])
        h_in, h_out = st.sem("h_in"), st.sem("h_out")
        with nc.Block() as block:

            @block.sync
            def _(sp):
                sp.dma_start(H[:, :, :], h2.rearrange("(t p) d -> p t d", p=P)).then_inc(h_in, 16)
                sp.dma_start(idn[:, :], const["ident"]).then_inc(h_in, 16)
                sp.wait_ge(h_in, 32)

        dense_stage(nc, H, idn, turned[6], ins["L0_ffn_in_bias"], ins["L0_ffn_out_weight"], mean, rstd, row_sems, turn_sems)
        sets_stage(nc, H, idn, turned[7], turned[8], turned[9], ins["L1_attn_bv"], const, mean, rstd, row_sems)
        experts_stage(nc, H, idn, *group("L1_ffn_", "ln_gamma ln_beta router_w w1 w2"), mean, rstd, row_sems, turn_sems)
        with nc.Block() as block:

            @block.sync
            def _(sp):
                sp.dma_start(rows_out.rearrange("(t p) d -> p t d", p=P), H[:, :, :]).then_inc(h_out, 16)
                sp.wait_ge(h_out, 16)


def kernel(**inputs):
    import numpy as _np
    import concourse.bacc as _bacc
    from concourse import mybir as _mybir
    from concourse.bass_utils import run_bass_kernel_spmd as _run

    nc = _bacc.Bacc("TRN2", target_bir_lowering=False, num_devices=1)
    arrays, ins, const = {}, {}, {}
    for group, names, values in ((ins, _INS, inputs), (const, list(_CONSTANTS), _CONSTANTS)):
        for name in names:
            a = _np.ascontiguousarray(values[name])
            arrays[f"in_{name}_dram"] = a
            group[name] = nc.dram_tensor(f"in_{name}_dram", a.shape, _mybir.dt.from_np(a.dtype), kind="ExternalInput").ap()
    out = nc.dram_tensor("out_0_dram", (NB, SEQ, D), F32, kind="ExternalOutput").ap()
    tower(nc, ins, const, out)
    r = _run(nc, [arrays], core_ids=[0])
    return r.results[0]["out_0_dram"]
```

```python
from contextlib import ExitStack

import concourse.bass as bass
import numpy as np
from concourse import mybir

F32 = mybir.dt.float32
BF16 = mybir.dt.bfloat16
I32 = mybir.dt.int32
U32 = mybir.dt.uint32
ALU = mybir.AluOpType
ACT = mybir.ActivationFunctionType
AX = mybir.AxisListType

P = 128
NB, SEQ, D = 16, 512, 192
TOKENS = NB * SEQ
VOCAB = 8000
NH, HD = 12, 16
PAD = 32
NG, GH = 3, 4
TT = SEQ // P
TILES = TOKENS // P
EPS = 1e-5
LAYERS = 2
NEG = -1.0e30


class Chain:

    def __init__(self, eng, sem, per=0, turn=0):
        self.eng, self.sem, self.base, self.per, self.n = eng, sem, turn * per, per, 0

    def __call__(self, ins):
        ins.then_inc(self.sem, 1)
        self.n += 1

    def wait(self):
        self.eng.wait_ge(self.sem, self.base + self.n)

    def end(self):
        assert self.n == self.per, (self.n, self.per)


class Store:

    taken = []

    def __init__(self, nc, ctx, stage):
        self.nc, self.ctx, self.stage = nc, ctx, stage

    def sb(self, name, shape, dt=F32):
        return self.ctx.enter_context(self.nc.sbuf_tensor(f"{self.stage}_{name}", shape, dt))

    def ps(self, name, shape, dt=F32):
        return self.ctx.enter_context(self.nc.psum_tensor(f"{self.stage}_{name}", shape, dt))

    def sem(self, name):
        sem = self.nc.alloc_semaphore(name=f"{self.stage}_{name}")
        self.taken.append(sem)
        return sem


def release(nc):
    nc.clear_and_free_semaphores(Store.taken[:])
    nc.all_engine_barrier()
    Store.taken.clear()




def token_stage(nc, x, emb, weights, pos, pad_rows, ident, h1, scratch):
    Wq, bq, Wk, bk, Wv, bv, Wf, bf, g1, b1, g2, b2 = weights
    q_parts, k_parts, v_rows = scratch
    SCALE = float(np.float32(1.0) / np.sqrt(np.float32(D)))
    UNITS = NB * NG
    SLOTS = 4

    with ExitStack() as stage:
        st = Store(nc, stage, "tok")
        hT = st.sb("hT", [P, NB, NG, SEQ])
        hT_u = hT[:, :, :, :].rearrange("p b g t -> p (b g) t")
        wq = st.sb("wq", [P, D])
        wk = st.sb("wk", [P, D])
        wv = st.sb("wv", [P, NH * PAD])
        wf = st.sb("wf", [P, NG, NH * PAD])
        affine = st.sb("affine", [P, NG, 4])
        norm = st.sb("norm", [P, 2, 2, NG])
        mean_var = st.sb("mean_var", [P, NG, 2])
        power = st.sb("power", [P, 2, NG])
        stats = st.sb("stats", [P, NG, NB, 6])
        idn = st.sb("idn", [P, P])
        idn_b = st.sb("idn_b", [P, P], BF16)

        with ExitStack() as part:
            pt = Store(nc, part, "emb")
            ids = pt.sb("ids", [P, TILES], I32)
            wrap = pt.sb("wrap", [P, TILES], I32)
            wrapped = pt.sb("wrapped", [P, TILES], I32)
            rows = pt.sb("rows", [P, TILES, D])
            posn = pt.sb("posn", [P, TT, D])
            tmp = pt.sb("tmp", [P, TT, D])
            padded = pt.sb("padded", [P, 2, TT, NH, PAD])
            turned = pt.ps("turned", [P, 2, 4, SEQ])
            ids_in, pos_in, idn_in = pt.sem("ids_in"), pt.sem("pos_in"), pt.sem("idn_in")
            zeroed, weights_in = pt.sem("zeroed"), pt.sem("weights_in")
            rows_in = [pt.sem("rows_in_even"), pt.sem("rows_in_odd")]
            own, idn_copied = pt.sem("own"), pt.sem("idn_copied")
            ready, padded_done, turned_done, copied = (
                pt.sem("ready"), pt.sem("padded_done"), pt.sem("turned_done"), pt.sem("copied"))
            with nc.Block() as block:

                @block.sync
                def _(sp):
                    with nc.allow_non_contiguous_dma(reason="one token number per partition"):
                        sp.dma_start(ids[:, :], x.rearrange("b (q p) -> p (b q)", p=P)).then_inc(ids_in, 16)
                    sp.dma_start(posn[:, :, :], pos.rearrange("(q p) d -> p q d", p=P)).then_inc(pos_in, 16)
                    sp.dma_start(idn[:, :], ident).then_inc(idn_in, 16)
                    sp.wait_ge(zeroed, 4)
                    sp.dma_start(wv[:, :], pad_rows[:, 0:NH * PAD]).then_inc(weights_in, 16)
                    sp.dma_start(affine[:, :, :], pad_rows[:, NH * PAD:].rearrange("p (g k) -> p g k", g=NG)).then_inc(weights_in, 16)
                    sp.wait_ge(weights_in, 32)
                    for j in range(GH):
                        rows_j = slice(PAD * j, PAD * j + HD)
                        in_j = slice(HD * j, HD * j + HD)
                        sp.dma_start(wq[rows_j, :], Wq[in_j, :]).then_inc(weights_in, 16)
                        sp.dma_start(wk[rows_j, :], Wk[in_j, :]).then_inc(weights_in, 16)
                        sp.dma_start(wv[rows_j, :].rearrange("p (h c) -> p h c", h=NH)[:, :, 0:HD],
                                     Wv[in_j, :].rearrange("p (h c) -> p h c", h=NH)).then_inc(weights_in, 16)
                        for g in range(NG):
                            c0 = HD * (GH * g + j)
                            sp.dma_start(wf[rows_j, g, :].rearrange("p (h c) -> p h c", h=NH)[:, :, 0:HD],
                                         Wf[c0:c0 + HD, :].rearrange("p (h c) -> p h c", h=NH)).then_inc(weights_in, 16)
                            for n, vec in enumerate((g1, b1, g2, b2)):
                                sp.dma_start(affine[rows_j, g, n:n + 1],
                                             vec[c0:c0 + HD].rearrange("(p a) -> p a", a=1)).then_inc(weights_in, 16)
                    one = slice(HD, HD + 1)
                    sp.dma_start(wq[one, :], bq.rearrange("(a n) -> a n", a=1)).then_inc(weights_in, 16)
                    sp.dma_start(wk[one, :], bk.rearrange("(a n) -> a n", a=1)).then_inc(weights_in, 16)
                    sp.dma_start(wv[one, :].rearrange("p (h c) -> p h c", h=NH)[:, :, 0:HD],
                                 bv.rearrange("(a h c) -> a h c", a=1, h=NH)).then_inc(weights_in, 16)
                    sp.dma_start(wf[one, 0, :].rearrange("p (h c) -> p h c", h=NH)[:, :, 0:HD],
                                 bf.rearrange("(a h c) -> a h c", a=1, h=NH)).then_inc(weights_in, 16)
                    sp.wait_ge(weights_in, 16 * (2 + GH * (3 + NG * 5) + 4))

                @block.gpsimd
                def _(pool):
                    pool.memset(wq[:, :], 0.0).then_inc(zeroed, 1)
                    pool.memset(wk[:, :], 0.0).then_inc(zeroed, 1)
                    pool.memset(wv[:, :], 0.0).then_inc(zeroed, 1)
                    pool.memset(wf[:, :, :], 0.0).then_inc(zeroed, 1)
                    pool.wait_ge(ready, 1)
                    for t in range(TILES):
                        b = t // TT
                        if t % TT == 0 and b >= 2:
                            pool.wait_ge(rows_in[b % 2], 16 * TT * (b // 2))
                        pool.indirect_dma_start(rows[:, t, :], None, emb[:, :],
                                                bass.IndirectOffsetOnAxis(ap=wrapped[:, t:t + 1].bitcast(U32), axis=0)
                                                ).then_inc(rows_in[b % 2], 16)

                @block.vector
                def _(dve):
                    chain = Chain(dve, own)
                    dve.wait_ge(ids_in, 16)
                    chain(dve.tensor_scalar(wrap[:, :], ids[:, :], 0.0, float(VOCAB), ALU.is_lt, ALU.mult))
                    chain.wait()
                    chain(dve.tensor_tensor(wrap[:, :], ids[:, :], wrap[:, :], ALU.add))
                    chain.wait()
                    dve.tensor_scalar(wrapped[:, :], wrap[:, :], 0.0, float(VOCAB - 1), ALU.max, ALU.min).then_inc(ready, 1)
                    chain(dve.memset(padded[:, :, :, :, :], 0.0))
                    chain.wait()
                    chain(dve.memset(padded[:, :, :, :, HD:HD + 1], 1.0))
                    chain(dve.memset(norm[:, 1, 0, :], 1.0))
                    chain(dve.memset(norm[:, 1, 1, :], 0.0))
                    chain.wait()
                    base = chain.n
                    dve.wait_ge(pos_in, 16)
                    with dve.Fori(0, NB // 2) as it:
                        for half in range(2):
                            b = it * 2 + half
                            dve.wait_ge(rows_in[half], it * (16 * TT) + 16 * TT)
                            e = rows[:, bass.ds(b * TT, TT), :]
                            dve.wait_ge(padded_done, b)
                            dve.tensor_tensor(tmp[:, :, :], e, posn[:, :, :], ALU.add).then_inc(own, 1)
                            dve.wait_ge(own, b + (base + 1))
                            dve.wait_ge(turned_done, b)
                            dve.tensor_tensor(padded[:, half, :, :, 0:HD],
                                              tmp[:, :, :].rearrange("p q (h c) -> p q h c", h=NH),
                                              e.rearrange("p q (h c) -> p q h c", h=NH), ALU.add).then_inc(padded_done, 1)

                @block.tensor
                def _(pe):
                    pe.wait_ge(idn_in, 16)
                    pe.sem_inc(turned_done, 1)
                    with pe.Fori(0, NB // 2) as it:
                        for half in range(2):
                            b = it * 2 + half
                            pe.wait_ge(padded_done, b + 1)
                            pe.wait_ge(copied, b)
                            for g in range(NG):
                                for q in range(TT):
                                    last = pe.transpose(turned[:, half, g, P * q:P * q + P],
                                                        padded[:, half, q, GH * g:GH * g + GH, :].rearrange("p h c -> p (h c)"),
                                                        idn[:, :])
                            last.then_inc(turned_done, 1)

                @block.scalar
                def _(act):
                    act.wait_ge(idn_in, 16)
                    act.activation(idn_b[:, :], idn[:, :], ACT.Copy).then_inc(idn_copied, 1)
                    act.sem_inc(copied, 1)
                    with act.Fori(0, NB // 2) as it:
                        for half in range(2):
                            b = it * 2 + half
                            act.wait_ge(turned_done, b + 2)
                            act.activation(hT[:, bass.ds(b, 1), :, :].rearrange("p b g t -> p (b g) t"),
                                           turned[:, half, 0:NG, :], ACT.Copy).then_inc(copied, 1)

        with nc.Fori(0, LAYERS) as layer:
            token_project(nc, layer, hT, wq, wk, wv, norm, q_parts, k_parts, v_rows)
            token_attention(nc, layer, hT_u, idn, idn_b, stats, q_parts, k_parts, v_rows, SCALE, UNITS, SLOTS)
            token_norm(nc, layer, 0, stats, mean_var, power, affine, norm)
            token_dense(nc, layer, hT, wf, norm, stats)
            token_norm(nc, layer, 1, stats, mean_var, power, affine, norm)

        with ExitStack() as part:
            pt = Store(nc, part, "end")
            staged = pt.sb("staged", [P, 2, NG, SEQ])
            out_rows = pt.sb("out_rows", [P, 2, TT, D])
            turned = pt.ps("turned", [P, TT, SEQ])
            staged_done, turned_done, out_done = pt.sem("staged_done"), pt.sem("turned_done"), pt.sem("out_done")
            stored = [pt.sem("stored_even"), pt.sem("stored_odd")]
            with nc.Block() as block:

                @block.scalar
                def _(act):
                    with act.Fori(0, NB // 2) as it:
                        for half in range(2):
                            b = it * 2 + half
                            act.wait_ge(turned_done, b)
                            for g in range(NG):
                                act.activation(staged[:, half, g, :], hT[:, bass.ds(b, 1), g, :].rearrange("p b t -> p (b t)"),
                                               ACT.Identity, bias=norm[:, 1, 1, g:g + 1],
                                               scale=norm[:, 1, 0, g:g + 1]).then_inc(staged_done, 1)

                @block.tensor
                def _(pe):
                    pe.sem_inc(turned_done, 1)
                    with pe.Fori(0, NB // 2) as it:
                        for half in range(2):
                            b = it * 2 + half
                            pe.wait_ge(staged_done, b * NG + NG)
                            pe.wait_ge(out_done, b * 2)
                            for q in range(TT):
                                for g in range(NG):
                                    last = pe.transpose(turned[:, q, P * g:P * g + P], staged[:, half, g, P * q:P * q + P], idn[:, :])
                            last.then_inc(turned_done, 1)

                @block.vector
                def _(dve):
                    with dve.Fori(0, NB // 2) as it:
                        for half in range(2):
                            b = it * 2 + half
                            dve.wait_ge(turned_done, b + 2)
                            dve.wait_ge(stored[half], it * 16)
                            for n in range(2):
                                dve.tensor_copy(
                                    out_rows[:, half, 2 * n:2 * n + 2, :].rearrange("p q (h c) -> p q h c", h=NH),
                                    turned[:, 2 * n:2 * n + 2, 0:NH * PAD].rearrange("p q (h c) -> p q h c", h=NH)[:, :, :, 0:HD]
                                ).then_inc(out_done, 1)

                @block.sync
                def _(sp):
                    with sp.Fori(0, NB // 2) as it:
                        for half in range(2):
                            b = it * 2 + half
                            sp.wait_ge(out_done, b * 2 + 2)
                            sp.dma_start(h1[bass.ds(b * SEQ, SEQ), :].rearrange("(q p) d -> p q d", p=P),
                                         out_rows[:, half, :, :]).then_inc(stored[half], 16)
                    for half in range(2):
                        sp.wait_ge(stored[half], 16 * NB // 2)


def token_project(nc, layer, hT, wq, wk, wv, norm, q_parts, k_parts, v_rows):
    with ExitStack() as part:
        pt = Store(nc, part, "proj")
        staged = pt.sb("staged", [P, 2, NG, SEQ])
        full = [pt.sb(f"full_{n}", [96, 2, 2, SEQ]) for n in "qk"]
        rest = [pt.sb(f"rest_{n}", [96, 2, SEQ]) for n in "qk"]
        parts = [pt.sb(f"parts_{n}", [96, 2, 3, 2, SEQ], BF16) for n in "qk"]
        v_sb = pt.sb("v_sb", [P, 2, TT, NH * PAD])
        qk_ps = [pt.ps(f"{n}_ps", [96, 2, SEQ]) for n in "qk"]
        v_ps = pt.ps("v_ps", [P, TT, SEQ])
        staged_done, restored = pt.sem("staged_done"), pt.sem("restored")
        qk_done, v_done = pt.sem("qk_done"), pt.sem("v_done")
        full_done = pt.sem("full_done")
        v_copied = pt.sem("v_copied")
        split = [pt.sem(f"split_{n}") for n in "qk"]
        stored = [[pt.sem(f"stored_{n}_{half}") for half in ("even", "odd")] for n in "qk"]
        v_stored = [pt.sem(f"v_stored_{half}") for half in ("even", "odd")]
        all_stored = pt.sem("all_stored")
        STORES = 3
        one_ahead = layer * (NB + 1)
        full_ahead = layer * (4 * NB + 2)
        with nc.Block() as block:

            @block.scalar
            def _(act):
                act.sem_inc(full_done, 2)

                def stage(b, half):
                    act.wait_ge(v_done, one_ahead + b)
                    act.wait_ge(restored, one_ahead + b)
                    for g in range(NG):
                        act.activation(staged[:, half, g, :], hT[:, bass.ds(b, 1), g, :].rearrange("p b t -> p (b t)"),
                                       ACT.Identity, bias=norm[:, 1, 1, g:g + 1],
                                       scale=norm[:, 1, 0, g:g + 1]).then_inc(staged_done, 1)

                def copies(b, half, pair):
                    n = layer * NB + b
                    for m in range(2):
                        act.wait_ge(qk_done, n * 2 + m + 1)
                        act.wait_ge(split[m], n * 3 - 3)
                        act.wait_ge(stored[m][half], (layer * (NB // 2) + pair) * (16 * STORES))
                        act.activation(full[m][:, half, :, :], qk_ps[m][:, :, :], ACT.Relu).then_inc(full_done, 1)
                        act.activation(parts[m][:, half, 0, :, :], qk_ps[m][:, :, :], ACT.Relu).then_inc(full_done, 1)

                def first_copies():
                    for m in range(2):
                        act.wait_ge(qk_done, layer * (2 * NB) + m + 1)
                        act.wait_ge(split[m], layer * (3 * NB))
                        act.wait_ge(stored[m][0], layer * (16 * STORES * NB // 2))
                        act.activation(full[m][:, 0, :, :], qk_ps[m][:, :, :], ACT.Relu).then_inc(full_done, 1)
                        act.activation(parts[m][:, 0, 0, :, :], qk_ps[m][:, :, :], ACT.Relu).then_inc(full_done, 1)

                stage(0, 0)
                stage(1, 1)
                first_copies()
                with act.Fori(0, NB // 2 - 1) as it:
                    stage(it * 2 + 2, 0)
                    copies(it * 2 + 1, 1, it)
                    stage(it * 2 + 3, 1)
                    copies(it * 2 + 2, 0, it + 1)
                copies(NB - 1, 1, NB // 2 - 1)

            @block.tensor
            def _(pe):
                pe.sem_inc(v_done, 1)
                with pe.Fori(0, NB // 2) as it:
                    for half in range(2):
                        b = it * 2 + half
                        n = layer * NB + b
                        pe.wait_ge(staged_done, n * NG + NG)
                        for m, w in enumerate((wq, wk)):
                            pe.wait_ge(full_done, full_ahead + b * 4 + 2 * m)
                            for c in range(2):
                                last = pe.matmul(qk_ps[m][:, c, :], w[:, 96 * c:96 * c + 96], staged[:, half, m, :],
                                                 start=True, stop=True)
                            last.then_inc(qk_done, 1)
                        pe.wait_ge(v_copied, n)
                        for q in range(TT):
                            last = pe.matmul(v_ps[:, q, 0:NH * PAD], staged[:, half, 2, P * q:P * q + P], wv[:, :],
                                             start=True, stop=True)
                        last.then_inc(v_done, 1)

            def split_parts(eng, m, b, half):
                n = layer * NB + b
                value, part = full[m][:, half, :, :], parts[m][:, half, :, :, :]
                eng.wait_ge(full_done, full_ahead + b * 4 + (2 * m + 4))
                eng.wait_ge(split[m], n * 3)
                eng.tensor_tensor(rest[m][:, :, :], value, part[:, 0, :, :], ALU.subtract).then_inc(split[m], 1)
                eng.tensor_tensor(part[:, 1, :, :], value, part[:, 0, :, :], ALU.subtract).then_inc(split[m], 1)
                eng.wait_ge(split[m], n * 3 + 2)
                eng.tensor_tensor(part[:, 2, :, :], rest[m][:, :, :], part[:, 1, :, :], ALU.subtract).then_inc(split[m], 1)

            @block.gpsimd
            def _(pool):
                with pool.Fori(0, NB // 2) as it:
                    for half in range(2):
                        split_parts(pool, 0, it * 2 + half, half)

            @block.vector
            def _(dve):
                dve.sem_inc(restored, 1)
                with dve.Fori(0, NB // 2) as it:
                    for half in range(2):
                        b = it * 2 + half
                        n = layer * NB + b
                        dve.wait_ge(staged_done, n * NG + NG)
                        dve.tensor_copy(hT[:, bass.ds(b, 1), :, :].rearrange("p b g t -> p (b g) t"),
                                        staged[:, half, :, :]).then_inc(restored, 1)
                        split_parts(dve, 1, b, half)
                        dve.wait_ge(v_done, one_ahead + b + 2)
                        dve.wait_ge(v_stored[half], (layer * (NB // 2) + it) * (16 * NG))
                        dve.tensor_scalar(v_sb[:, half, :, :], v_ps[:, :, 0:NH * PAD], 0.0, None, ALU.max).then_inc(v_copied, 1)

            @block.sync
            def _(sp):
                with sp.Fori(0, NB // 2) as it:
                    for half in range(2):
                        b = it * 2 + half
                        n = layer * NB + b
                        for m, dram in enumerate((q_parts, k_parts)):
                            sp.wait_ge(split[m], n * 3 + 3)
                            for k in range(3):
                                sp.dma_start(dram[bass.ds(b * D + k * (NB * D), D), :].rearrange("(c p) t -> p c t", c=2),
                                             parts[m][:, half, k, :, :]).then_inc(stored[m][half], 16)
                        sp.wait_ge(v_copied, n + 1)
                        for g in range(NG):
                            sp.dma_start(v_rows[bass.ds(b * (NG * SEQ) + g * SEQ, SEQ), :].rearrange("(q p) c -> p q c", p=P),
                                         v_sb[:, half, :, P * g:P * g + P]).then_inc(v_stored[half], 16)
                for half in range(2):
                    for m in range(2):
                        sp.wait_ge(stored[m][half], (layer + 1) * (8 * STORES * NB))
                    sp.wait_ge(v_stored[half], (layer + 1) * (8 * NG * NB))
                sp.sem_inc(all_stored, 1)


def token_attention(nc, layer, hT_u, idn, idn_b, stats, q_parts, k_parts, v_rows, SCALE, UNITS, SLOTS):
    ROWS = 96 + 3
    with ExitStack() as part:
        pt = Store(nc, part, "att")
        q_sb = pt.sb("q_sb", [ROWS, SLOTS, GH, SEQ], BF16)
        k_sb = pt.sb("k_sb", [ROWS, SLOTS, GH, SEQ], BF16)
        v_sb = pt.sb("v_sb", [P, SLOTS, TT, P])
        probs = pt.sb("probs", [P, 2, GH, SEQ])
        neg_max = pt.sb("neg_max", [P, 2, GH, TT])
        max_rest = pt.sb("max_rest", [P, GH, TT])
        max_parts = pt.sb("max_parts", [P, 2, 3, GH, TT], BF16)
        max_rows = pt.sb("max_rows", [3 * GH, SEQ], BF16)
        o_raw = pt.sb("o_raw", [P, SEQ])
        o_norm = pt.sb("o_norm", [P, TT, GH, PAD])
        recip = pt.sb("recip", [P, TT, GH])
        s_ps = pt.ps("s_ps", [P, 2, SEQ])
        st_ps = pt.ps("st_ps", [P, GH, SEQ])
        o_ps = pt.ps("o_ps", [P, SEQ])
        misc = pt.ps("misc", [P, SEQ])
        misc_b = misc[0:3 * GH, :].bitcast(BF16)[:, 0:SEQ]
        loaded = [pt.sem(f"loaded{s}") for s in range(SLOTS)]
        s_done, s_read = pt.sem("s_done"), pt.sem("s_read")
        st_done, exp_done, pv_done = pt.sem("st_done"), pt.sem("exp_done"), pt.sem("pv_done")
        o_copied, o_turned, o_normed, o_back, h_added = (
            pt.sem("o_copied"), pt.sem("o_turned"), pt.sem("o_normed"), pt.sem("o_back"), pt.sem("h_added"))
        max_split, rows_turned, rows_copied, rows_sent = (
            pt.sem("max_split"), pt.sem("rows_turned"), pt.sem("rows_copied"), pt.sem("rows_sent"))
        all_sent = pt.sem("all_sent")
        own, ones_set, recip_done = pt.sem("own"), pt.sem("ones_set"), pt.sem("recip_done")
        split_begun, k_ones_set = pt.sem("split_begun"), pt.sem("k_ones_set")
        LOADS = 13
        TURNS = UNITS // SLOTS

        with nc.Block() as block:

            def load(sp, s, u):
                for dst, src, order in ((q_sb, q_parts, (0, 1, 2, 0, 1, 0)), (k_sb, k_parts, (0, 0, 0, 1, 1, 2))):
                    for at, k in enumerate(order):
                        rows = src[bass.ds(u * (GH * HD) + k * (NB * D), GH * HD), :]
                        sp.dma_start(dst[HD * at:HD * at + HD, s, :, :],
                                     rows.rearrange("(h r) t -> r h t", h=GH)).then_inc(loaded[s], 16)
                sp.dma_start(v_sb[:, s, :, :], v_rows[bass.ds(u * SEQ, SEQ), :].rearrange("(q p) c -> p q c", p=P)
                             ).then_inc(loaded[s], 16)

            @block.sync
            def _(sp):
                for s in range(SLOTS):
                    load(sp, s, s)

                def send(s, u):
                    n = layer * UNITS + u
                    sp.wait_ge(rows_copied, n + 1)
                    sp.dma_start(q_sb[96:99, s % SLOTS, :, :], max_rows[:, :]).then_inc(rows_sent, 16)

                send(0, 0)
                with sp.Fori(0, TURNS - 1) as turn:
                    for s in range(SLOTS):
                        u = turn * SLOTS + s
                        send(s + 1, u + 1)
                        sp.wait_ge(pv_done, (layer * UNITS + u) * TT + TT)
                        load(sp, s, u + SLOTS)
                for s in range(SLOTS - 1):
                    send(s + 1, (TURNS - 1) * SLOTS + s + 1)
                sp.wait_ge(rows_sent, (layer + 1) * (16 * UNITS))
                sp.sem_inc(all_sent, 1)

            def score_row(pe, s, u, q, h):
                n = layer * UNITS + u
                m = 4 * q + h
                pe.wait_ge(s_read, n * 16 + max(m - 1, 0))
                pe.matmul(s_ps[:, m % 2, :], q_sb[0:96, s, h, P * q:P * q + P], k_sb[0:96, s, h, :],
                          start=True, stop=True).then_inc(s_done, 1)

            def turn_maxima(pe, s, u):
                n = layer * UNITS + u
                pe.wait_ge(max_split, n + 1)
                for q in range(TT):
                    last = pe.transpose(misc_b[:, P * q:P * q + P],
                                        max_parts[:, s % 2, :, :, q].rearrange("p k h -> p (k h)"), idn_b[:, :])
                last.then_inc(rows_turned, 1)

            @block.tensor
            def _(pe):
                for s in range(2):
                    pe.wait_ge(loaded[s], (layer * TURNS + 1) * (16 * LOADS))
                    for q in range(TT):
                        for h in range(GH):
                            score_row(pe, s, s, q, h)
                turn_maxima(pe, 0, 0)
                pe.wait_ge(k_ones_set, layer + 1)
                pe.wait_ge(ones_set, layer + 1)

                def turn_out(n, rows):
                    pe.wait_ge(o_copied, n + 1)
                    pe.wait_ge(rows_copied, rows)
                    for q in range(TT):
                        last = pe.transpose(misc[:, P * q:P * q + P], o_raw[:, P * q:P * q + P], idn[:, :])
                    last.then_inc(o_turned, 1)

                def turn_back(n):
                    pe.wait_ge(o_normed, n + 1)
                    for q in range(TT):
                        last = pe.transpose(misc[:, P * q:P * q + P],
                                            o_norm[:, q, :, :].rearrange("p h c -> p (h c)"), idn[:, :])
                    last.then_inc(o_back, 1)

                def values(s, n, t):
                    pe.wait_ge(exp_done, n * 8 + (2 * t + 2))
                    if t == 0:
                        pe.wait_ge(o_copied, n)
                    for h in range(GH):
                        last = pe.matmul(o_ps[PAD * h:PAD * h + PAD, :], v_sb[:, s, t, PAD * h:PAD * h + PAD],
                                         probs[:, t % 2, h, :], start=(t == 0), stop=(t == TT - 1))
                    last.then_inc(pv_done, 1)

                def unit(s, u, turn, ahead, following, first):
                    n = layer * UNITS + u
                    s2, s1 = (s + 2) % SLOTS, (s + 1) % SLOTS
                    pe.wait_ge(rows_sent, n * 16 + 16)
                    if ahead:
                        pe.wait_ge(loaded[s2], (layer * TURNS + turn + (2 if s + 2 >= SLOTS else 1)) * (16 * LOADS))

                    def scores(t, half):
                        if t:
                            pe.wait_ge(exp_done, n * 8 + (2 * t + half - 1))
                        else:
                            pe.wait_ge(exp_done, n * 8 if first else n * 8 + (half - 1))
                        for h in (2 * half, 2 * half + 1):
                            last = pe.matmul(st_ps[:, h, :], k_sb[0:ROWS, s, h, P * t:P * t + P], q_sb[0:ROWS, s, h, :],
                                             start=True, stop=True)
                        last.then_inc(st_done, 1)

                    for t in range(TT):
                        scores(t, 0)
                        if ahead:
                            score_row(pe, s2, u + 2, t, 0)
                        scores(t, 1)
                        if ahead:
                            score_row(pe, s2, u + 2, t, 1)
                        if t:
                            values(s, n, t - 1)
                        elif not first:
                            values((s - 1) % SLOTS, n - 1, TT - 1)
                        if ahead:
                            score_row(pe, s2, u + 2, t, 2)
                            score_row(pe, s2, u + 2, t, 3)
                        if t == 0 and not first:
                            pe.wait_ge(h_added, n - 1)
                        if t == 0 and following:
                            turn_maxima(pe, s1, u + 1)
                        if t == 1 and not first:
                            turn_out(n - 1, n + (2 if following else 1))
                        if t == 2 and not first:
                            turn_back(n - 1)

                for s in range(SLOTS):
                    unit(s, s, 0, True, True, s == 0)
                with pe.Fori(1, TURNS - 1) as turn:
                    for s in range(SLOTS):
                        unit(s, turn * SLOTS + s, turn, True, True, False)
                for s in range(SLOTS):
                    unit(s, (TURNS - 1) * SLOTS + s, TURNS - 1, s < SLOTS - 2, s < SLOTS - 1, False)
                end = (layer + 1) * UNITS
                values(SLOTS - 1, end - 1, TT - 1)
                pe.wait_ge(h_added, end - 1)
                turn_out(end - 1, end)
                turn_back(end - 1)

            @block.scalar
            def _(act):
                def copy_out(n):
                    act.wait_ge(pv_done, n * TT + TT)
                    act.wait_ge(o_turned, n)
                    act.activation(o_raw[:, :], o_ps[:, :], ACT.Copy).then_inc(o_copied, 1)

                def copy_rows(n):
                    act.wait_ge(rows_turned, n + 1)
                    act.wait_ge(rows_sent, n * 16)
                    act.activation(max_rows[:, :], misc_b, ACT.Copy).then_inc(rows_copied, 1)

                def unit(s, u, first, following=True):
                    n = layer * UNITS + u
                    for t in range(TT):
                        for half in range(2):
                            act.wait_ge(st_done, n * 8 + 2 * t + half + 1)
                            if t >= 2:
                                act.wait_ge(pv_done, n * TT + t - 1)
                            else:
                                act.wait_ge(pv_done, n * TT if t == 1 or first else n * TT - 1)
                            act.activation(probs[:, t % 2, 2 * half:2 * half + 2, :], st_ps[:, 2 * half:2 * half + 2, :],
                                           ACT.Exp, scale=SCALE).then_inc(exp_done, 1)
                        if t == 0 and not first:
                            copy_out(n - 1)
                        if t == 0 and following:
                            copy_rows(n + 1)

                copy_rows(layer * UNITS)
                for s in range(SLOTS):
                    unit(s, s, s == 0)
                with act.Fori(1, TURNS - 1) as turn:
                    for s in range(SLOTS):
                        unit(s, turn * SLOTS + s, False)
                for s in range(SLOTS):
                    unit(s, UNITS - SLOTS + s, False, s < SLOTS - 1)
                copy_out(layer * UNITS + UNITS - 1)

            @block.gpsimd
            def _(pool):
                pool.memset(k_sb[96:99, :, :, :].rearrange("p s h t -> p (s h t)"), 1.0).then_inc(k_ones_set, 1)
                pool.wait_ge(k_ones_set, layer + 1)

                def split_maxima(half, u, first):
                    n = layer * UNITS + u
                    pool.wait_ge(s_read, n * 16 + 16)
                    pool.wait_ge(max_split, n)
                    if not first:
                        pool.wait_ge(rows_turned, n - 1)
                    pool.sem_inc(split_begun, 1)
                    mp = max_parts[:, half, :, :, :]
                    nm = neg_max[:, half, :, :]
                    pool.tensor_copy(mp[:, 0, :, :], nm).then_inc(own, 1)
                    pool.wait_ge(own, n * 3 + 1)
                    pool.tensor_tensor(max_rest[:, :, :], nm, mp[:, 0, :, :], ALU.subtract).then_inc(own, 1)
                    pool.wait_ge(own, n * 3 + 2)
                    pool.sem_inc(split_begun, 1)
                    pool.tensor_copy(mp[:, 1, :, :], max_rest[:, :, :]).then_inc(own, 1)
                    pool.wait_ge(own, n * 3 + 3)
                    pool.tensor_tensor(mp[:, 2, :, :], max_rest[:, :, :], mp[:, 1, :, :], ALU.subtract).then_inc(max_split, 1)

                for half in range(2):
                    split_maxima(half, half, True)
                with pool.Fori(1, UNITS // 2) as it:
                    for half in range(2):
                        split_maxima(half, it * 2 + half, False)

            @block.vector
            def _(dve):
                def maxima(s, u, q):
                    n = layer * UNITS + u
                    if q == 0:
                        dve.wait_ge(max_split, layer * UNITS if isinstance(u, int) and u < 2 else n - 1)
                    for h in range(GH):
                        m = 4 * q + h
                        dve.wait_ge(s_done, n * 16 + m + 1)
                        dve.tensor_reduce(neg_max[:, s % 2, h, q:q + 1], s_ps[:, m % 2, :], AX.X, ALU.max,
                                          negate=True).then_inc(s_read, 1)

                def normalise(n):
                    dve.wait_ge(o_turned, n + 1)
                    o = misc[:, :].rearrange("p (q h c) -> p q h c", q=TT, h=GH)
                    dve.reciprocal(recip[:, :, :], o[:, :, :, HD]).then_inc(recip_done, 1)
                    dve.wait_ge(recip_done, n + 1)
                    dve.wait_ge(ones_set, layer + 1)
                    dve.wait_ge(o_back, n)
                    dve.tensor_tensor(o_norm[:, :, :, 0:HD].rearrange("p q h c -> p (q h) c"),
                                      o[:, :, :, 0:HD].rearrange("p q h c -> p (q h) c"),
                                      recip[:, :, :].rearrange("p q h -> p (q h)").unsqueeze(2).to_broadcast([P, TT * GH, HD]),
                                      ALU.mult).then_inc(o_normed, 1)

                def add(n, u):
                    dve.wait_ge(o_back, n + 1)
                    dst = hT_u[:, bass.ds(u, 1), :].rearrange("p u t -> p (u t)")
                    dve.tensor_tensor(dst, dst, misc[:, :], ALU.add).then_inc(h_added, 1)

                dve.memset(o_norm[:, :, :, :], 0.0).then_inc(ones_set, 1)
                for s in range(2):
                    for q in range(TT):
                        maxima(s, s, q)

                def unit(s, u, ahead, first):
                    n = layer * UNITS + u
                    for q in range(TT):
                        if ahead:
                            maxima(s + 2, u + 2, q)
                        if q == 1 and not first:
                            normalise(n - 1)
                        if q == 2 and not first:
                            add(n - 1, u - 1)

                for s in range(SLOTS):
                    unit(s, s, True, s == 0)
                with dve.Fori(1, TURNS - 1) as turn:
                    for s in range(SLOTS):
                        unit(s, turn * SLOTS + s, True, False)
                for s in range(SLOTS):
                    unit(s, (TURNS - 1) * SLOTS + s, s < SLOTS - 2, False)
                normalise(layer * UNITS + UNITS - 1)
                add(layer * UNITS + UNITS - 1, UNITS - 1)
                with dve.Fori(0, NB) as b:
                    dve.wait_ge(h_added, (layer + 1) * UNITS)
                    for g in range(NG):
                        dve.bn_stats(stats[:, g, bass.ds(b, 1), :].rearrange("p b k -> p (b k)"),
                                     hT_u[:, bass.ds(b * NG + g, 1), :].rearrange("p u t -> p (u t)"))


def token_norm(nc, layer, which, stats, mean_var, power, affine, norm):
    with ExitStack() as part:
        pt = Store(nc, part, f"norm{which}")
        own, var_done, pow_done = pt.sem("own"), pt.sem("var_done"), pt.sem("pow_done")
        scale, shift = norm[:, which, 0, :], norm[:, which, 1, :]
        with nc.Block() as block:

            @block.vector
            def _(dve):
                for g in range(NG):
                    dve.bn_aggr(mean_var[:, g, :], stats[:, g, :, :].rearrange("p b k -> p (b k)")).then_inc(own, 1)
                dve.wait_ge(own, layer * 5 + 3)
                dve.memset(power[:, 1, :], -0.5).then_inc(var_done, 1)
                dve.tensor_scalar(power[:, 0, :], mean_var[:, :, 1], EPS, None, ALU.add).then_inc(var_done, 1)
                dve.wait_ge(pow_done, layer + 1)
                dve.tensor_tensor(scale, power[:, 0, :], affine[:, :, 2 * which], ALU.mult).then_inc(own, 1)
                dve.wait_ge(own, layer * 5 + 4)
                dve.tensor_tensor(shift, mean_var[:, :, 0], scale, ALU.mult).then_inc(own, 1)
                dve.wait_ge(own, layer * 5 + 5)
                dve.tensor_tensor(shift, affine[:, :, 2 * which + 1], shift, ALU.subtract)

            @block.gpsimd
            def _(pool):
                pool.wait_ge(var_done, layer * 2 + 2)
                pool.tensor_tensor(power[:, 0, :], power[:, 0, :], power[:, 1, :], ALU.pow).then_inc(pow_done, 1)


def token_dense(nc, layer, hT, wf, norm, stats):
    with ExitStack() as part:
        pt = Store(nc, part, "dense")
        staged = pt.sb("staged", [P, 2, NG, SEQ])
        out_ps = pt.ps("out_ps", [P, 2, 4, SEQ])
        staged_done, product_done, added, stats_done = (
            pt.sem("staged_done"), pt.sem("product_done"), pt.sem("added"), pt.sem("stats_done"))
        with nc.Block() as block:

            @block.scalar
            def _(act):
                with act.Fori(0, NB // 2) as it:
                    for half in range(2):
                        b = it * 2 + half
                        n = layer * NB + b
                        act.wait_ge(added, layer * (NB + 1) + b)
                        for g in range(NG):
                            act.activation(staged[:, half, g, :], hT[:, bass.ds(b, 1), g, :].rearrange("p b t -> p (b t)"),
                                           ACT.Identity, bias=norm[:, 0, 1, g:g + 1],
                                           scale=norm[:, 0, 0, g:g + 1]).then_inc(staged_done, 1)

            @block.tensor
            def _(pe):
                with pe.Fori(0, NB // 2) as it:
                    for half in range(2):
                        b = it * 2 + half
                        pe.wait_ge(staged_done, (layer * NB + b) * NG + NG)
                        pe.wait_ge(added, layer * (NB + 1) + b)
                        for m in range(NG):
                            for g in range(NG):
                                last = pe.matmul(out_ps[:, half, m, :], wf[:, g, P * m:P * m + P], staged[:, half, g, :],
                                                 start=(g == 0), stop=(g == NG - 1))
                        last.then_inc(product_done, 1)

            @block.vector
            def _(dve):
                dve.sem_inc(added, 1)
                with dve.Fori(0, NB // 2) as it:
                    for half in range(2):
                        b = it * 2 + half
                        n = layer * NB + b
                        dve.wait_ge(product_done, n + 1)
                        dve.tensor_tensor(hT[:, bass.ds(b, 1), :, :].rearrange("p b g t -> p (b g) t"),
                                          out_ps[:, half, 0:NG, :], staged[:, half, :, :], ALU.add).then_inc(added, 1)
                        dve.wait_ge(added, layer * (NB + 1) + b + 2)
                        for g in range(NG):
                            ins = dve.bn_stats(stats[:, g, bass.ds(b, 1), :].rearrange("p b k -> p (b k)"),
                                               hT[:, bass.ds(b, 1), g, :].rearrange("p b t -> p (b t)"))
                        ins.then_inc(stats_done, 1)


C2 = D // 2
GROUPS = TILES // TT


def is_number(x, value):
    return isinstance(x, int) and x == value


def row_statistics(nc, H, mean, rstd):
    with ExitStack() as part:
        pt = Store(nc, part, "row_stats")
        stats = pt.sb("stats", [P, TILES, 6])
        mean_var = pt.sb("mean_var", [P, TILES, 2])
        var = pt.sb("var", [P, TILES])
        half = pt.sb("half", [P, TILES])
        stats_done, aggr_done, var_done, pow_done = (
            pt.sem("stats_done"), pt.sem("aggr_done"), pt.sem("var_done"), pt.sem("pow_done"))
        with nc.Block() as block:

            @block.vector
            def _(dve):
                with dve.Fori(0, TILES // TT) as i:
                    for k in range(TT):
                        t = bass.ds(i * TT + k, 1)
                        dve.bn_stats(stats[:, t, :].rearrange("p t k -> p (t k)"),
                                     H[:, t, :].rearrange("p t d -> p (t d)")).then_inc(stats_done, 1)
                for t in range(TILES):
                    if t % 16 == 0:
                        dve.wait_ge(stats_done, t + 16)
                    dve.bn_aggr(mean_var[:, t, :], stats[:, t, :]).then_inc(aggr_done, 1)
                dve.wait_ge(aggr_done, TILES)
                dve.memset(half[:, :], -0.5).then_inc(var_done, 1)
                dve.tensor_copy(mean[:, :], mean_var[:, :, 0])
                dve.tensor_scalar(var[:, :], mean_var[:, :, 1], EPS, None, ALU.add).then_inc(var_done, 1)

            @block.gpsimd
            def _(pool):
                pool.wait_ge(var_done, 2)
                pool.tensor_tensor(rstd[:, :], var[:, :], half[:, :], ALU.pow).then_inc(pow_done, 1)


def turned_norm(nc, name, H, idn, xT, add=False, twice=False, gamma_beta=None, store_to=None):
    levels = 2 if twice else 1
    with ExitStack() as part:
        pt = Store(nc, part, name)
        stats = pt.sb("stats", [P, levels, 2, TT, 6])
        mean_var = pt.sb("mean_var", [P, levels, 2, TT, 2])
        var = pt.sb("var", [P, levels, 2, TT])
        rstd = pt.sb("rstd", [P, levels, 2, TT])
        power = pt.sb("power", [P, TT])
        once = pt.sb("once", [P, 2, TT, D]) if twice else None
        rows = pt.sb("rows", [P, 2, TT, D])
        turned = pt.ps("turned", [C2, 2, 2, SEQ])
        steps = [pt.sem(f"steps{n}") for n in range(levels)]
        var_done = [pt.sem(f"var_done{n}") for n in range(levels)]
        pow_done = [pt.sem(f"pow_done{n}") for n in range(levels)]
        begun = pt.sem("begun")
        power_set, once_done, rows_done = pt.sem("power_set"), pt.sem("once_done"), pt.sem("rows_done")
        turned_done, copied, added = pt.sem("turned_done"), pt.sem("copied"), pt.sem("added")
        stored = [pt.sem("stored_even"), pt.sem("stored_odd")] if store_to is not None else None

        def turns(eng, statistics, middle, rows_of):
            lead = 2 if twice else 1

            def turn(g, half, more, mid):
                if more:
                    statistics(0, g + lead, (half + lead) % 2, 0)
                if twice and mid:
                    middle(g + 1, 1 - half)
                if more:
                    statistics(0, g + lead, (half + lead) % 2, 1)
                rows_of(g, half)
                if twice and mid:
                    statistics(1, g + 1, 1 - half, 1)

            for g in range(lead):
                for step in range(2):
                    statistics(0, g, g, step)
            if twice:
                middle(0, 0)
                statistics(1, 0, 0, 1)
            with eng.Fori(0, GROUPS // 2 - 1) as it:
                for half in range(2):
                    turn(it * 2 + half, half, True, True)
            turn(GROUPS - 2, 0, not twice, True)
            turn(GROUPS - 1, 1, False, False)

        with nc.Block() as block:

            @block.vector
            def _(dve):
                def source(g, k):
                    return H[:, bass.ds(g * TT + k, 1), :].rearrange("p t d -> p (t d)")

                def statistics(level, g, half, step):
                    if step == 0:
                        for k in range(TT):
                            src = once[:, half, k, :] if level else source(g, k)
                            dve.bn_stats(stats[:, level, half, k, :], src).then_inc(steps[level], 1)
                        return
                    dve.wait_ge(steps[level], g * (2 * TT) + TT)
                    dve.sem_inc(begun, 1)
                    for k in range(TT):
                        dve.bn_aggr(mean_var[:, level, half, k, :], stats[:, level, half, k, :]).then_inc(steps[level], 1)
                    dve.wait_ge(steps[level], g * (2 * TT) + 2 * TT)
                    dve.tensor_scalar(var[:, level, half, :], mean_var[:, level, half, :, 1], EPS, None, ALU.add).then_inc(var_done[level], 1)

                def scaled(level, g, half, k, dst, src):
                    return dve.tensor_scalar(dst, src, mean_var[:, level, half, k, 0:1], rstd[:, level, half, k:k + 1],
                                             ALU.subtract, ALU.mult)

                def add_rows(g, src):
                    dst = H[:, bass.ds(g * TT, TT), :]
                    dve.tensor_tensor(dst, dst, src, ALU.add).then_inc(added, 1)

                def middle(g, half):
                    dve.wait_ge(pow_done[0], g + 1)
                    if not is_number(g, 0):
                        dve.wait_ge(rows_done, g * TT - TT)
                    for k in range(TT):
                        scaled(0, g, half, k, once[:, half, k, :], source(g, k)).then_inc(once_done, 1)
                    dve.wait_ge(once_done, g * TT + TT)
                    add_rows(g, once[:, half, :, :])
                    statistics(1, g, half, 0)

                def rows_of(g, half):
                    level = levels - 1
                    dve.wait_ge(pow_done[level], g + 1)
                    dve.wait_ge(turned_done, g)
                    if store_to is not None and not (isinstance(g, int) and g < 2):
                        dve.wait_ge(stored[half], (g - half) * 8)
                    for k in range(TT):
                        src = once[:, half, k, :] if twice else source(g, k)
                        scaled(level, g, half, k, rows[:, half, k, :], src).then_inc(rows_done, 1)
                    if add:
                        dve.wait_ge(rows_done, g * TT + TT)
                        add_rows(g, rows[:, half, :, :])

                turns(dve, statistics, middle, rows_of)

            @block.gpsimd
            def _(pool):
                def power_of(level, g, half):
                    pool.wait_ge(var_done[level], g + 1)
                    pool.tensor_tensor(rstd[:, level, half, :], var[:, level, half, :], power[:, :], ALU.pow).then_inc(pow_done[level], 1)

                pool.memset(power[:, :], -0.5).then_inc(power_set, 1)
                pool.wait_ge(power_set, 1)
                turns(pool, lambda level, g, half, step: power_of(level, g, half) if step else None,
                      lambda g, half: None, lambda g, half: None)

            @block.tensor
            def _(pe):
                pe.sem_inc(turned_done, 1)
                with pe.Fori(0, GROUPS // 2) as it:
                    for half in range(2):
                        g = it * 2 + half
                        pe.wait_ge(rows_done, g * TT + TT)
                        pe.wait_ge(copied, g * 2)
                        for c in range(2):
                            for k in range(TT):
                                last = pe.transpose(turned[:, half, c, P * k:P * k + P], rows[:, half, k, C2 * c:C2 * c + C2],
                                                    idn[:, :])
                        last.then_inc(turned_done, 1)

            @block.scalar
            def _(act):
                act.sem_inc(copied, 2)
                with act.Fori(0, GROUPS // 2) as it:
                    for half in range(2):
                        g = it * 2 + half
                        act.wait_ge(turned_done, g + 2)
                        for c in range(2):
                            dst = xT[:, c, bass.ds(g * SEQ, SEQ)]
                            if gamma_beta is None:
                                act.activation(dst, turned[:, half, c, :], ACT.Copy).then_inc(copied, 1)
                            else:
                                act.activation(dst, turned[:, half, c, :], ACT.Identity, bias=gamma_beta[:, c, 1:2],
                                               scale=gamma_beta[:, c, 0:1]).then_inc(copied, 1)

            if store_to is not None:

                @block.sync
                def _(sp):
                    with sp.Fori(0, GROUPS // 2) as it:
                        for half in range(2):
                            g = it * 2 + half
                            sp.wait_ge(rows_done, g * TT + TT)
                            sp.dma_start(store_to[bass.ds(g * SEQ, SEQ), :].rearrange("(k p) d -> p k d", p=P),
                                         rows[:, half, :, :]).then_inc(stored[half], 16)
                    for half in range(2):
                        sp.wait_ge(stored[half], 16 * (GROUPS // 2))


def feed_forward(nc, name, H, xT, experts, hidden, w_in, w_out, func, bias=None, gates=None):
    M = hidden // P
    PAIRS = GROUPS // 2
    with ExitStack() as part:
        pt = Store(nc, part, name)
        copies = min(2, experts)
        w1 = pt.sb("w1", [C2, copies, 2, hidden])
        w2 = pt.sb("w2", [P, copies, M, D])
        hid = pt.sb("hid", [P, 2, M, SEQ])
        hid_ps = pt.ps("hid_ps", [P, 4, SEQ])
        out_ps = pt.ps("out_ps", [P, 2, 2, SEQ])
        w_in_sem = [pt.sem(f"weights_in{c}") for c in range(copies)]
        hid_done, func_done, out_done, added = (
            pt.sem("hid_done"), pt.sem("func_done"), pt.sem("out_done"), pt.sem("added"))
        with nc.Block() as block:

            def over_experts(eng, body):
                if experts == 1:
                    body(0, 0)
                else:
                    with eng.Fori(0, experts // 2) as pair:
                        for c in range(2):
                            body(pair * 2 + c, c)

            @block.sync
            def _(sp):
                def load(e, c):
                    sp.dma_start(w1[:, c, :, :], w_in(e)).then_inc(w_in_sem[c], 16)
                    sp.dma_start(w2[:, c, :, :], w_out(e)).then_inc(w_in_sem[c], 16)

                for c in range(copies):
                    load(c, c)
                if experts > 2:
                    with sp.Fori(0, experts // 2 - 1) as pair:
                        for c in range(2):
                            e = pair * 2 + c
                            sp.wait_ge(out_done, e * GROUPS + GROUPS + 1)
                            load(e + 2, c)

            @block.tensor
            def _(pe):
                def first(e, c, g, half):
                    n = e * GROUPS + g
                    for m in range(M):
                        at = (half * M + m) % 4
                        pe.wait_ge(func_done, n * M + m)
                        for k in range(2):
                            last = pe.matmul(hid_ps[:, at, :], w1[:, c, k, P * m:P * m + P], xT[:, k, bass.ds(g * SEQ, SEQ)],
                                             start=(k == 0), stop=(k == 1))
                        last.then_inc(hid_done, 1)

                def second(e, c, g, half):
                    n = e * GROUPS + g
                    pe.wait_ge(func_done, n * M + M + 3)
                    pe.wait_ge(added, n * TT)
                    for k in range(TT):
                        for m in range(M):
                            last = pe.matmul(out_ps[:, half, k // 2, D * (k % 2):D * (k % 2) + D], hid[:, half, m, P * k:P * k + P],
                                             w2[:, c, m, :], start=(m == 0), stop=(m == M - 1))
                    last.then_inc(out_done, 1)

                def expert(e, c):
                    pe.wait_ge(w_in_sem[c], (e - c) * 16 + 32 if experts > 1 else 32)
                    first(e, c, 0, 0)
                    with pe.Fori(0, PAIRS - 1) as it:
                        first(e, c, it * 2 + 1, 1)
                        second(e, c, it * 2, 0)
                        first(e, c, it * 2 + 2, 0)
                        second(e, c, it * 2 + 1, 1)
                    first(e, c, GROUPS - 1, 1)
                    second(e, c, GROUPS - 2, 0)
                    second(e, c, GROUPS - 1, 1)

                pe.sem_inc(out_done, 1)
                over_experts(pe, expert)

            @block.scalar
            def _(act):
                def group(n, half):
                    act.wait_ge(out_done, n)
                    for m in range(M):
                        act.wait_ge(hid_done, n * M + m + 1)
                        if bias is None:
                            act.activation(hid[:, half, m, :], hid_ps[:, (half * M + m) % 4, :], func).then_inc(func_done, 1)
                        else:
                            act.activation(hid[:, half, m, :], hid_ps[:, (half * M + m) % 4, :], func,
                                           bias=bias[:, m:m + 1]).then_inc(func_done, 1)

                act.sem_inc(func_done, 3)
                with act.Fori(0, experts * PAIRS) as it:
                    for half in range(2):
                        group(it * 2 + half, half)

            @block.vector
            def _(dve):
                def expert(e, c):
                    with dve.Fori(0, PAIRS) as it:
                        for half in range(2):
                            g = it * 2 + half
                            n = e * GROUPS + g
                            dve.wait_ge(out_done, n + 2)
                            for k in range(TT):
                                dst = H[:, bass.ds(g * TT + k, 1), :].rearrange("p t d -> p (t d)")
                                out = out_ps[:, half, k // 2, D * (k % 2):D * (k % 2) + D]
                                if gates is None:
                                    dve.tensor_tensor(dst, out, dst, ALU.add).then_inc(added, 1)
                                else:
                                    gate = gates[:, bass.ds((g * TT + k) * experts + e, 1)]
                                    dve.scalar_tensor_tensor(dst, out, gate, dst, ALU.mult, ALU.add).then_inc(added, 1)

                dve.sem_inc(added, TT)
                over_experts(dve, expert)


WIN = 5
COLS = P // NB
SPAN = COLS + WIN - 1
KEYS = NB * SPAN
HID = 96
HEADS, DH = 4, 24
RPB = 2 * WIN - 1
UROWS = 2 * NB - 1


def neighborhood_stage(nc, h1, h2, weights, turned, small, const):
    fc1_b, convA_b, convB_b, qkv_b, rpb, proj_b, fc2_b = weights
    fc1_t, convA_t, convB_t, qkv_t, proj_t, fc2_t = turned
    shifts = small
    with ExitStack() as stage:
        st = Store(nc, stage, "near")
        H = st.sb("H", [P, TILES, D])
        idn = st.sb("idn", [P, P])
        xs = st.sb("xs", [HID + 1, NB, SEQ + WIN - 1])
        table = st.sb("table", [P, 3, HEADS, KEYS])
        in_sem, out_sem, zero_done = st.sem("in"), st.sem("out"), st.sem("zero_done")

        with ExitStack() as part:
            pt = Store(nc, part, "near_load")
            bias = pt.sb("bias", [P, HEADS, KEYS])
            mask = pt.sb("mask", [P, 3, KEYS])
            zeros = pt.sb("zeros", [HID, COLS * HEADS * UROWS * SPAN // HID])
            shifted = pt.sem("shifted")
            with nc.Block() as block:

                @block.gpsimd
                def _(pool):
                    pool.memset(zeros[:, :], 0.0).then_inc(zero_done, 1)
                    pool.memset(xs[0:HID, :, :].rearrange("p b w -> p (b w)"), 0.0).then_inc(zero_done, 1)
                    pool.memset(xs[HID:, :, :].rearrange("p b w -> p (b w)"), 1.0).then_inc(zero_done, 1)

                @block.sync
                def _(sp):
                    for b in range(NB):
                        sp.dma_start(H[COLS * b:COLS * b + COLS, :, :],
                                     h1[SEQ * b:SEQ * b + SEQ, :].rearrange("(j w) d -> w j d", w=COLS)).then_inc(in_sem, 16)
                    sp.dma_start(idn[:, :], const["ident"]).then_inc(in_sem, 16)
                    sp.dma_start(mask[:, :, :], const["near_mask"].rearrange("p (v k) -> p v k", v=3)).then_inc(in_sem, 16)
                    sp.wait_ge(zero_done, 1)
                    sp.dma_start(shifts.rearrange("w n u c -> (w n u c)").rearrange("(p k) -> p k", p=HID),
                                 zeros[:, :]).then_inc(shifted, 16)
                    sp.wait_ge(shifted, 16)
                    half = WIN // 2
                    for w in range(COLS):
                        c0, c1 = max(0, w - half), min(SPAN, w + half + WIN)
                        r0 = c0 - half - w + WIN - 1
                        sp.dma_start(shifts[w, :, NB - WIN:NB - WIN + RPB, c0:c1], rpb[:, :, r0:r0 + c1 - c0]).then_inc(shifted, 16)
                    sp.wait_ge(shifted, 16 * (1 + COLS))
                    for b in range(NB):
                        sp.dma_start(bias[COLS * b:COLS * b + COLS, :, :].rearrange("w n (b c) -> w n b c", b=NB),
                                     shifts[:, :, NB - 1 - b:2 * NB - 1 - b, :]).then_inc(in_sem, 16)
                    sp.wait_ge(in_sem, 16 * (2 * NB + 2))

                @block.vector
                def _(dve):
                    dve.wait_ge(in_sem, 16 * (2 * NB + 2))
                    for v in range(3):
                        dve.tensor_tensor(table[:, v, :, :], bias[:, :, :],
                                          mask[:, v, :].unsqueeze(1).to_broadcast([P, HEADS, KEYS]), ALU.add)

        with ExitStack() as part:
            pt = Store(nc, part, "near_in")
            xT = pt.sb("xT", [C2, 2, TOKENS])
            turned_norm(nc, "near_norm", H, idn, xT, add=True)
            CA = 64
            w1 = pt.sb("w1", [C2, 2, HID])
            wa = pt.sb("wa", [HID, CA])
            wb = pt.sb("wb", [CA, HID])
            b1 = pt.sb("b1", [HID, 1])
            ba = pt.sb("ba", [CA, 1])
            bb = pt.sb("bb", [HID, 1])
            x1 = pt.sb("x1", [HID, 2, SEQ])
            mid = pt.sb("mid", [CA, 2, SEQ])
            total = pt.sb("total", [HID, 2, SEQ])
            x1_ps = pt.ps("x1_ps", [HID, 2, SEQ])
            mid_ps = pt.ps("mid_ps", [CA, 2, SEQ])
            total_ps = pt.ps("total_ps", [HID, 2, SEQ])
            loaded, x1_done, x1_copied = pt.sem("loaded"), pt.sem("x1_done"), pt.sem("x1_copied")
            mid_done, mid_copied = pt.sem("mid_done"), pt.sem("mid_copied")
            total_done, summed, gelu_done = pt.sem("total_done"), pt.sem("summed"), pt.sem("gelu_done")
            nc.scalar.preload_act_table(ACT.Gelu)
            with nc.Block() as block:

                @block.sync
                def _(sp):
                    sp.dma_start(w1[:, :, :], fc1_t).then_inc(loaded, 16)
                    sp.dma_start(wa[:, :], convA_t.rearrange("p a n -> p (a n)")).then_inc(loaded, 16)
                    sp.dma_start(wb[:, :], convB_t.rearrange("p a n -> p (a n)")).then_inc(loaded, 16)
                    for dst, src in ((b1, fc1_b), (ba, convA_b), (bb, convB_b)):
                        sp.dma_start(dst[:, :], src.rearrange("(p a) -> p a", a=1)).then_inc(loaded, 16)
                    sp.wait_ge(loaded, 16 * 6)

                @block.tensor
                def _(pe):
                    def front(g, half):
                        pe.wait_ge(x1_copied, g)
                        for c in range(2):
                            last = pe.matmul(x1_ps[:, half, :], w1[:, c, :], xT[:, c, bass.ds(g * SEQ, SEQ)], start=(c == 0), stop=(c == 1))
                        last.then_inc(x1_done, 1)

                    def middle(g, half):
                        pe.wait_ge(x1_copied, g + 3)
                        pe.wait_ge(mid_copied, g)
                        pe.matmul(mid_ps[:, half, :], wa[:, :], x1[:, half, :], start=True, stop=True).then_inc(mid_done, 1)

                    def back(g, half):
                        pe.wait_ge(mid_copied, g + 3)
                        pe.wait_ge(summed, g)
                        pe.matmul(total_ps[:, half, :], wb[:, :], mid[:, half, :], start=True, stop=True).then_inc(total_done, 1)

                    pe.wait_ge(loaded, 16 * 6)
                    front(0, 0)
                    middle(0, 0)
                    with pe.Fori(0, GROUPS // 2 - 1) as it:
                        for half in (1, 0):
                            g = it * 2 + (1 if half else 2)
                            front(g, half)
                            back(it * 2 + (0 if half else 1), 1 - half)
                            middle(g, half)
                    front(GROUPS - 1, 1)
                    back(GROUPS - 2, 0)
                    middle(GROUPS - 1, 1)
                    back(GROUPS - 1, 1)

                @block.scalar
                def _(act):
                    act.wait_ge(loaded, 16 * 6)
                    act.sem_inc(x1_copied, 2)
                    act.sem_inc(gelu_done, 2)

                    def front(g, half):
                        act.wait_ge(x1_done, g + 1)
                        act.wait_ge(summed, g)
                        act.activation(x1[:, half, :], x1_ps[:, half, :], ACT.Identity, bias=b1[:, :]).then_inc(x1_copied, 1)

                    def last(g, half):
                        act.wait_ge(summed, g + 3)
                        act.activation(xs[0:HID, :, bass.ds(g * (TT * COLS) + WIN // 2, TT * COLS)].rearrange("p b (k w) -> p k b w", k=TT),
                                       total[:, half, :].rearrange("p (k b w) -> p k b w", k=TT, b=NB), ACT.Gelu).then_inc(gelu_done, 1)

                    front(0, 0)
                    with act.Fori(0, GROUPS // 2 - 1) as it:
                        for half in (1, 0):
                            front(it * 2 + (1 if half else 2), half)
                            last(it * 2 + (0 if half else 1), 1 - half)
                    front(GROUPS - 1, 1)
                    last(GROUPS - 2, 0)
                    last(GROUPS - 1, 1)

                @block.vector
                def _(dve):
                    dve.wait_ge(loaded, 16 * 6)
                    dve.sem_inc(mid_copied, 2)
                    dve.sem_inc(summed, 2)

                    def middle(g, half):
                        dve.wait_ge(mid_done, g + 1)
                        dve.tensor_scalar(mid[:, half, :], mid_ps[:, half, :], ba[:, :], None, ALU.add).then_inc(mid_copied, 1)

                    def last(g, half):
                        dve.wait_ge(total_done, g + 1)
                        dve.wait_ge(gelu_done, g)
                        dve.scalar_tensor_tensor(total[:, half, :], total_ps[:, half, :], bb[:, :], x1[:, half, :],
                                                 ALU.add, ALU.add).then_inc(summed, 1)

                    middle(0, 0)
                    with dve.Fori(0, GROUPS // 2 - 1) as it:
                        for half in (1, 0):
                            last(it * 2 + (0 if half else 1), 1 - half)
                            middle(it * 2 + (1 if half else 2), half)
                    last(GROUPS - 2, 0)
                    middle(GROUPS - 1, 1)
                    last(GROUPS - 1, 1)

        with ExitStack() as part:
            pt = Store(nc, part, "near_att")
            wq = pt.sb("wq", [HID + 1, HEADS, PAD])
            wk = pt.sb("wk", [HID + 1, HEADS, PAD])
            wv = pt.sb("wv", [HID + 1, HEADS, PAD])
            wp = pt.sb("wp", [HID + 1, HID])
            w2 = pt.sb("w2", [HID + 1, D])
            xw = pt.sb("xw", [HID + 1, 2, KEYS])
            q_t = pt.sb("q_t", [P, 2, P])
            k_diag = pt.sb("k_diag", [P, 2, HEADS, KEYS])
            v = pt.sb("v", [KEYS // 2, 2, 2, HEADS * PAD])
            logits = pt.sb("logits", [P, HEADS, KEYS])
            shifted = pt.sb("shifted", [P, HEADS, KEYS])
            probs = pt.sb("probs", [P, 2, HEADS, KEYS])
            high = pt.sb("high", [P, HEADS])
            recip = pt.sb("recip", [P, HEADS])
            probs_t = pt.sb("probs_t", [KEYS // 2, 2, TT, P])
            raw = pt.sb("raw", [P, P])
            att = pt.sb("att", [P, HEADS, DH])
            att_t = pt.sb("att_t", [HID + 1, P])
            proj = pt.sb("proj", [HID + 1, P])
            qk_ps = pt.ps("qk_ps", [P, SEQ])
            v_ps = pt.ps("v_ps", [P, SEQ])
            logits_ps = pt.ps("logits_ps", [P, 2, SEQ])
            turned_ps = pt.ps("turned_ps", [KEYS // 2, 2, SEQ])
            att_ps = pt.ps("att_ps", [P, 4, P])
            out_ps = pt.ps("out_ps", [P, SEQ])
            loaded, zeroed = pt.sem("loaded"), pt.sem("zeroed")
            xw_done, qkv_done, qk_copied, v_copied = (
                pt.sem("xw_done"), pt.sem("qkv_done"), pt.sem("qk_copied"), pt.sem("v_copied"))
            logits_done, logits_read = pt.sem("logits_done"), pt.sem("logits_read")
            max_done, shifted_done, exp_done = pt.sem("max_done"), pt.sem("shifted_done"), pt.sem("exp_done")
            turned_done, turned_copied = pt.sem("turned_done"), pt.sem("turned_copied")
            pv_done, att_done, own = pt.sem("pv_done"), pt.sem("att_done"), pt.sem("own")
            raw_copied, end_done, end_copied, added = (
                pt.sem("raw_copied"), pt.sem("end_done"), pt.sem("end_copied"), pt.sem("added"))
            SCALE = DH ** -0.5
            LOADS = 10
            HALF = KEYS // 2
            with nc.Block() as block:

                @block.sync
                def _(sp):
                    sp.wait_ge(zeroed, 5)
                    for m, dst in enumerate((wq, wk, wv)):
                        sp.dma_start(dst[0:HID, :, 0:DH], qkv_t[:, 0, HID * m:HID * m + HID].rearrange("p (h c) -> p h c", h=HEADS)).then_inc(loaded, 16)
                        sp.dma_start(dst[HID:, :, 0:DH], qkv_b[HID * m:HID * m + HID].rearrange("(a h c) -> a h c", a=1, h=HEADS)).then_inc(loaded, 16)
                    sp.dma_start(wp[0:HID, :], proj_t.rearrange("p a n -> p (a n)")).then_inc(loaded, 16)
                    sp.dma_start(wp[HID:, :], proj_b.rearrange("(a n) -> a n", a=1)).then_inc(loaded, 16)
                    sp.dma_start(w2[0:HID, :], fc2_t.rearrange("p a n -> p (a n)")).then_inc(loaded, 16)
                    sp.dma_start(w2[HID:, :], fc2_b.rearrange("(a n) -> a n", a=1)).then_inc(loaded, 16)
                    sp.wait_ge(loaded, 16 * LOADS)

                @block.gpsimd
                def _(pool):
                    for w in (wq, wk):
                        pool.memset(w[:, :, :].rearrange("p h c -> p (h c)"), 0.0).then_inc(zeroed, 1)
                    pool.memset(wv[:, :, :].rearrange("p h c -> p (h c)"), 0.0).then_inc(zeroed, 1)
                    pool.memset(k_diag[:, :, :, :].rearrange("p a h k -> p (a h k)"), 0.0).then_inc(zeroed, 1)
                    pool.wait_ge(zeroed, 4)
                    pool.memset(wv[HID:, :, DH:DH + 1], 1.0).then_inc(zeroed, 1)
                    pool.memset(att_t[HID:, :], 1.0).then_inc(zeroed, 1)
                    pool.memset(proj[HID:, :], 1.0).then_inc(zeroed, 1)

            with nc.Block() as block:

                def turns(eng, fronts, turn):
                    fronts()
                    turn(0, 0, 1)
                    with eng.Fori(0, TILES // 2 - 2) as it:
                        turn(it * 2 + 1, 1, 1)
                        turn(it * 2 + 2, 0, 1)
                    turn(TILES - 3, 1, 2)
                    turn(TILES - 2, 0, None)
                    turn(TILES - 1, 1, None)

                @block.gpsimd
                def _(pool):
                    def window(j, half):
                        pool.tensor_copy(xw[:, half, :].rearrange("p (b c) -> p b c", b=NB), xs[:, :, bass.ds(j * COLS, SPAN)]).then_inc(xw_done, 1)

                    def subtract(j):
                        pool.wait_ge(max_done, j + 1)
                        pool.wait_ge(exp_done, j)
                        pool.tensor_tensor(shifted[:, :, :], logits[:, :, :],
                                           high[:, :].unsqueeze(2).to_broadcast([P, HEADS, KEYS]), ALU.subtract).then_inc(shifted_done, 1)

                    def turn(j, half, variant):
                        if variant is not None:
                            if variant == 1:
                                pool.wait_ge(qkv_done, j + 2)
                                window(j + 3, 1 - half)
                            subtract(j + 2)

                    def fronts():
                        window(0, 0)
                        window(1, 1)
                        pool.wait_ge(qkv_done, 1)
                        window(2, 0)
                        subtract(0)
                        subtract(1)

                    turns(pool, fronts, turn)

                @block.tensor
                def _(pe):
                    def project(j, half):
                        pe.wait_ge(xw_done, j + 1)
                        pe.wait_ge(qk_copied, j * 3)
                        pe.wait_ge(v_copied, j)
                        inner = xw[:, half, :].rearrange("p (b c) -> p b c", b=NB)[:, :, WIN // 2:WIN // 2 + COLS]
                        pe.matmul(qk_ps[:, 0:P], wq[:, :, :].rearrange("p h c -> p (h c)"), inner, start=True, stop=True)
                        pe.matmul(qk_ps[:, P:P + KEYS], wk[:, :, :].rearrange("p h c -> p (h c)"), xw[:, half, :], start=True, stop=True)
                        for m in range(2):
                            last = pe.matmul(v_ps[0:HALF, P * m:P * m + P], xw[:, half, HALF * m:HALF * m + HALF],
                                             wv[:, :, :].rearrange("p h c -> p (h c)"), start=True, stop=True)
                        last.then_inc(qkv_done, 1)

                    def scores(j, half):
                        pe.wait_ge(qk_copied, j * 3 + 3)
                        pe.wait_ge(logits_read, j)
                        for m in range(2):
                            last = pe.matmul(logits_ps[:, m, 0:2 * KEYS], q_t[:, half, :],
                                             k_diag[:, half, 2 * m:2 * m + 2, :].rearrange("p h k -> p (h k)"), start=True, stop=True)
                        last.then_inc(logits_done, 1)

                    def fronts():
                        for j in range(2):
                            project(j, j)
                            scores(j, j)

                    def turn_out(j):
                        pe.wait_ge(raw_copied, j)
                        pe.transpose(att_ps[:, 1, :], raw[:, :], idn[:, :]).then_inc(end_done, 1)

                    def turn_back(j):
                        pe.wait_ge(att_done, j)
                        pe.transpose(att_ps[0:HID, 2, :], att[:, :, :].rearrange("p h c -> p (h c)"), idn[:, :]).then_inc(end_done, 1)

                    def project_out(j):
                        pe.wait_ge(end_copied, j * 2 - 1)
                        pe.wait_ge(added, j - 1)
                        pe.matmul(out_ps[0:HID, 0:P], wp[:, :], att_t[:, :], start=True, stop=True).then_inc(end_done, 1)

                    def widen(j):
                        pe.wait_ge(end_copied, j * 2)
                        pe.matmul(out_ps[:, P:P + D], proj[:, :], w2[:, :], start=True, stop=True).then_inc(end_done, 1)

                    def turn(j, half, variant):
                        has_end = not is_number(j, 0)
                        if has_end:
                            turn_out(j)
                        pe.wait_ge(exp_done, j + 1)
                        for m in range(2):
                            pe.wait_ge(turned_copied, j * 2 + m)
                            for h in range(HEADS):
                                last = pe.transpose(turned_ps[:, m, P * h:P * h + P], probs[:, half, h, HALF * m:HALF * m + HALF], idn[:, :])
                            last.then_inc(turned_done, 1)
                        if variant is not None:
                            project(j + 2, half)
                        if has_end:
                            turn_back(j)
                        pe.wait_ge(turned_copied, j * 2 + 2)
                        if has_end:
                            pe.wait_ge(end_copied, j * 2 - 1)
                        for m in range(2):
                            for h in range(HEADS):
                                last = pe.matmul(att_ps[PAD * h:PAD * h + PAD, 0, :], v[:, half, m, PAD * h:PAD * h + PAD],
                                                 probs_t[:, m, h, :], start=(m == 0), stop=(m == 1))
                        last.then_inc(pv_done, 1)
                        if has_end:
                            project_out(j)
                        if variant is not None:
                            scores(j + 2, half)
                        if has_end:
                            widen(j)

                    turns(pe, fronts, turn)
                    turn_out(TILES)
                    turn_back(TILES)
                    project_out(TILES)
                    widen(TILES)

                @block.scalar
                def _(act):
                    def qk_copies(j, half):
                        act.wait_ge(qkv_done, j + 1)
                        if not (isinstance(j, int) and j < 2):
                            act.wait_ge(logits_done, j - 1)
                        act.activation(q_t[:, half, :], qk_ps[:, 0:P], ACT.Copy).then_inc(qk_copied, 1)
                        for h in range(HEADS):
                            rows_h = slice(PAD * h, PAD * h + PAD)
                            ins = act.activation(k_diag[rows_h, half, h, :], qk_ps[rows_h, P:P + KEYS], ACT.Copy)
                            if h % 2:
                                ins.then_inc(qk_copied, 1)

                    def v_copies(j, half):
                        act.activation(v[:, half, :, :].rearrange("p m c -> p (m c)"), v_ps[0:HALF, 0:2 * P], ACT.Copy).then_inc(v_copied, 1)

                    def exponentials(j, half):
                        act.wait_ge(shifted_done, j + 1)
                        act.activation(probs[:, half, :, :], shifted[:, :, :], ACT.Exp).then_inc(exp_done, 1)

                    def fronts():
                        for j in range(2):
                            qk_copies(j, j)
                            v_copies(j, j)
                        exponentials(0, 0)

                    def copy_back(j):
                        act.wait_ge(end_done, j * 4 - 2)
                        act.activation(att_t[0:HID, :], att_ps[0:HID, 2, :], ACT.Copy).then_inc(end_copied, 1)

                    def copy_projection(j):
                        act.wait_ge(end_done, j * 4 - 1)
                        act.activation(proj[0:HID, :], out_ps[0:HID, 0:P], ACT.Copy).then_inc(end_copied, 1)

                    def turn(j, half, variant):
                        has_end = not is_number(j, 0)
                        for m in range(2):
                            act.wait_ge(turned_done, j * 2 + m + 1)
                            act.activation(probs_t[:, m, :, :].rearrange("p h q -> p (h q)"), turned_ps[:, m, :], ACT.Copy).then_inc(turned_copied, 1)
                        if variant is not None:
                            qk_copies(j + 2, half)
                        if has_end:
                            copy_back(j)
                        if not is_number(j, TILES - 1):
                            exponentials(j + 1, 1 - half)
                        act.wait_ge(pv_done, j + 1)
                        if variant is not None:
                            v_copies(j + 2, half)
                        act.activation(raw[:, :], att_ps[:, 0, :], ACT.Copy).then_inc(raw_copied, 1)
                        if has_end:
                            copy_projection(j)

                    turns(act, fronts, turn)
                    copy_back(TILES)
                    copy_projection(TILES)

                @block.vector
                def _(dve):
                    def scores(j, half, variant):
                        dve.wait_ge(logits_done, j + 1)
                        dve.wait_ge(shifted_done, j)
                        dve.scalar_tensor_tensor(logits[:, :, :].rearrange("p (m h) k -> p m (h k)", m=2), logits_ps[:, :, 0:2 * KEYS], SCALE,
                                                 table[:, variant, :, :].rearrange("p (m h) k -> p m (h k)", m=2),
                                                 ALU.mult, ALU.add).then_inc(logits_read, 1)
                        dve.wait_ge(logits_read, j + 1)
                        dve.tensor_reduce(high[:, :], logits[:, :, :], AX.X, ALU.max).then_inc(max_done, 1)

                    def normalise(j):
                        dve.wait_ge(end_done, j * 4 - 3)
                        sums = att_ps[:, 1, :].rearrange("p (h c) -> p h c", h=HEADS)
                        dve.reciprocal(recip[:, :], sums[:, :, DH]).then_inc(own, 1)
                        dve.wait_ge(own, j)
                        dve.tensor_tensor(att[:, :, :], sums[:, :, 0:DH], recip[:, :].unsqueeze(2).to_broadcast([P, HEADS, DH]),
                                          ALU.mult).then_inc(att_done, 1)

                    def add(j):
                        dve.wait_ge(end_done, j * 4)
                        dst = H[:, bass.ds(j - 1, 1), :].rearrange("p t d -> p (t d)")
                        dve.tensor_tensor(dst, out_ps[:, P:P + D], dst, ALU.add).then_inc(added, 1)

                    def fronts():
                        scores(0, 0, 0)
                        scores(1, 1, 1)

                    def turn(j, half, variant):
                        if not is_number(j, 0):
                            normalise(j)
                        if variant is not None:
                            scores(j + 2, half, variant)
                        if not is_number(j, 0):
                            add(j)

                    turns(dve, fronts, turn)
                    normalise(TILES)
                    add(TILES)

                @block.sync
                def _(sp):
                    sp.wait_ge(added, TILES)
                    for b in range(NB):
                        sp.dma_start(h2[SEQ * b:SEQ * b + SEQ, :].rearrange("(j w) d -> w j d", w=COLS),
                                     H[COLS * b:COLS * b + COLS, :, :]).then_inc(out_sem, 16)
                    sp.wait_ge(out_sem, 16 * NB)


def dense_stage(nc, H, idn, in_weight_t, in_bias, out_weight):
    hidden = in_bias.shape[0]
    with ExitStack() as stage:
        st = Store(nc, stage, "dense_ffn")
        xT = st.sb("xT", [C2, 2, TOKENS])
        bias = st.sb("bias", [P, hidden // P])
        turned_norm(nc, "ffn_norm", H, idn, xT)
        bias_in = st.sem("bias_in")
        with nc.Block() as block:

            @block.sync
            def _(sp):
                with nc.allow_non_contiguous_dma(reason="one bias per partition"):
                    sp.dma_start(bias[:, :], in_bias.rearrange("(m p) -> p m", p=P)).then_inc(bias_in, 16)
                sp.wait_ge(bias_in, 16)

        feed_forward(nc, "ffn", H, xT, 1, hidden, lambda e: in_weight_t,
                     lambda e: out_weight.rearrange("(m p) d -> p m d", p=P), ACT.Gelu, bias=bias)


def turned_weights(nc, weights, ident):
    steps, outs = [], []
    with ExitStack() as part:
        pt = Store(nc, part, "turn_weights")
        idn = pt.sb("idn", [P, P])
        for i, weight in enumerate(weights):
            rows, cols = weight.shape
            n = max(1, -(-cols // P))
            size = cols // n
            out = nc.dram_tensor(f"turned_weight{i}", (size, n, rows), F32).ap()
            tiles = [(r, min(P, rows - r)) for r in range(0, rows, P)]
            w = pt.sb(f"w{i}", [P, len(tiles), cols])
            wT = pt.sb(f"wT{i}", [size, n, rows])
            steps += [(w, wT, t, r, m, c, size) for t, (r, m) in enumerate(tiles) for c in range(n)]
            outs.append((weight, w, wT, out, tiles, len(steps)))
        ps = pt.ps("ps", [P, 2, SEQ])
        loaded, turned, copied, stored = pt.sem("loaded"), pt.sem("turned"), pt.sem("copied"), pt.sem("stored")
        loads = 1 + sum(len(tiles) for *_, tiles, _ in outs)
        with nc.Block() as block:

            @block.sync
            def _(sp):
                sp.dma_start(idn[:, :], ident).then_inc(loaded, 16)
                for weight, w, _, _, tiles, _ in outs:
                    for t, (r, m) in enumerate(tiles):
                        sp.dma_start(w[0:m, t, :], weight[r:r + m, :]).then_inc(loaded, 16)
                for _, _, wT, out, _, end in outs:
                    sp.wait_ge(copied, end)
                    sp.dma_start(out, wT[:, :, :]).then_inc(stored, 16)
                sp.wait_ge(stored, 16 * len(outs))

            @block.tensor
            def _(pe):
                pe.wait_ge(loaded, 16 * loads)
                for j, (w, _, t, _, m, c, size) in enumerate(steps):
                    if j >= 2:
                        pe.wait_ge(copied, j - 1)
                    pe.transpose(ps[0:size, j % 2, 0:m], w[0:m, t, size * c:size * c + size], idn[0:m, 0:m]).then_inc(turned, 1)

            @block.vector
            def _(dve):
                for j, (_, wT, _, r, m, c, size) in enumerate(steps):
                    dve.wait_ge(turned, j + 1)
                    dve.tensor_copy(wT[:, c, r:r + m], ps[0:size, j % 2, 0:m]).then_inc(copied, 1)
    return [out for _, _, _, out, _, _ in outs]


SETS = 64


def sets_stage(nc, H, idn, wqkv_t, wproj_t, wv_t, bv, const):
    HH = HD * HD
    SCALE = 0.25
    assert SCALE == HD ** -0.5
    BATCHES = NH // 2
    X, QT, OUT, OT, PT, VT, TURN = 0, 1, 2, (3, 4, 5, 6, 7, 8), (9, 10), 11, 12
    KSUM, VSUM = TT * TURN, TT * TURN + 1
    PER_SEQ = TT * TURN + 2
    DVE_BATCHES = 4
    with ExitStack() as stage:
        st = Store(nc, stage, "sets")
        mean = st.sb("mean", [P, TILES])
        rstd = st.sb("rstd", [P, TILES])
        wqkv = st.sb("wqkv", [C2, 2, 3 * D])
        wproj = st.sb("wproj", [C2, 2, D])
        wv = st.sb("wv", [P, 2, PAD])
        bias = st.sb("bias", [P, 1])
        setm = st.sb("setm", [P, TT, P])
        tri = st.sb("tri", [P, P])
        mask = st.sb("mask", [P, TT, SETS])
        rows = st.sb("rows", [P, 2, D])
        xs = st.sb("xs", [C2, 2, 2, P])
        qk = st.sb("qk", [P, 2, TT, 2, NH, PAD])
        v0 = st.sb("v0", [P, 2, NH, HD])
        v = st.sb("v", [P, 2, TT, NH, PAD])
        v_t = st.sb("v_t", [P, NG, P])
        outer = st.sb("outer", [P, 2, NH, HH])
        outer_t = st.sb("outer_t", [P, 2, 2 * NH, P])
        k_diag = st.sb("k_diag", [P, 2, NG, GH * SETS])
        v_diag = st.sb("v_diag", [P, 2, NH // 2, 2, HD + 1])
        q_t = st.sb("q_t", [P, 2, NG, P])
        logits = st.sb("logits", [P, NH, SETS])
        shifted = st.sb("shifted", [P, NH, SETS])
        probs = st.sb("probs", [P, 2, NH, SETS])
        probs_t = st.sb("probs_t", [P, NH // 2, P])
        q_tail = st.sb("q_tail", [P, NH, HD])
        tail = st.sb("tail", [P, NH])
        high = st.sb("high", [P, NH])
        recip = st.sb("recip", [P, NH])
        out = st.sb("out", [P, NH, HD])
        out_n = st.sb("out_n", [P, NH, HD])
        out_t = st.sb("out_t", [C2, 2, P])
        row_statistics(nc, H, mean, rstd)
        logits_ps = st.ps("logits_ps", [P, 2, SEQ])
        tails_ps = st.ps("tails_ps", [P, SEQ])
        qk_ps = st.ps("qk_ps", [P, SEQ])
        v0_ps = logits_ps[:, 1, 256:256 + D]
        v_ps = st.ps("v_ps", [P, 4, P])[:, 0:NG, :]
        ring = st.ps("ring", [P, 2, SEQ])
        out_ps = st.ps("out_ps", [P, 2, SEQ // 2])
        loaded, zeroed = st.sem("loaded"), st.sem("zeroed")
        rows_done, ring_done, ring_copied = st.sem("rows_done"), st.sem("ring_done"), st.sem("ring_copied")
        qkv_done, qkv_copied = st.sem("qkv_done"), st.sem("qkv_copied")
        outer_done = {"dve": st.sem("outer_dve"), "pool": st.sem("outer_pool")}
        v_done, v_turned = st.sem("v_done"), st.sem("v_turned")
        tails_done, logits_done, logits_read = st.sem("tails_done"), st.sem("logits_done"), st.sem("logits_read")
        max_done, shifted_done, exp_done = st.sem("max_done"), st.sem("shifted_done"), st.sem("exp_done")
        pv_done, combined, proj_done, added = (
            st.sem("pv_done"), st.sem("combined"), st.sem("proj_done"), st.sem("added"))
        own, tail_steps = st.sem("own"), st.sem("tail_steps")

        with nc.Block() as block:

            @block.sync
            def _(sp):
                sp.dma_start(wqkv[:, :, :], wqkv_t).then_inc(loaded, 16)
                sp.dma_start(wproj[:, :, :], wproj_t).then_inc(loaded, 16)
                sp.wait_ge(zeroed, 7)
                sp.dma_start(wv[:, :, 0:HD], wv_t).then_inc(loaded, 16)
                for j in range(GH):
                    sp.dma_start(bias[PAD * j:PAD * j + HD, :], bv.rearrange("(e a) -> e a", a=1)).then_inc(loaded, 16)
                sp.dma_start(setm[:, :, :], const["sets"].rearrange("(q p) s -> p q s", p=P)).then_inc(loaded, 16)
                sp.dma_start(tri[:, :], const["tail_sums"]).then_inc(loaded, 16)
                sp.dma_start(mask[:, :, :], const["sets_mask"].rearrange("(q p) s -> p q s", p=P)).then_inc(loaded, 16)
                sp.wait_ge(loaded, 16 * (6 + GH))

            @block.gpsimd
            def _(pool):
                pool.memset(qk[:, :, :, :, :, :].rearrange("p a q m h c -> p (a q m h c)"), 0.0).then_inc(zeroed, 1)
                pool.memset(k_diag[:, :, :, :].rearrange("p a g s -> p (a g s)"), 0.0).then_inc(zeroed, 1)
                pool.memset(v_diag[:, :, :, :, :].rearrange("p a h m c -> p (a h m c)"), 0.0).then_inc(zeroed, 1)
                pool.wait_ge(zeroed, 3)
                pool.memset(v_diag[0:SETS, :, :, 0, HD:], 1.0).then_inc(zeroed, 1)
                pool.memset(v_diag[SETS:P, :, :, 1, HD:], 1.0).then_inc(zeroed, 1)
                pool.wait_ge(zeroed, 5)
                pool.memset(wv[:, :, :].rearrange("p m c -> p (m c)"), 0.0).then_inc(zeroed, 1)
                pool.memset(bias[:, :], 0.0).then_inc(zeroed, 1)

        def at(s, q, use):
            return s * PER_SEQ + (TURN + q * TURN + use)

        def bank(use):
            return ring[:, use % 2, :]

        def present(s, q, use):
            t1 = s * TT + q
            if use == X:
                return t1 < TILES - 1
            if use in (QT, *PT):
                return TT <= t1 < TILES + TT
            if use == OUT:
                return t1 > TT
            if use in (KSUM, VSUM):
                return s < NB
            return t1 < TILES

        ORDER = [at(0, 0, X) - TURN]
        for s in range(NB + 2):
            for q in range(TT if s <= NB else 1):
                ORDER += [at(s, q, use) for use in range(TURN) if present(s, q, use)]
            if s < NB:
                ORDER += [at(s, 0, KSUM), at(s, 0, VSUM)]
        NEXT = dict(zip(ORDER, ORDER[1:] + [ORDER[-1] + 1]))

        def counted(number):
            return NEXT[number] - number if isinstance(number, int) else 1

        with nc.Block() as block:

            def steps(eng, turn, sums):
                def one(s, par, q, fixed=None):
                    t1 = fixed * TT + q if fixed is not None else None
                    if t1 is None:
                        turn(s, par, q, True, True, True, True)
                    else:
                        turn(s, par, q, t1 < TILES - 1, t1 < TILES, TT <= t1 < TILES + TT, t1 > TT)

                for s in (0, 1):
                    for q in range(TT):
                        one(s, s % 2, q, s)
                    sums(s, s % 2)
                with eng.Fori(0, (NB - 4) // 2) as it:
                    for par in range(2):
                        for q in range(TT):
                            one(it * 2 + (2 + par), par, q)
                        sums(it * 2 + (2 + par), par)
                for s in (NB - 2, NB - 1):
                    for q in range(TT):
                        one(s, s % 2, q, s)
                    sums(s, s % 2)
                for q in range(TT):
                    one(NB, 0, q, NB)
                one(NB + 1, 1, 0, NB + 1)

            @block.tensor
            def _(pe):
                def claim(number):
                    if not (isinstance(number, int) and number <= at(0, 0, X)):
                        pe.wait_ge(ring_copied, number - 1)

                def rows_turned(number, at_q, T):
                    pe.wait_ge(rows_done, T + 1)
                    claim(number)
                    for c in range(2):
                        last = pe.transpose(bank(X)[0:C2, P * c:P * c + P], rows[:, at_q, C2 * c:C2 * c + C2], idn[:, :])
                    last.then_inc(ring_done, counted(number))

                def projections(number, at_q, T):
                    pe.wait_ge(ring_copied, number + 1)
                    pe.wait_ge(qkv_copied, T * 2)
                    for c in range(2):
                        pe.matmul(qk_ps[:, 0:2 * D], xs[:, at_q, c, :], wqkv[:, c, 0:2 * D], start=(c == 0), stop=(c == 1))
                    for c in range(2):
                        last = pe.matmul(v0_ps, xs[:, at_q, c, :], wqkv[:, c, 2 * D:], start=(c == 0), stop=(c == 1))
                    last.then_inc(qkv_done, 1)

                def batch(s, q, T1, k):
                    number = at(s, q, OT[k])
                    claim(number)
                    pe.wait_ge(outer_done["dve" if k < DVE_BATCHES else "pool"], T1 + 1)
                    for m in range(4):
                        last = pe.transpose(bank(OT[k])[:, P * m:P * m + P],
                                            outer[:, q % 2, 2 * k + m // 2, P * (m % 2):P * (m % 2) + P], idn[:, :])
                    last.then_inc(ring_done, counted(number))

                def value(s, q, T1, k):
                    pe.wait_ge(ring_copied, at(s, q, OT[k]) + 1)
                    if k == 0:
                        pe.wait_ge(v_turned, T1)
                    for m in range(2):
                        for h in (2 * k, 2 * k + 1):
                            j, g = PAD * (h % GH), h // GH
                            last = pe.matmul(v_ps[j:j + PAD, g, :], wv[:, m, :], outer_t[:, q % 2, 2 * h + m, :],
                                             start=(m == 0), stop=(m == 1))
                    if k == BATCHES - 1:
                        last.then_inc(v_done, 1)

                def turn(s, par, q, following, values, scores, end):
                    T1 = s * TT + q
                    T2 = T1 - TT
                    if following:
                        rows_turned(at(s, q, X), 1 - q % 2, T1 + 1)
                    if scores:
                        claim(at(s, q, QT))
                        for g in range(NG):
                            last = pe.transpose(bank(QT)[:, P * g:P * g + P],
                                                qk[:, 1 - par, q, 0, GH * g:GH * g + GH, :].rearrange("p h c -> p (h c)"), idn[:, :])
                        last.then_inc(ring_done, counted(at(s, q, QT)))
                    if following:
                        if scores:
                            pe.wait_ge(logits_read, T2)
                        projections(at(s, q, X), 1 - q % 2, T1 + 1)
                    if end:
                        pe.wait_ge(combined, T2)
                        claim(at(s, q, OUT))
                        for c in range(2):
                            last = pe.transpose(bank(OUT)[0:C2, P * c:P * c + P],
                                                out_n[:, :, :].rearrange("p h c -> p (h c)")[:, C2 * c:C2 * c + C2], idn[:, :])
                        last.then_inc(ring_done, counted(at(s, q, OUT)))
                    if scores:
                        pe.matmul(tails_ps[:, 0:D], tri[:, :], qk[:, 1 - par, q, 1, :, 0:HD], start=True, stop=True)
                        pe.matmul(tails_ps[:, D:2 * D], tri[:, :], v[:, 1 - par, q, :, 0:HD], start=True, stop=True).then_inc(tails_done, 1)
                        pe.wait_ge(ring_copied, at(s, q, QT) + 1)
                        pe.wait_ge(logits_read, T2)
                        if following:
                            pe.wait_ge(qkv_copied, T1 * 2 + 4)
                        for g in range(NG):
                            last = pe.matmul(logits_ps[:, g // 2, 256 * (g % 2):256 * (g % 2) + 256], q_t[:, q % 2, g, :],
                                             k_diag[:, 1 - par, g, :], start=True, stop=True)
                        last.then_inc(logits_done, 1)
                    if values:
                        for k in range(BATCHES):
                            batch(s, q, T1, k)
                            if k >= 2:
                                value(s, q, T1, k - 2)
                    if end:
                        pe.wait_ge(ring_copied, at(s, q, OUT) + 1)
                        for c in range(2):
                            last = pe.matmul(out_ps[:, 1, 0:D], out_t[:, c, :], wproj[:, c, :], start=(c == 0), stop=(c == 1))
                        last.then_inc(proj_done, 1)
                    if values:
                        value(s, q, T1, BATCHES - 2)
                        value(s, q, T1, BATCHES - 1)
                    if scores:
                        pe.wait_ge(exp_done, T2 + 1)
                        for k in range(2):
                            claim(at(s, q, PT[k]))
                            for m in range(3):
                                h = 2 * (3 * k + m)
                                last = pe.transpose(bank(PT[k])[:, P * m:P * m + P],
                                                    probs[:, q % 2, h:h + 2, :].rearrange("p h s -> p (h s)"), idn[:, :])
                            last.then_inc(ring_done, counted(at(s, q, PT[k])))
                    if values:
                        pe.wait_ge(v_turned, T1 + 1)
                        claim(at(s, q, VT))
                        for g in range(NG):
                            last = pe.transpose(bank(VT)[:, P * g:P * g + P], v_t[:, g, :], idn[:, :])
                        last.then_inc(ring_done, counted(at(s, q, VT)))
                    if scores:
                        pe.wait_ge(ring_copied, at(s, q, PT[1]) + 1)
                        pe.wait_ge(added, T2)
                        for m in range(NH // 2):
                            last = pe.matmul(out_ps[:, 0, 34 * m:34 * m + 34], probs_t[:, m, :],
                                             v_diag[:, 1 - par, m, :, :].rearrange("p h c -> p (h c)"), start=True, stop=True)
                        last.then_inc(pv_done, 1)

                def sums(s, par):
                    claim(at(s, 0, KSUM))
                    for g in range(NG):
                        for q in range(TT):
                            last = pe.matmul(bank(KSUM)[:, SETS * g:SETS * g + SETS],
                                             qk[:, par, q, 1, GH * g:GH * g + GH, :].rearrange("p h c -> p (h c)"),
                                             setm[:, q, 0:SETS], start=(q == 0), stop=(q == TT - 1))
                    last.then_inc(ring_done, counted(at(s, 0, KSUM)))
                    pe.wait_ge(ring_copied, at(s, TT - 1, VT) + 1)
                    claim(at(s, 0, VSUM))
                    for q in range(TT):
                        last = pe.matmul(bank(VSUM)[:, 0:D], setm[:, q, :], v[:, par, q, :, 0:HD], start=(q == 0), stop=(q == TT - 1))
                    last.then_inc(ring_done, counted(at(s, 0, VSUM)))

                rows_turned(at(0, 0, X) - TURN, 0, 0)
                projections(at(0, 0, X) - TURN, 0, 0)
                steps(pe, turn, sums)

            @block.scalar
            def _(act):
                def copy(number, dst, src):
                    act.wait_ge(ring_done, number + 1)
                    act.activation(dst, src, ACT.Copy).then_inc(ring_copied, counted(number))

                def rows_copied(number, at_q):
                    copy(number, xs[:, at_q, :, :].rearrange("p c t -> p (c t)"), bank(X)[0:C2, 0:2 * P])

                def qkv(par, q, T):
                    act.wait_ge(qkv_done, T + 1)
                    act.activation(qk[:, par, q, :, :, 0:HD].rearrange("p m h c -> p (m h) c"),
                                   qk_ps[:, 0:2 * D].rearrange("p (m c) -> p m c", c=HD), ACT.Copy).then_inc(qkv_copied, 1)
                    act.activation(v0[:, q % 2, :, :].rearrange("p h c -> p (h c)"), v0_ps, ACT.Copy).then_inc(qkv_copied, 1)

                def turn(s, par, q, following, values, scores, end):
                    T1 = s * TT + q
                    T2 = T1 - TT
                    if following:
                        act.wait_ge(qkv_done, T1)
                        rows_copied(at(s, q, X), 1 - q % 2)
                    if scores:
                        act.wait_ge(logits_done, T2)
                        copy(at(s, q, QT), q_t[:, q % 2, :, :].rearrange("p g t -> p (g t)"), bank(QT)[:, 0:NG * P])
                    if following:
                        if q < TT - 1:
                            qkv(par, q + 1, T1 + 1)
                        else:
                            qkv(1 - par, 0, T1 + 1)
                    if end:
                        act.wait_ge(proj_done, T2 - 1)
                        copy(at(s, q, OUT), out_t[:, :, :].rearrange("p c t -> p (c t)"), bank(OUT)[0:C2, 0:2 * P])
                    if values:
                        act.wait_ge(v_done, T1)
                        for k in range(BATCHES):
                            copy(at(s, q, OT[k]), outer_t[:, q % 2, 4 * k:4 * k + 4, :].rearrange("p m t -> p (m t)"), bank(OT[k]))
                    if scores:
                        act.wait_ge(shifted_done, T2 + 1)
                        act.activation(probs[:, q % 2, :, :], shifted[:, :, :], ACT.Exp).then_inc(exp_done, 1)
                    if values:
                        act.wait_ge(v_done, T1 + 1)
                        act.activation(v_t[:, :, :], v_ps[:, :, :], ACT.Identity, bias=bias[:, :]).then_inc(v_turned, 1)
                    if scores:
                        act.wait_ge(pv_done, T2)
                        for k in range(2):
                            copy(at(s, q, PT[k]), probs_t[:, 3 * k:3 * k + 3, :].rearrange("p m t -> p (m t)"), bank(PT[k])[:, 0:3 * P])
                    if values:
                        copy(at(s, q, VT), v[:, par, q, :, :].rearrange("p h c -> p (h c)"), bank(VT)[:, 0:NG * P])

                def sums(s, par):
                    act.wait_ge(ring_done, at(s, 0, KSUM) + 1)
                    for j in range(GH):
                        rows_j = slice(PAD * j, PAD * j + PAD)
                        ins = act.activation(k_diag[rows_j, par, :, SETS * j:SETS * j + SETS],
                                             bank(KSUM)[rows_j, 0:NG * SETS].rearrange("p (g s) -> p g s", g=NG), ACT.Copy)
                    ins.then_inc(ring_copied, counted(at(s, 0, KSUM)))
                    act.wait_ge(ring_done, at(s, 0, VSUM) + 1)
                    for m in range(2):
                        rows_m = slice(SETS * m, SETS * m + SETS)
                        ins = act.activation(v_diag[rows_m, par, :, m, 0:HD],
                                             bank(VSUM)[rows_m, 0:D].rearrange("p (h m c) -> p h m c", m=2, c=HD)[:, :, m, :], ACT.Copy)
                    ins.then_inc(ring_copied, counted(at(s, 0, VSUM)))

                rows_copied(at(0, 0, X) - TURN, 0)
                qkv(0, 0, 0)
                steps(act, turn, sums)

            def products(eng, which, par, q, T, heads):
                n = heads.stop - heads.start
                eng.wait_ge(qkv_copied, T * 2 + 2)
                if not (isinstance(T, int) and T < 2):
                    eng.wait_ge(v_done, T - 1)
                k = qk[:, par, q, 1, heads, 0:HD].unsqueeze(3).to_broadcast([P, n, HD, HD])
                w = v0[:, q % 2, heads, :].unsqueeze(2).to_broadcast([P, n, HD, HD])
                eng.tensor_tensor(outer[:, q % 2, heads, :].rearrange("p h (i j) -> p h i j", i=HD), k, w,
                                  ALU.mult).then_inc(outer_done[which], 1)

            def next_products(eng, which, par, q, T1, heads):
                if q < TT - 1:
                    products(eng, which, par, q + 1, T1 + 1, heads)
                else:
                    products(eng, which, 1 - par, 0, T1 + 1, heads)

            @block.gpsimd
            def _(pool):
                heads = slice(2 * DVE_BATCHES, NH)

                def turn(s, par, q, following, values, scores, end):
                    T2 = s * TT + (q - TT)
                    if scores:
                        pool.wait_ge(max_done, T2 + 1)
                        pool.wait_ge(exp_done, T2)
                        pool.tensor_tensor(shifted[:, :, :], logits[:, :, :],
                                           high[:, :].unsqueeze(2).to_broadcast([P, NH, SETS]), ALU.subtract).then_inc(shifted_done, 1)
                    if following:
                        next_products(pool, "pool", par, q, s * TT + q, heads)

                products(pool, "pool", 0, 0, 0, heads)
                steps(pool, turn, lambda s, par: None)

            @block.vector
            def _(dve):
                heads = slice(0, 2 * DVE_BATCHES)

                def rows_of(T, at_q):
                    if not (isinstance(T, int) and T < 2):
                        dve.wait_ge(qkv_done, T - 1)
                    t = bass.ds(T, 1)
                    dve.tensor_scalar(rows[:, at_q, :], H[:, t, :].rearrange("p t d -> p (t d)"),
                                      mean[:, t], rstd[:, t], ALU.subtract, ALU.mult).then_inc(rows_done, 1)

                def combine(T, at_q):
                    dve.wait_ge(pv_done, T + 1)
                    pv = out_ps[:, 0, 0:NH * (HD + 1)].rearrange("p (h c) -> p h c", h=NH)
                    dve.reciprocal(recip[:, :], pv[:, :, HD]).then_inc(own, 1)
                    dve.tensor_tensor(out[:, :, :], tails_ps[:, D:2 * D].rearrange("p (h c) -> p h c", h=NH),
                                      probs[:, at_q, :, SETS - 1:].to_broadcast([P, NH, HD]), ALU.mult).then_inc(own, 1)
                    dve.wait_ge(own, T * 3 + 2)
                    dve.tensor_tensor(out[:, :, :], out[:, :, :], pv[:, :, 0:HD], ALU.add).then_inc(own, 1)
                    dve.wait_ge(own, T * 3 + 3)
                    dve.tensor_tensor(out_n[:, :, :], out[:, :, :], recip[:, :].unsqueeze(2).to_broadcast([P, NH, HD]),
                                      ALU.mult).then_inc(combined, 1)

                def turn(s, par, q, following, values, scores, end):
                    T1 = s * TT + q
                    T2 = T1 - TT
                    if end:
                        combine(T2 - 1, 1 - q % 2)
                    if scores:
                        dve.wait_ge(tails_done, T2 + 1)
                        dve.tensor_tensor(q_tail[:, :, :], qk[:, 1 - par, q, 0, :, 0:HD],
                                          tails_ps[:, 0:D].rearrange("p (h c) -> p h c", h=NH), ALU.mult).then_inc(tail_steps, 1)
                        dve.wait_ge(tail_steps, T2 * 3 + 1)
                        dve.tensor_reduce(tail[:, :], q_tail[:, :, :], AX.X, ALU.add).then_inc(tail_steps, 1)
                        dve.wait_ge(logits_done, T2 + 1)
                        dve.wait_ge(shifted_done, T2)
                        dve.scalar_tensor_tensor(logits[:, :, :],
                                                 logits_ps[:, :, :].rearrange("p b s -> p (b s)")[:, 0:NH * SETS].rearrange("p (h s) -> p h s", h=NH),
                                                 SCALE, mask[:, q, :].unsqueeze(1).to_broadcast([P, NH, SETS]),
                                                 ALU.mult, ALU.add).then_inc(logits_read, 1)
                        dve.wait_ge(logits_read, T2 + 1)
                        dve.wait_ge(tail_steps, T2 * 3 + 2)
                        dve.tensor_scalar(logits[:, :, SETS - 1], tail[:, :], SCALE, None, ALU.mult).then_inc(tail_steps, 1)
                        dve.wait_ge(tail_steps, T2 * 3 + 3)
                        dve.tensor_reduce(high[:, :], logits[:, :, :], AX.X, ALU.max).then_inc(max_done, 1)
                    if following:
                        next_products(dve, "dve", par, q, T1, heads)
                        if not (isinstance(T1, int) and T1 + 2 >= TILES):
                            rows_of(T1 + 2, q % 2)
                    if end:
                        dve.wait_ge(proj_done, T2)
                        dst = H[:, bass.ds(T2 - 1, 1), :].rearrange("p t d -> p (t d)")
                        dve.tensor_tensor(dst, out_ps[:, 1, 0:D], dst, ALU.add).then_inc(added, 1)

                rows_of(0, 0)
                products(dve, "dve", 0, 0, 0, heads)
                rows_of(1, 1)
                steps(dve, turn, lambda s, par: None)


GROUP_ROWS = TT * P
SLOT_GROUPS = 2 * TOKENS // GROUP_ROWS + 8
SLOTS = SLOT_GROUPS * GROUP_ROWS


def experts_stage(nc, H, idn, gamma, beta, router_w, w1, w2, const, rows_out, out_stored):
    E, hidden = w1.shape[0], w1.shape[2]
    assert E == 8
    x_rows = nc.dram_tensor("x_rows", (TOKENS, D), F32).ap()
    y_rows = nc.dram_tensor("y_rows", (SLOTS, D), F32).ap()
    slot_tokens = nc.dram_tensor("slot_tokens", (SLOTS, 1), F32).ap()
    with ExitStack() as stage:
        st = Store(nc, stage, "experts")
        gamma_beta = st.sb("gamma_beta", [C2, 2, 2])
        gates = st.sb("gates", [P, 2, TILES])
        slots = st.sb("slots", [P, 2, TILES], I32)
        tokens = st.sb("tokens", [P, SLOTS // P], I32)
        group_expert = st.sb("group_expert", [P, SLOT_GROUPS], I32)
        with ExitStack() as part:
            pt = Store(nc, part, "moe")
            xT = pt.sb("xT", [C2, 2, TOKENS])
            router = pt.sb("router", [C2, 2, E])
            small_in = st.sem("small_in")
            with nc.Block() as block:

                @block.sync
                def _(sp):
                    with nc.allow_non_contiguous_dma(reason="one value per partition"):
                        sp.dma_start(gamma_beta[:, :, 0], gamma.rearrange("(c p) -> p c", c=2)).then_inc(small_in, 16)
                        sp.dma_start(gamma_beta[:, :, 1], beta.rearrange("(c p) -> p c", c=2)).then_inc(small_in, 16)
                    sp.dma_start(router[:, :, :], router_w.rearrange("(c p) e -> p c e", c=2)).then_inc(small_in, 16)
                    sp.wait_ge(small_in, 48)

            turned_norm(nc, "moe_norm", H, idn, xT, twice=True, gamma_beta=gamma_beta, store_to=x_rows)
            route(nc, xT, router, idn, const["routing"], gates, slots, tokens, group_expert, slot_tokens, E)
        slot_products(nc, idn, gamma_beta, w1, w2, hidden, tokens, group_expert, x_rows, y_rows)
        combine_experts(nc, H, gates, slots, y_rows, rows_out, out_stored)


def slot_products(nc, idn, gamma_beta, w1, w2, hidden, tokens, group_expert, x_rows, y_rows):
    M = hidden // P
    PAIRS = SLOT_GROUPS // 2
    with ExitStack() as part:
        pt = Store(nc, part, "slots")
        w1_sb = pt.sb("w1", [C2, 2, 2, hidden])
        w2_sb = pt.sb("w2", [P, 2, M, D])
        index = pt.sb("index", [P, 2, TT], I32)
        x = pt.sb("x", [P, 2, TT, D])
        xT = pt.sb("xT", [C2, 2, 2, SEQ])
        hid = pt.sb("hid", [P, 2, M, SEQ])
        y = pt.sb("y", [P, 2, TT, D])
        hid_ps = pt.ps("hid_ps", [P, 4, SEQ])
        turned_ps = pt.ps("turned_ps", [C2, 2, SEQ])
        out_ps = pt.ps("out_ps", [P, 2, SEQ])
        w1_in = [pt.sem("w1_in_even"), pt.sem("w1_in_odd")]
        w2_in = [pt.sem("w2_in_even"), pt.sem("w2_in_odd")]
        gathered = [pt.sem("gathered_even"), pt.sem("gathered_odd")]
        stored = [pt.sem("stored_even"), pt.sem("stored_odd")]
        indexed, turned_done, turned_copied = pt.sem("indexed"), pt.sem("turned_done"), pt.sem("turned_copied")
        hid_done, func_done, out_done, out_copied = (
            pt.sem("hid_done"), pt.sem("func_done"), pt.sem("out_done"), pt.sem("out_copied"))
        all_stored, begun = pt.sem("all_stored"), pt.sem("begun")
        nc.scalar.preload_act_table(ACT.Silu)
        with nc.Block() as block:

            @block.sync
            def _(sp):
                def expert(g):
                    return sp.value_load(group_expert[0:1, bass.ds(g, 1)], min_val=0, max_val=7)

                def load_first(e, c):
                    sp.dma_start(w1_sb[:, c, :, :], w1[bass.ds(e, 1), :, :].rearrange("e (c p) f -> p (e c) f", c=2)).then_inc(w1_in[c], 16)

                def load_second(e, c):
                    sp.dma_start(w2_sb[:, c, :, :], w2[bass.ds(e, 1), :, :].rearrange("e (m p) d -> p (e m) d", p=P)).then_inc(w2_in[c], 16)

                def store(g, c):
                    sp.wait_ge(out_copied, g * 2 + 2)
                    sp.dma_start(y_rows[bass.ds(g * GROUP_ROWS, GROUP_ROWS), :].rearrange("(k p) d -> p k d", p=P),
                                 y[:, c, :, :]).then_inc(stored[c], 16)

                def turn(g, c, has_before):
                    e = expert(g + 2)
                    sp.wait_ge(hid_done, g * M + M)
                    load_first(e, c)
                    if has_before:
                        store(g - 1, 1 - c)
                    sp.wait_ge(out_done, g + 1)
                    load_second(e, c)

                for c in range(2):
                    e = expert(c)
                    load_first(e, c)
                    load_second(e, c)
                turn(0, 0, False)
                with sp.Fori(0, PAIRS - 2) as it:
                    turn(it * 2 + 1, 1, True)
                    turn(it * 2 + 2, 0, True)
                turn(SLOT_GROUPS - 3, 1, True)
                for g in (SLOT_GROUPS - 3, SLOT_GROUPS - 2, SLOT_GROUPS - 1):
                    store(g, g % 2)
                for c in range(2):
                    sp.wait_ge(stored[c], 16 * PAIRS)
                sp.sem_inc(all_stored, 1)

            @block.gpsimd
            def _(pool):
                def gather(g, c):
                    pool.tensor_copy(index[:, c, :], tokens[:, bass.ds(g * TT, TT)]).then_inc(indexed, 1)
                    pool.wait_ge(indexed, g + 1)
                    pool.sem_inc(begun, 1)
                    for k in range(TT):
                        pool.indirect_dma_start(x[:, c, k, :], None, x_rows[:, :],
                                                bass.IndirectOffsetOnAxis(ap=index[:, c, k:k + 1].bitcast(U32), axis=0)
                                                ).then_inc(gathered[c], 16)

                gather(0, 0)
                gather(1, 1)
                with pool.Fori(1, PAIRS) as it:
                    for c in range(2):
                        g = it * 2 + c
                        pool.wait_ge(turned_done, g - 1)
                        pool.wait_ge(gathered[c], it * (16 * TT))
                        gather(g, c)

            @block.tensor
            def _(pe):
                def turn_x(g, c, pair):
                    pe.wait_ge(gathered[c], pair * (16 * TT) + 16 * TT)
                    if not (isinstance(g, int) and g == 0):
                        pe.wait_ge(turned_copied, g * 2)
                    for n in range(2):
                        for k in range(TT):
                            last = pe.transpose(turned_ps[:, n, P * k:P * k + P], x[:, c, k, C2 * n:C2 * n + C2], idn[:, :])
                    last.then_inc(turned_done, 1)

                def first(g, c, pair):
                    pe.wait_ge(w1_in[c], pair * 16 + 16)
                    pe.wait_ge(turned_copied, g * 2 + 2)
                    for m in range(M):
                        at = (c * M + m) % 4
                        if not (isinstance(g, int) and g * M + m < 4):
                            pe.wait_ge(func_done, g * M + (m - 3))
                        for k in range(2):
                            last = pe.matmul(hid_ps[:, at, :], w1_sb[:, c, k, P * m:P * m + P], xT[:, c, k, :],
                                             start=(k == 0), stop=(k == 1))
                        last.then_inc(hid_done, 1)

                def second(g, c, pair):
                    pe.wait_ge(w2_in[c], pair * 16 + 16)
                    pe.wait_ge(func_done, g * M + M)
                    if not (isinstance(g, int) and g == 0):
                        pe.wait_ge(out_copied, g * 2)
                    for k in range(TT):
                        for m in range(M):
                            last = pe.matmul(out_ps[:, k // 2, D * (k % 2):D * (k % 2) + D], hid[:, c, m, P * k:P * k + P],
                                             w2_sb[:, c, m, :], start=(m == 0), stop=(m == M - 1))
                    last.then_inc(out_done, 1)

                turn_x(0, 0, 0)
                turn_x(1, 1, 0)
                first(0, 0, 0)
                with pe.Fori(0, PAIRS - 1) as it:
                    first(it * 2 + 1, 1, it)
                    turn_x(it * 2 + 2, 0, it + 1)
                    second(it * 2, 0, it)
                    first(it * 2 + 2, 0, it + 1)
                    turn_x(it * 2 + 3, 1, it + 1)
                    second(it * 2 + 1, 1, it)
                first(SLOT_GROUPS - 1, 1, PAIRS - 1)
                second(SLOT_GROUPS - 2, 0, PAIRS - 1)
                second(SLOT_GROUPS - 1, 1, PAIRS - 1)

            @block.scalar
            def _(act):
                def function(g, c):
                    if not (isinstance(g, int) and g < 2):
                        act.wait_ge(out_done, g - 1)
                    for m in range(M):
                        act.wait_ge(hid_done, g * M + m + 1)
                        act.activation(hid[:, c, m, :], hid_ps[:, (c * M + m) % 4, :], ACT.Silu).then_inc(func_done, 1)

                function(0, 0)
                function(1, 1)
                with act.Fori(1, PAIRS) as it:
                    for c in range(2):
                        function(it * 2 + c, c)

            @block.vector
            def _(dve):
                def scale(g, c):
                    dve.wait_ge(turned_done, g + 1)
                    if not (isinstance(g, int) and g < 2):
                        dve.wait_ge(hid_done, g * M - M)
                    for n in range(2):
                        dve.tensor_scalar(xT[:, c, n, :], turned_ps[:, n, :], gamma_beta[:, n, 0:1], gamma_beta[:, n, 1:2],
                                          ALU.mult, ALU.add).then_inc(turned_copied, 1)

                def copy(g, c, pair):
                    dve.wait_ge(out_done, g + 1)
                    if not isinstance(pair, int):
                        dve.wait_ge(stored[c], pair * 16)
                    for n in range(2):
                        dve.tensor_copy(y[:, c, 2 * n:2 * n + 2, :].rearrange("p k d -> p (k d)"), out_ps[:, n, 0:2 * D]).then_inc(out_copied, 1)

                scale(0, 0)
                scale(1, 1)
                scale(2, 0)
                copy(0, 0, 0)
                scale(3, 1)
                copy(1, 1, 0)
                with dve.Fori(1, PAIRS - 1) as it:
                    scale(it * 2 + 2, 0)
                    copy(it * 2, 0, it)
                    scale(it * 2 + 3, 1)
                    copy(it * 2 + 1, 1, it)
                for c in range(2):
                    dve.wait_ge(stored[c], 16 * (PAIRS - 1))
                    copy(SLOT_GROUPS - 2 + c, c, PAIRS - 1)


def combine_experts(nc, H, gates, slots, y_rows, rows_out, stored):
    with ExitStack() as part:
        pt = Store(nc, part, "combine")
        y = pt.sb("y", [P, 2, TT, 2, D])
        gathered = [pt.sem("gathered_even"), pt.sem("gathered_odd")]
        added = pt.sem("added")
        with nc.Block() as block:

            @block.gpsimd
            def _(pool):
                for g in range(GROUPS):
                    if g >= 2:
                        pool.wait_ge(gathered[g % 2], 16 * 2 * TT * (g // 2))
                        pool.wait_ge(added, (g - 1) * 2 * TT)
                    for k in range(TT):
                        for n in range(2):
                            t = g * TT + k
                            pool.indirect_dma_start(y[:, g % 2, k, n, :], None, y_rows[:, :],
                                                    bass.IndirectOffsetOnAxis(ap=slots[:, n, t:t + 1].bitcast(U32), axis=0)
                                                    ).then_inc(gathered[g % 2], 16)

            @block.vector
            def _(dve):
                with dve.Fori(0, GROUPS // 2) as it:
                    for half in range(2):
                        g = it * 2 + half
                        dve.wait_ge(gathered[half], it * (32 * TT) + 32 * TT)
                        for n in range(2):
                            if n:
                                dve.wait_ge(added, g * (2 * TT) + TT)
                            for k in range(TT):
                                t = bass.ds(g * TT + k, 1)
                                dst = H[:, t, :].rearrange("p t d -> p (t d)")
                                dve.scalar_tensor_tensor(dst, y[:, half, k, n, :], gates[:, n, t], dst, ALU.mult, ALU.add).then_inc(added, 1)

            @block.sync
            def _(sp):
                with sp.Fori(0, GROUPS) as g:
                    sp.wait_ge(added, g * (2 * TT) + 2 * TT)
                    sp.dma_start(rows_out[bass.ds(g * GROUP_ROWS, GROUP_ROWS), :].rearrange("(k p) d -> p k d", p=P),
                                 H[:, bass.ds(g * TT, TT), :]).then_inc(stored, 16)
                sp.wait_ge(stored, 16 * GROUPS)


def route(nc, xT, router, idn, routing, gates, slots, tokens, group_expert, slot_tokens, E):
    NT = SLOTS // P
    MAXG = GROUPS
    with ExitStack() as part:
        pt = Store(nc, part, "route")
        logits_t = pt.sb("logits_t", [E, 2, SEQ])
        full = [P, TILES, E]
        probs = pt.sb("probs", full)
        left = pt.sb("left", full)
        equal = pt.sb("equal", full)
        masks = [pt.sb("mask1", full), pt.sb("mask2", full)]
        both = pt.sb("both", full)
        count = pt.sb("count", full)
        sums = [pt.sb("sums_a", full), pt.sb("sums_b", full)]
        place = pt.sb("place", full)
        high = pt.sb("high", [P, TILES])
        top1 = pt.sb("top1", [P, TILES])
        index = pt.sb("index", [P, TILES])
        known = pt.sb("known", [P, routing.shape[1]])
        sizes = pt.sb("sizes", [P, E, MAXG])
        ends = [pt.sb(f"ends{n}", [P, E]) for n in range(4)]
        base = pt.sb("base", [P, E])
        past = pt.sb("past", [P, SLOT_GROUPS, E])
        owner = pt.sb("owner", [P, SLOT_GROUPS])
        slots_f = pt.sb("slots_f", [P, TILES])
        zeros = pt.sb("zeros", [P, NT])
        listed = pt.sb("listed", [NT // 2, 2, P])
        product = pt.ps("product", [E, 2, SEQ])
        turned = pt.ps("turned", [P, 2, SEQ])
        ranks = pt.ps("ranks", [P, SEQ])
        totals = pt.ps("totals", [P, SEQ])
        at = 0
        views = []
        for width in (TILES, E * MAXG, SLOT_GROUPS, TILES * E, P, P):
            views.append(known[:, at:at + width])
            at += width
        token_numbers, firsts, group_numbers, number, before, ones = views
        number = number.rearrange("p (t e) -> p t e", e=E)
        product_done, copied, turned_done, placed, known_in = (
            pt.sem("product_done"), pt.sem("copied"), pt.sem("turned_done"), pt.sem("placed"), pt.sem("known_in"))
        turn_begun = pt.sem("turn_begun")
        own, exp_ready, exp_done = pt.sem("own"), pt.sem("exp_ready"), pt.sem("exp_done")
        masks_ready, ranked, slots_ready, list_in = pt.sem("masks_ready"), pt.sem("ranked"), pt.sem("slots_ready"), pt.sem("list_in")
        scattered = pt.sem("scattered")

        def wide(x):
            return x[:, :].unsqueeze(2).to_broadcast(full)

        with nc.Block() as block:

            @block.sync
            def _(sp):
                sp.dma_start(known[:, :], routing).then_inc(known_in, 16)
                sp.wait_ge(placed, 1)
                sp.dma_start(slot_tokens.rearrange("(p k) a -> p (k a)", p=P), zeros[:, :]).then_inc(list_in, 16)
                sp.wait_ge(scattered, 16 * 2 * TILES)
                sp.dma_start(listed[:, :, :], slot_tokens.rearrange("(c i p) a -> i c (p a)", c=2, p=P)).then_inc(list_in, 16)

            @block.tensor
            def _(pe):
                pe.sem_inc(turned_done, 1)
                with pe.Fori(0, GROUPS // 2) as it:
                    for half in range(2):
                        g = it * 2 + half
                        pe.wait_ge(copied, g)
                        for k in range(2):
                            last = pe.matmul(product[:, half, :], router[:, k, :], xT[:, k, bass.ds(g * SEQ, SEQ)],
                                             start=(k == 0), stop=(k == 1))
                        last.then_inc(product_done, 1)
                        pe.wait_ge(copied, g + 2)
                        pe.wait_ge(placed, g)
                        pe.sem_inc(turn_begun, 1)
                        for k in range(TT):
                            last = pe.transpose(turned[:, half, E * k:E * k + E], logits_t[:, half, P * k:P * k + P], idn[0:E, 0:E])
                        last.then_inc(turned_done, 1)
                pe.wait_ge(known_in, 16)
                pe.wait_ge(masks_ready, 1)
                chosen = both[:, :, :].rearrange("p t e -> p (t e)")
                pe.matmul(ranks[:, :], before, chosen, start=True, stop=True)
                pe.matmul(totals[:, :], ones, chosen, start=True, stop=True).then_inc(ranked, 1)
                pe.wait_ge(list_in, 32)
                pe.wait_ge(slots_ready, 2)
                for c in range(2):
                    last = pe.transpose(ranks[:, P * c:P * c + NT // 2], listed[:, c, :], idn[0:NT // 2, 0:NT // 2])
                last.then_inc(ranked, 1)

            @block.scalar
            def _(act):
                act.sem_inc(copied, 1)
                with act.Fori(0, GROUPS // 2) as it:
                    for half in range(2):
                        g = it * 2 + half
                        act.wait_ge(product_done, g + 1)
                        act.wait_ge(turned_done, g)
                        act.activation(logits_t[:, half, :], product[:, half, :], ACT.Copy).then_inc(copied, 1)
                act.wait_ge(exp_ready, 1)
                act.activation(equal[:, :, :], left[:, :, :], ACT.Exp).then_inc(exp_done, 1)

            @block.vector
            def _(dve):
                dve.memset(zeros[:, :], 0.0).then_inc(placed, 1)
                with dve.Fori(0, GROUPS // 2) as it:
                    for half in range(2):
                        g = it * 2 + half
                        dve.wait_ge(turned_done, g + 2)
                        dve.tensor_copy(probs[:, bass.ds(g * TT, TT), :].rearrange("p t e -> p (t e)"),
                                        turned[:, half, 0:TT * E]).then_inc(placed, 1)
                dve.wait_ge(placed, GROUPS + 1)
                chain = Chain(dve, own)

                def step(ins):
                    chain(ins)
                    chain.wait()

                step(dve.tensor_reduce(high[:, :], probs[:, :, :], AX.X, ALU.max))
                dve.tensor_tensor(left[:, :, :], probs[:, :, :], wide(high), ALU.subtract).then_inc(exp_ready, 1)
                dve.wait_ge(exp_done, 1)
                step(dve.tensor_reduce(high[:, :], equal[:, :, :], AX.X, ALU.add))
                step(dve.reciprocal(index[:, :], high[:, :]))
                step(dve.tensor_tensor(probs[:, :, :], equal[:, :, :], wide(index), ALU.mult))
                dve.wait_ge(known_in, 16)

                def first_largest(values, top, mask):
                    step(dve.tensor_reduce(top[:, :], values[:, :, :], AX.X, ALU.max))
                    step(dve.tensor_tensor(equal[:, :, :], values[:, :, :], wide(top), ALU.not_equal))
                    step(dve.scalar_tensor_tensor(equal[:, :, :], equal[:, :, :], float(E), number, ALU.mult, ALU.add))
                    step(dve.tensor_reduce(index[:, :], equal[:, :, :], AX.X, ALU.min))
                    step(dve.tensor_tensor(mask[:, :, :], number, wide(index), ALU.is_equal))

                first_largest(probs, top1, masks[0])
                step(dve.scalar_tensor_tensor(left[:, :, :], masks[0][:, :, :], -2.0, probs[:, :, :], ALU.mult, ALU.add))
                first_largest(left, high, masks[1])
                dve.tensor_tensor(both[:, :, :], masks[0][:, :, :], masks[1][:, :, :], ALU.add).then_inc(masks_ready, 1)
                step(dve.tensor_tensor(index[:, :], top1[:, :], high[:, :], ALU.add))
                step(dve.reciprocal(index[:, :], index[:, :]))
                chain(dve.tensor_tensor(gates[:, 0, :], top1[:, :], index[:, :], ALU.mult))
                chain(dve.tensor_tensor(gates[:, 1, :], high[:, :], index[:, :], ALU.mult))

                dve.wait_ge(ranked, 1)
                step(dve.tensor_copy(count[:, :, :].rearrange("p t e -> p (t e)"), totals[:, :]))
                src, shift, n = count, 1, 0
                while shift < TILES:
                    dst = sums[n % 2]
                    chain(dve.tensor_copy(dst[:, 0:shift, :], src[:, 0:shift, :]))
                    step(dve.tensor_tensor(dst[:, shift:, :], src[:, shift:, :], src[:, 0:TILES - shift, :], ALU.add))
                    src, shift, n = dst, shift * 2, n + 1
                running = src
                step(dve.tensor_tensor(sizes[:, :, :], running[:, TILES - 1, :].unsqueeze(2).to_broadcast([P, E, MAXG]),
                                       firsts.rearrange("p (e j) -> p e j", e=E), ALU.is_gt))
                step(dve.tensor_reduce(ends[0][:, :], sizes[:, :, :], AX.X, ALU.add))
                for n, shift in enumerate((1, 2, 4)):
                    chain(dve.tensor_copy(ends[n + 1][:, 0:shift], ends[n][:, 0:shift]))
                    step(dve.tensor_tensor(ends[n + 1][:, shift:], ends[n][:, shift:], ends[n][:, 0:E - shift], ALU.add))
                step(dve.tensor_tensor(base[:, :], ends[3][:, :], ends[0][:, :], ALU.subtract))
                step(dve.tensor_scalar(base[:, :], base[:, :], float(GROUP_ROWS), None, ALU.mult))
                step(dve.tensor_tensor(place[:, :, :], running[:, :, :], count[:, :, :], ALU.subtract))
                step(dve.tensor_tensor(place[:, :, :].rearrange("p t e -> p (t e)"), ranks[:, :],
                                       place[:, :, :].rearrange("p t e -> p (t e)"), ALU.add))
                step(dve.tensor_tensor(place[:, :, :], place[:, :, :], base[:, :].unsqueeze(1).to_broadcast(full), ALU.add))
                for n in range(2):
                    step(dve.tensor_tensor(equal[:, :, :], masks[n][:, :, :], place[:, :, :], ALU.mult))
                    step(dve.tensor_reduce(slots_f[:, :], equal[:, :, :], AX.X, ALU.add))
                    dve.tensor_copy(slots[:, n, :], slots_f[:, :]).then_inc(slots_ready, 1)
                    dve.wait_ge(slots_ready, n + 1)
                step(dve.tensor_tensor(past[:, :, :], group_numbers.unsqueeze(2).to_broadcast([P, SLOT_GROUPS, E]),
                                       ends[3][:, :].unsqueeze(1).to_broadcast([P, SLOT_GROUPS, E]), ALU.is_ge))
                step(dve.tensor_reduce(owner[:, :], past[:, :, :], AX.X, ALU.add))
                chain(dve.tensor_scalar(group_expert[:, :], owner[:, :], float(E - 1), None, ALU.min))
                dve.wait_ge(ranked, 2)
                chain(dve.tensor_copy(tokens[:, :].rearrange("p (c i) -> p c i", c=2),
                                      ranks[:, 0:2 * P].rearrange("p (c i) -> p c i", c=2)[:, :, 0:NT // 2]))

            @block.gpsimd
            def _(pool):
                pool.wait_ge(list_in, 16)
                pool.wait_ge(known_in, 16)
                for n in range(2):
                    pool.wait_ge(slots_ready, n + 1)
                    for t in range(TILES):
                        pool.indirect_dma_start(slot_tokens[:, :], bass.IndirectOffsetOnAxis(ap=slots[:, n, t:t + 1].bitcast(U32), axis=0),
                                                token_numbers[:, t:t + 1], None).then_inc(scattered, 16)


def constants():
    p, i = np.meshgrid(np.arange(SEQ), np.arange(D // 2))
    pos = np.zeros((SEQ, D), dtype=np.float32)
    pos[:, ::2] = np.sin(p / 2500 ** (2 * i / D)).T
    pos[:, 1::2] = np.cos(p / 2500 ** (2 * i / D)).T
    wv = np.zeros((P, NH, PAD), np.float32)
    wv[HD, :, HD:] = 1.0
    affine = np.zeros((P, NG, 4), np.float32)
    affine[HD, :, 1] = affine[HD, :, 3] = 1.0
    t = np.arange(SEQ)
    spans = [(i, i + size - 1) for size in (16 << n for n in range(6)) for i in range(0, SEQ, size)]
    sets = np.zeros((SEQ, 2, SETS), np.float32)
    sets_mask = np.zeros((SEQ, SETS), np.float32)
    for n, (first, last) in enumerate(spans):
        sets[first:last + 1, :, n] = 1.0
        sets_mask[:, n] = np.where(t >= last, 0.0, NEG)
    near_mask = np.full((NB, COLS, 3, NB, SPAN), NEG, np.float32)
    for v, column0 in enumerate((0, COLS, SEQ - COLS)):
        for b in range(NB):
            for w in range(COLS):
                top = min(max(b - WIN // 2, 0), NB - WIN)
                left = min(max(column0 + w - WIN // 2, 0), SEQ - WIN) - (column0 - WIN // 2)
                near_mask[b, w, v, top:top + WIN, left:left + WIN] = 0.0
    r = np.arange(P)
    tail_sums = ((r[:, None] // 16 == r[None, :] // 16) & (r[:, None] <= r[None, :])).astype(np.float32)
    def alike(values):
        return np.broadcast_to(np.asarray(values, np.float32).reshape(1, -1), (P, np.size(values)))

    routing = [
        r[:, None] + P * np.arange(TILES)[None, :],
        alike(np.tile(np.arange(GROUPS) * GROUP_ROWS, 8)),
        alike(np.arange(SLOT_GROUPS)),
        alike(np.tile(np.arange(8), TILES)),
        r[:, None] < r[None, :],
        np.ones((P, P)),
    ]
    return {
        "routing": np.concatenate(routing, axis=1).astype(np.float32),
        "near_mask": near_mask.reshape(P, 3 * KEYS),
        "sets": sets.reshape(SEQ, 2 * SETS),
        "sets_mask": sets_mask,
        "tail_sums": tail_sums,
        "pos": pos,
        "pad_rows": np.concatenate([wv.reshape(P, -1), affine.reshape(P, -1)], axis=1),
        "ident": np.eye(P, dtype=np.float32),
    }


_CONSTANTS = constants()
_INS = [
    "x", "L0_tok_emb", "L0_tok_Wq", "L0_tok_bq", "L0_tok_Wk", "L0_tok_bk", "L0_tok_Wv", "L0_tok_bv", "L0_tok_Wf",
    "L0_tok_bf", "L0_tok_g1", "L0_tok_b1", "L0_tok_g2", "L0_tok_b2", "L0_attn_fc1_w", "L0_attn_fc1_b",
    "L0_attn_convA_w", "L0_attn_convA_b", "L0_attn_convB_w", "L0_attn_convB_b", "L0_attn_qkv_w", "L0_attn_qkv_b",
    "L0_attn_rpb", "L0_attn_proj_w", "L0_attn_proj_b", "L0_attn_fc2_w", "L0_attn_fc2_b", "L0_ffn_in_weight",
    "L0_ffn_in_bias", "L0_ffn_out_weight", "L1_attn_Wqkv", "L1_attn_Wproj", "L1_attn_Wv", "L1_attn_bv",
    "L1_ffn_ln_gamma", "L1_ffn_ln_beta", "L1_ffn_router_w", "L1_ffn_w1", "L1_ffn_w2",
]


def tower(nc, ins, const, out):

    def dram(name, shape, dt=F32):
        return nc.dram_tensor(name, shape, dt).ap()

    def group(prefix, names):
        return [ins[prefix + n] for n in names.split()]

    rows_out = out.rearrange("b s d -> (b s) d")
    h1, h2 = dram("h1", (TOKENS, D)), dram("h2", (TOKENS, D))
    scratch = dram("q_parts", (3 * NB * D, SEQ), BF16), dram("k_parts", (3 * NB * D, SEQ), BF16), dram("v_rows", (NB * NG * SEQ, P))
    shifts = dram("shifts", (COLS, HEADS, UROWS, SPAN))
    to_turn = group("L0_attn_", "fc1_w convA_w convB_w qkv_w proj_w fc2_w") + group("L0_ffn_", "in_weight") + group("L1_attn_", "Wqkv Wproj Wv")
    out_stored = nc.alloc_semaphore(name="out_stored")
    Store.taken.clear()
    turned = turned_weights(nc, to_turn, const["ident"])
    token_stage(nc, ins["x"], ins["L0_tok_emb"], group("L0_tok_", "Wq bq Wk bk Wv bv Wf bf g1 b1 g2 b2"),
                const["pos"], const["pad_rows"], const["ident"], h1, scratch)
    release(nc)
    neighborhood_stage(nc, h1, h2, group("L0_attn_", "fc1_b convA_b convB_b qkv_b rpb proj_b fc2_b"), turned[0:6], shifts,
                       const)
    release(nc)
    with ExitStack() as ctx:
        st = Store(nc, ctx, "main")
        H = st.sb("H", [P, TILES, D])
        idn = st.sb("idn", [P, P])
        h_in = st.sem("h_in")
        with nc.Block() as block:

            @block.sync
            def _(sp):
                sp.dma_start(H[:, :, :], h2.rearrange("(t p) d -> p t d", p=P)).then_inc(h_in, 16)
                sp.dma_start(idn[:, :], const["ident"]).then_inc(h_in, 16)
                sp.wait_ge(h_in, 32)

        dense_stage(nc, H, idn, turned[6], ins["L0_ffn_in_bias"], ins["L0_ffn_out_weight"])
        sets_stage(nc, H, idn, turned[7], turned[8], turned[9], ins["L1_attn_bv"], const)
        experts_stage(nc, H, idn, *group("L1_ffn_", "ln_gamma ln_beta router_w w1 w2"), const, rows_out, out_stored)


def kernel(**inputs):
    import numpy as _np
    import concourse.bacc as _bacc
    from concourse import mybir as _mybir
    from concourse.bass_utils import run_bass_kernel_spmd as _run

    nc = _bacc.Bacc("TRN2", target_bir_lowering=False, num_devices=1)
    arrays, ins, const = {}, {}, {}
    for group, names, values in ((ins, _INS, inputs), (const, list(_CONSTANTS), _CONSTANTS)):
        for name in names:
            a = _np.ascontiguousarray(values[name])
            arrays[f"in_{name}_dram"] = a
            group[name] = nc.dram_tensor(f"in_{name}_dram", a.shape, _mybir.dt.from_np(a.dtype), kind="ExternalInput").ap()
    out = nc.dram_tensor("out_0_dram", (NB, SEQ, D), F32, kind="ExternalOutput").ap()
    tower(nc, ins, const, out)
    r = _run(nc, [arrays], core_ids=[0])
    return r.results[0]["out_0_dram"]
```
